# Optimizing a Trainium2 kernel written in Bass

```python
import numpy as np
import jax
import jax.numpy as jnp

def _softmax(x, axis=-1):
    return jax.nn.softmax(x, axis=axis)

def _gelu(x):
    return jax.nn.gelu(x, approximate=True)

def _silu(x):
    return jax.nn.silu(x)

def _sigmoid(x):
    return jax.nn.sigmoid(x)

def _layernorm(x, axis=-1, eps=1e-05):
    m = jnp.mean(x, axis=axis, keepdims=True)
    v = jnp.var(x, axis=axis, keepdims=True)
    return (x - m) / jnp.sqrt(v + eps)

def _scatter_add(tgt, idx, src, axis=0):
    return tgt.at[idx].add(src)

def _segment_sum(src, seg, n):
    return jax.ops.segment_sum(src, seg, n)
kernel_name = 'mk_gnn_ffn_d4_gnn_r16_363a4b'

def setup_inputs(seed: int=0):
    np.random.seed(seed)
    _w = jnp.asarray

    def _rec_inputs():
        import jax
        import jax.numpy as jnp
        _gk = jax.random.key(seed)
        x = -0.0002117 + 1 * jax.random.normal(jax.random.fold_in(_gk, 1), (625, 512), jnp.float32)
        src = jax.random.randint(jax.random.fold_in(_gk, 2), (10000,), 0, 625, jnp.int32)
        dst = jnp.minimum((625 * jax.random.uniform(jax.random.fold_in(_gk, 3), (10000,)) ** 2.0).astype(jnp.int32), 9999)
        _o = jnp.argsort(dst, stable=True)
        src = src[_o]
        dst = dst[_o]
        return (x, src, dst)
    x, src, dst = _rec_inputs()

    def _L0_gnn_setup():
        import jax, jax.numpy as jnp
        import numpy as np
        N, E, D = (3125, 25000, 512)
        EPS = 1e-05
        key = jax.random.key(seed)
        ks = jax.random.split(key, 5)
        scale = 1.0 / np.sqrt(D)
        x = jax.random.normal(ks[0], (N, D), dtype=jnp.float32)
        edge_index = jax.random.randint(ks[1], (2, E), 0, N, dtype=jnp.int32)
        W_l = jax.random.normal(ks[2], (D, D), dtype=jnp.float32) * scale
        b_l = jnp.zeros((D,), dtype=jnp.float32)
        W_r = jax.random.normal(ks[3], (D, D), dtype=jnp.float32) * scale
        gamma = jnp.ones((D,), dtype=jnp.float32)
        beta = jnp.zeros((D,), dtype=jnp.float32)
        return {'x': x, 'edge_index': edge_index, 'W_l': W_l, 'b_l': b_l, 'W_r': W_r, 'gamma': gamma, 'beta': beta}
    _L0_gnn_all = _L0_gnn_setup()
    _L0_gnn_in = {k: v for k, v in _L0_gnn_all.items() if k in ('W_l', 'b_l', 'W_r', 'gamma', 'beta')}
    del _L0_gnn_all

    def _L0_ffn_setup():
        import jax, jax.numpy as jnp
        import numpy as np
        B, N, DIM = (1, 128, 512)
        DH, H = (64, 8)
        E, FF = (8, 128)

        def _layernorm(x, g, b, eps=1e-05):
            mu = jnp.mean(x, axis=-1, keepdims=True)
            var = jnp.mean(jnp.square(x - mu), axis=-1, keepdims=True)
            return (x - mu) * jax.lax.rsqrt(var + eps) * g + b

        def _l2norm(x, eps=1e-12):
            return x / jnp.sqrt(jnp.sum(jnp.square(x), axis=-1, keepdims=True) + eps)
        key = jax.random.key(seed)
        ks = jax.random.split(key, 12)
        g = lambda k, shape: jax.random.normal(k, shape, jnp.float32) * 0.02
        return {'x': jax.random.normal(ks[0], (B, N, DIM), jnp.float32), 'ln_g': jnp.ones((DIM,), jnp.float32), 'ln_b': jnp.zeros((DIM,), jnp.float32), 'Wq': g(ks[1], (DIM, DIM)), 'Wk': g(ks[2], (DIM, DIM)), 'Wv': g(ks[3], (DIM, DIM)), 'Wo': g(ks[4], (DIM, DIM)), 'qn_g': jnp.ones((DH,), jnp.float32), 'kn_g': jnp.ones((DH,), jnp.float32), 'gate_W': g(ks[5], (DIM, E)), 'gate_b': jnp.zeros((E,), jnp.float32), 'W1': g(ks[6], (E, DIM, FF)), 'b1': jnp.zeros((E, FF), jnp.float32), 'W2': g(ks[7], (E, FF, DIM)), 'b2': jnp.zeros((E, DIM), jnp.float32)}
    _L0_ffn_all = _L0_ffn_setup()
    _L0_ffn_in = {k: v for k, v in _L0_ffn_all.items() if k in ('ln_g', 'ln_b', 'Wq', 'Wk', 'Wv', 'Wo', 'qn_g', 'kn_g', 'gate_W', 'gate_b', 'W1', 'b1', 'W2', 'b2')}
    del _L0_ffn_all

    def _L1_gnn_setup():
        import jax, jax.numpy as jnp
        import numpy as np
        D = 512
        H = 8
        DH = D // H
        F = 128
        L = 2
        N = 1250
        E = 20000
        EPS = 1e-05

        def _xavier(key, shape):
            fan_out, fan_in = (shape[-2], shape[-1])
            lim = float(np.sqrt(6.0 / (fan_in + fan_out)))
            return jax.random.uniform(key, shape, jnp.float32, -lim, lim)

        def _batchnorm(x, g, b):
            mu = jnp.mean(x, axis=0)
            var = jnp.mean(jnp.square(x - mu), axis=0)
            return (x - mu) * jax.lax.rsqrt(var + EPS) * g + b

        def _layernorm(x, g, b):
            mu = jnp.mean(x, axis=-1, keepdims=True)
            var = jnp.mean(jnp.square(x - mu), axis=-1, keepdims=True)
            return (x - mu) * jax.lax.rsqrt(var + EPS) * g + b
        key = jax.random.key(seed)
        ks = jax.random.split(key, 12)
        src = jax.random.normal(ks[0], (N, D), jnp.float32)
        edge_index = jax.random.randint(ks[1], (2, E), 0, N)
        return {'src': src, 'edge_index': edge_index, 'Wq': _xavier(ks[2], (L, D, D)), 'bq': jnp.zeros((L, D), jnp.float32), 'Wk': _xavier(ks[3], (L, D, D)), 'Wv': _xavier(ks[4], (L, D, D)), 'Wo': _xavier(ks[5], (L, D, D)), 'bo': jnp.zeros((L, D), jnp.float32), 'W1': _xavier(ks[6], (L, F, D)), 'b1': jnp.zeros((L, F), jnp.float32), 'W2': _xavier(ks[7], (L, D, F)), 'b2': jnp.zeros((L, D), jnp.float32), 'g1': jnp.ones((L, D), jnp.float32), 'beta1': jnp.zeros((L, D), jnp.float32), 'g2': jnp.ones((L, D), jnp.float32), 'beta2': jnp.zeros((L, D), jnp.float32), 'ln_g': jnp.ones((D,), jnp.float32), 'ln_b': jnp.zeros((D,), jnp.float32)}
    _L1_gnn_all = _L1_gnn_setup()
    _L1_gnn_in = {k: v for k, v in _L1_gnn_all.items() if k in ('Wq', 'bq', 'Wk', 'Wv', 'Wo', 'bo', 'W1', 'b1', 'W2', 'b2', 'g1', 'beta1', 'g2', 'beta2', 'ln_g', 'ln_b')}
    del _L1_gnn_all

    def _L1_ffn_setup():
        import jax, jax.numpy as jnp
        import numpy as np
        B, S, H, E, K = (8, 256, 512, 8, 2)
        key = jax.random.key(seed)
        ks = jax.random.split(key, 7)
        s_h = 1.0 / np.sqrt(H)
        s_2h = 1.0 / np.sqrt(2 * H)
        return {'x': jax.random.normal(ks[0], (B, S, H), dtype=jnp.float32), 'gate_w': jax.random.uniform(ks[1], (H, E), minval=-s_h, maxval=s_h, dtype=jnp.float32), 'gate_b': jax.random.uniform(ks[2], (E,), minval=-s_h, maxval=s_h, dtype=jnp.float32), 'w1': jax.random.uniform(ks[3], (E, H, 2 * H), minval=-s_h, maxval=s_h, dtype=jnp.float32), 'b1': jax.random.uniform(ks[4], (E, 2 * H), minval=-s_h, maxval=s_h, dtype=jnp.float32), 'w2': jax.random.uniform(ks[5], (E, 2 * H, H), minval=-s_2h, maxval=s_2h, dtype=jnp.float32), 'b2': jax.random.uniform(ks[6], (E, H), minval=-s_2h, maxval=s_2h, dtype=jnp.float32)}
    _L1_ffn_all = _L1_ffn_setup()
    _L1_ffn_in = {k: v for k, v in _L1_ffn_all.items() if k in ('gate_w', 'gate_b', 'w1', 'b1', 'w2', 'b2')}
    del _L1_ffn_all

    def _L2_gnn_setup():
        import jax, jax.numpy as jnp
        import numpy as np
        N, E = (3125, 50000)
        IN, OUT, H, B = (512, 512, 8, 4)
        FH = OUT // H
        EPS = 1e-05
        key = jax.random.key(seed)
        ks = jax.random.split(key, 8)
        s_in = 1.0 / np.sqrt(IN)
        return {'x': jax.random.normal(ks[0], (N, IN), jnp.float32), 'edge_index': jax.random.randint(ks[1], (2, E), 0, N, jnp.int32), 'W_bases': jax.random.normal(ks[2], (IN, B * FH), jnp.float32) * s_in, 'W_comb': jax.random.normal(ks[3], (IN, H * B), jnp.float32) * s_in, 'b_comb': jnp.zeros((H * B,), jnp.float32), 'conv_bias': jnp.zeros((OUT,), jnp.float32), 'W_res': jax.random.normal(ks[4], (IN, OUT), jnp.float32) * s_in, 'b_res': jnp.zeros((OUT,), jnp.float32), 'gamma': jnp.ones((OUT,), jnp.float32), 'beta': jnp.zeros((OUT,), jnp.float32)}
    _L2_gnn_all = _L2_gnn_setup()
    _L2_gnn_in = {k: v for k, v in _L2_gnn_all.items() if k in ('W_bases', 'W_comb', 'b_comb', 'conv_bias', 'W_res', 'b_res', 'gamma', 'beta')}
    del _L2_gnn_all

    def _L2_ffn_setup():
        import jax, jax.numpy as jnp
        import numpy as np
        NUM_EXPERTS = 8
        TOP_K = 2
        HIDDEN = 512
        INTERMEDIATE = 128
        BATCH, SEQ = (8, 128)
        key = jax.random.key(seed)
        ks = jax.random.split(key, 7)
        s_in = 1.0 / np.sqrt(HIDDEN)
        s_mid = 1.0 / np.sqrt(INTERMEDIATE)
        return {'x': jax.random.normal(ks[0], (BATCH, SEQ, HIDDEN), jnp.float32), 'Wg': jax.random.normal(ks[1], (HIDDEN, NUM_EXPERTS), jnp.float32) * s_in, 'bg': jnp.zeros((NUM_EXPERTS,), jnp.float32), 'W1': jax.random.normal(ks[2], (NUM_EXPERTS, HIDDEN, INTERMEDIATE), jnp.float32) * s_in, 'b1': jnp.zeros((NUM_EXPERTS, INTERMEDIATE), jnp.float32), 'W2': jax.random.normal(ks[3], (NUM_EXPERTS, INTERMEDIATE, HIDDEN), jnp.float32) * s_mid, 'b2': jnp.zeros((NUM_EXPERTS, HIDDEN), jnp.float32)}
    _L2_ffn_all = _L2_ffn_setup()
    _L2_ffn_in = {k: v for k, v in _L2_ffn_all.items() if k in ('Wg', 'bg', 'W1', 'b1', 'W2', 'b2')}
    del _L2_ffn_all

    def _L3_gnn_setup():
        import jax, jax.numpy as jnp
        import numpy as np
        N = 3125
        E = 50000
        D = 512

        def _gcn_conv(x, edge_index, W, b):
            n = x.shape[0]
            xw = x @ W.T
            loop = jnp.arange(n, dtype=edge_index.dtype)
            row = jnp.concatenate([edge_index[0], loop])
            col = jnp.concatenate([edge_index[1], loop])
            deg = jax.ops.segment_sum(jnp.ones_like(row, dtype=xw.dtype), col, num_segments=n)
            dinv = jnp.where(deg > 0, jax.lax.rsqrt(deg), 0.0)
            norm = dinv[row] * dinv[col]
            msgs = norm[:, None] * xw[row]
            out = jax.ops.segment_sum(msgs, col, num_segments=n)
            return out + b

        def _batch_norm(h, gamma, beta, eps=1e-05):
            mean = jnp.mean(h, axis=0)
            var = jnp.var(h, axis=0)
            return (h - mean) * jax.lax.rsqrt(var + eps) * gamma + beta
        key = jax.random.key(seed)
        k1, k2, k3, k4, k5, k6 = jax.random.split(key, 6)
        x = jax.random.normal(k1, (N, D), dtype=jnp.float32)
        edge_index = jax.random.randint(k2, (2, E), 0, N, dtype=jnp.int64)
        W = jax.random.normal(k3, (D, D), dtype=jnp.float32) * (1.0 / np.sqrt(D))
        b = jnp.zeros((D,), dtype=jnp.float32)
        gamma = jnp.ones((D,), dtype=jnp.float32)
        beta = jnp.zeros((D,), dtype=jnp.float32)
        return {'x': x, 'edge_index': edge_index, 'W': W, 'b': b, 'gamma': gamma, 'beta': beta}
    _L3_gnn_all = _L3_gnn_setup()
    _L3_gnn_in = {k: v for k, v in _L3_gnn_all.items() if k in ('W', 'b', 'gamma', 'beta')}
    del _L3_gnn_all

    def _L3_ffn_setup():
        import jax, jax.numpy as jnp
        import numpy as np
        B, T, C = (8, 256, 512)
        E, K = (8, 2)
        H = 1536
        key = jax.random.key(seed)
        ks = jax.random.split(key, 5)
        x = jax.random.normal(ks[0], (B, T, C), dtype=jnp.float32)
        router_w = jax.random.normal(ks[1], (E, C), dtype=jnp.float32) * 0.02
        w1 = jax.random.normal(ks[2], (E, H, C), dtype=jnp.float32) * 0.02
        wgate = jax.random.normal(ks[3], (E, H, C), dtype=jnp.float32) * 0.02
        w2 = jax.random.normal(ks[4], (E, C, H), dtype=jnp.float32) * (0.02 / np.sqrt(2.0))
        return {'x': x, 'router_w': router_w, 'w1': w1, 'wgate': wgate, 'w2': w2}
    _L3_ffn_all = _L3_ffn_setup()
    _L3_ffn_in = {k: v for k, v in _L3_ffn_all.items() if k in ('router_w', 'w1', 'wgate', 'w2')}
    del _L3_ffn_all
    return {'x': x, 'src': src, 'dst': dst, 'L0_gnn_W_l': _L0_gnn_in['W_l'], 'L0_gnn_b_l': _L0_gnn_in['b_l'], 'L0_gnn_W_r': _L0_gnn_in['W_r'], 'L0_gnn_gamma': _L0_gnn_in['gamma'], 'L0_gnn_beta': _L0_gnn_in['beta'], 'L0_ffn_ln_g': _L0_ffn_in['ln_g'], 'L0_ffn_ln_b': _L0_ffn_in['ln_b'], 'L0_ffn_Wq': _L0_ffn_in['Wq'], 'L0_ffn_Wk': _L0_ffn_in['Wk'], 'L0_ffn_Wv': _L0_ffn_in['Wv'], 'L0_ffn_Wo': _L0_ffn_in['Wo'], 'L0_ffn_qn_g': _L0_ffn_in['qn_g'], 'L0_ffn_kn_g': _L0_ffn_in['kn_g'], 'L0_ffn_gate_W': _L0_ffn_in['gate_W'], 'L0_ffn_gate_b': _L0_ffn_in['gate_b'], 'L0_ffn_W1': _L0_ffn_in['W1'], 'L0_ffn_b1': _L0_ffn_in['b1'], 'L0_ffn_W2': _L0_ffn_in['W2'], 'L0_ffn_b2': _L0_ffn_in['b2'], 'L1_gnn_Wq': _L1_gnn_in['Wq'], 'L1_gnn_bq': _L1_gnn_in['bq'], 'L1_gnn_Wk': _L1_gnn_in['Wk'], 'L1_gnn_Wv': _L1_gnn_in['Wv'], 'L1_gnn_Wo': _L1_gnn_in['Wo'], 'L1_gnn_bo': _L1_gnn_in['bo'], 'L1_gnn_W1': _L1_gnn_in['W1'], 'L1_gnn_b1': _L1_gnn_in['b1'], 'L1_gnn_W2': _L1_gnn_in['W2'], 'L1_gnn_b2': _L1_gnn_in['b2'], 'L1_gnn_g1': _L1_gnn_in['g1'], 'L1_gnn_beta1': _L1_gnn_in['beta1'], 'L1_gnn_g2': _L1_gnn_in['g2'], 'L1_gnn_beta2': _L1_gnn_in['beta2'], 'L1_gnn_ln_g': _L1_gnn_in['ln_g'], 'L1_gnn_ln_b': _L1_gnn_in['ln_b'], 'L1_ffn_gate_w': _L1_ffn_in['gate_w'], 'L1_ffn_gate_b': _L1_ffn_in['gate_b'], 'L1_ffn_w1': _L1_ffn_in['w1'], 'L1_ffn_b1': _L1_ffn_in['b1'], 'L1_ffn_w2': _L1_ffn_in['w2'], 'L1_ffn_b2': _L1_ffn_in['b2'], 'L2_gnn_W_bases': _L2_gnn_in['W_bases'], 'L2_gnn_W_comb': _L2_gnn_in['W_comb'], 'L2_gnn_b_comb': _L2_gnn_in['b_comb'], 'L2_gnn_conv_bias': _L2_gnn_in['conv_bias'], 'L2_gnn_W_res': _L2_gnn_in['W_res'], 'L2_gnn_b_res': _L2_gnn_in['b_res'], 'L2_gnn_gamma': _L2_gnn_in['gamma'], 'L2_gnn_beta': _L2_gnn_in['beta'], 'L2_ffn_Wg': _L2_ffn_in['Wg'], 'L2_ffn_bg': _L2_ffn_in['bg'], 'L2_ffn_W1': _L2_ffn_in['W1'], 'L2_ffn_b1': _L2_ffn_in['b1'], 'L2_ffn_W2': _L2_ffn_in['W2'], 'L2_ffn_b2': _L2_ffn_in['b2'], 'L3_gnn_W': _L3_gnn_in['W'], 'L3_gnn_b': _L3_gnn_in['b'], 'L3_gnn_gamma': _L3_gnn_in['gamma'], 'L3_gnn_beta': _L3_gnn_in['beta'], 'L3_ffn_router_w': _L3_ffn_in['router_w'], 'L3_ffn_w1': _L3_ffn_in['w1'], 'L3_ffn_wgate': _L3_ffn_in['wgate'], 'L3_ffn_w2': _L3_ffn_in['w2']}

def reference(x, src, dst, L0_gnn_W_l, L0_gnn_b_l, L0_gnn_W_r, L0_gnn_gamma, L0_gnn_beta, L0_ffn_ln_g, L0_ffn_ln_b, L0_ffn_Wq, L0_ffn_Wk, L0_ffn_Wv, L0_ffn_Wo, L0_ffn_qn_g, L0_ffn_kn_g, L0_ffn_gate_W, L0_ffn_gate_b, L0_ffn_W1, L0_ffn_b1, L0_ffn_W2, L0_ffn_b2, L1_gnn_Wq, L1_gnn_bq, L1_gnn_Wk, L1_gnn_Wv, L1_gnn_Wo, L1_gnn_bo, L1_gnn_W1, L1_gnn_b1, L1_gnn_W2, L1_gnn_b2, L1_gnn_g1, L1_gnn_beta1, L1_gnn_g2, L1_gnn_beta2, L1_gnn_ln_g, L1_gnn_ln_b, L1_ffn_gate_w, L1_ffn_gate_b, L1_ffn_w1, L1_ffn_b1, L1_ffn_w2, L1_ffn_b2, L2_gnn_W_bases, L2_gnn_W_comb, L2_gnn_b_comb, L2_gnn_conv_bias, L2_gnn_W_res, L2_gnn_b_res, L2_gnn_gamma, L2_gnn_beta, L2_ffn_Wg, L2_ffn_bg, L2_ffn_W1, L2_ffn_b1, L2_ffn_W2, L2_ffn_b2, L3_gnn_W, L3_gnn_b, L3_gnn_gamma, L3_gnn_beta, L3_ffn_router_w, L3_ffn_w1, L3_ffn_wgate, L3_ffn_w2):
    import jax
    import jax.numpy as jnp

    def _L0_gnn_ref(x, edge_index, W_l, b_l, W_r, gamma, beta):
        import jax, jax.numpy as jnp
        import numpy as np
        N, E, D = (3125, 25000, 512)
        EPS = 1e-05
        n = x.shape[0]
        src, dst = (edge_index[0], edge_index[1])
        agg = jax.ops.segment_sum(x[src], dst, num_segments=n)
        cnt = jax.ops.segment_sum(jnp.ones((src.shape[0],), x.dtype), dst, num_segments=n)
        mean_agg = agg / jnp.maximum(cnt, 1.0)[:, None]
        h = mean_agg @ W_l.T + b_l + x @ W_r.T
        mu = jnp.mean(h, axis=0)
        var = jnp.var(h, axis=0)
        h = (h - mu) * jax.lax.rsqrt(var + EPS) * gamma + beta
        return jax.nn.relu(h) + x

    def _L0_ffn_ref(x, ln_g, ln_b, Wq, Wk, Wv, Wo, qn_g, kn_g, gate_W, gate_b, W1, b1, W2, b2):
        import jax, jax.numpy as jnp
        import numpy as np
        B, N, DIM = (1, 128, 512)
        DH, H = (64, 8)
        E, FF = (8, 128)

        def _layernorm(x, g, b, eps=1e-05):
            mu = jnp.mean(x, axis=-1, keepdims=True)
            var = jnp.mean(jnp.square(x - mu), axis=-1, keepdims=True)
            return (x - mu) * jax.lax.rsqrt(var + eps) * g + b

        def _l2norm(x, eps=1e-12):
            return x / jnp.sqrt(jnp.sum(jnp.square(x), axis=-1, keepdims=True) + eps)
        b, n, d = x.shape
        dh = qn_g.shape[0]
        h = d // dh
        hx = _layernorm(x, ln_g, ln_b)
        q = (hx @ Wq).reshape(b, n, h, dh).transpose(0, 2, 1, 3)
        k = (hx @ Wk).reshape(b, n, h, dh).transpose(0, 2, 1, 3)
        v = (hx @ Wv).reshape(b, n, h, dh).transpose(0, 2, 1, 3)
        scale = jnp.sqrt(jnp.float32(dh))
        q = _l2norm(q) * scale * qn_g
        k = _l2norm(k) * scale * kn_g
        scores = jnp.einsum('bhqd,bhkd->bhqk', q, k) * dh ** (-0.5)
        causal = jnp.tril(jnp.ones((n, n), bool))
        scores = jnp.where(causal, scores, jnp.finfo(scores.dtype).min)
        attn = jax.nn.softmax(scores, axis=-1)
        o = jnp.einsum('bhqk,bhkd->bhqd', attn, v)
        y = o.transpose(0, 2, 1, 3).reshape(b, n, d) @ Wo
        gate = jax.nn.softmax(y @ gate_W + gate_b, axis=-1)
        hid = jax.nn.gelu(jnp.einsum('bnd,edf->bnef', y, W1) + b1)
        eo = jnp.einsum('bnef,efd->bned', hid, W2) + b2
        out = jnp.einsum('bned,bne->bnd', eo, gate)
        return out

    def _L1_gnn_ref(src, edge_index, Wq, bq, Wk, Wv, Wo, bo, W1, b1, W2, b2, g1, beta1, g2, beta2, ln_g, ln_b):
        import jax, jax.numpy as jnp
        import numpy as np
        D = 512
        H = 8
        DH = D // H
        F = 128
        L = 2
        N = 1250
        E = 20000
        EPS = 1e-05

        def _xavier(key, shape):
            fan_out, fan_in = (shape[-2], shape[-1])
            lim = float(np.sqrt(6.0 / (fan_in + fan_out)))
            return jax.random.uniform(key, shape, jnp.float32, -lim, lim)

        def _batchnorm(x, g, b):
            mu = jnp.mean(x, axis=0)
            var = jnp.mean(jnp.square(x - mu), axis=0)
            return (x - mu) * jax.lax.rsqrt(var + EPS) * g + b

        def _layernorm(x, g, b):
            mu = jnp.mean(x, axis=-1, keepdims=True)
            var = jnp.mean(jnp.square(x - mu), axis=-1, keepdims=True)
            return (x - mu) * jax.lax.rsqrt(var + EPS) * g + b
        n = src.shape[0]
        scaling = float(DH) ** (-0.5)
        tgt = edge_index[1]
        srcidx = edge_index[0]
        x = src
        for l in range(L):
            q = ((x @ Wq[l].T + bq[l]) * scaling).reshape(n, H, DH)
            k = (x @ Wk[l].T).reshape(n, H, DH)
            v = (x @ Wv[l].T).reshape(n, H, DH)
            scores = jnp.einsum('ehd,ehd->eh', q[tgt], k[srcidx])
            m = jax.ops.segment_max(scores, tgt, num_segments=n)
            p = jnp.exp(scores - m[tgt])
            s = jax.ops.segment_sum(p, tgt, num_segments=n)
            w = p / (s[tgt] + 1e-16)
            agg = jax.ops.segment_sum(w[:, :, None] * v[srcidx], tgt, num_segments=n)
            attn = agg.reshape(n, D) @ Wo[l].T + bo[l]
            x = _batchnorm(x + attn, g1[l], beta1[l])
            ff = jax.nn.relu(x @ W1[l].T + b1[l]) @ W2[l].T + b2[l]
            x = _batchnorm(x + ff, g2[l], beta2[l])
        return _layernorm(x, ln_g, ln_b)

    def _L1_ffn_ref(x, gate_w, gate_b, w1, b1, w2, b2):
        import jax, jax.numpy as jnp
        import numpy as np
        B, S, H, E, K = (8, 256, 512, 8, 2)
        logits = jnp.einsum('bsh,he->bse', x, gate_w) + gate_b
        topk_vals, topk_idx = jax.lax.top_k(logits, K)
        topk_weights = jax.nn.softmax(topk_vals, axis=-1)
        mask = jax.nn.one_hot(topk_idx, E, dtype=topk_weights.dtype)
        weights = jnp.einsum('bske,bsk->bse', mask, topk_weights)
        h = jax.nn.relu(jnp.einsum('bsh,ehf->bsef', x, w1) + b1)
        expert_out = jnp.einsum('bsef,efh->bseh', h, w2) + b2
        return jnp.einsum('bseh,bse->bsh', expert_out, weights)

    def _L2_gnn_ref(x, edge_index, W_bases, W_comb, b_comb, conv_bias, W_res, b_res, gamma, beta):
        import jax, jax.numpy as jnp
        import numpy as np
        N, E = (3125, 50000)
        IN, OUT, H, B = (512, 512, 8, 4)
        FH = OUT // H
        EPS = 1e-05
        n = x.shape[0]
        loops = jnp.arange(n, dtype=edge_index.dtype)
        src = jnp.concatenate([edge_index[0], loops])
        dst = jnp.concatenate([edge_index[1], loops])
        deg = jax.ops.segment_sum(jnp.ones_like(src, dtype=x.dtype), dst, num_segments=n)
        dinv = jnp.where(deg > 0, jax.lax.rsqrt(jnp.maximum(deg, 1.0)), 0.0)
        norm = dinv[src] * dinv[dst]
        bases = x @ W_bases
        agg = jax.ops.segment_sum(bases[src] * norm[:, None], dst, num_segments=n)
        weightings = (x @ W_comb + b_comb).reshape(n, H, B)
        agg = agg.reshape(n, B, FH)
        conv_out = jnp.einsum('nhb,nbf->nhf', weightings, agg).reshape(n, OUT) + conv_bias
        out = conv_out + x @ W_res + b_res
        mu = out.mean(-1, keepdims=True)
        var = out.var(-1, keepdims=True)
        out = (out - mu) * jax.lax.rsqrt(var + EPS) * gamma + beta
        return jax.nn.relu(out)

    def _L2_ffn_ref(x, Wg, bg, W1, b1, W2, b2):
        import jax, jax.numpy as jnp
        import numpy as np
        NUM_EXPERTS = 8
        TOP_K = 2
        HIDDEN = 512
        INTERMEDIATE = 128
        BATCH, SEQ = (8, 128)
        B, S, H = x.shape
        xf = x.reshape(B * S, H)
        logits = xf @ Wg + bg
        probs = jax.nn.softmax(logits, axis=-1)
        _, top_idx = jax.lax.top_k(probs, TOP_K)
        mask = jnp.any(top_idx[:, :, None] == jnp.arange(NUM_EXPERTS)[None, None, :], axis=1)
        comb = probs * mask.astype(probs.dtype)
        out = jnp.zeros_like(xf)
        for e in range(NUM_EXPERTS):
            h = jax.nn.gelu(xf @ W1[e] + b1[e])
            y = h @ W2[e] + b2[e]
            out = out + comb[:, e:e + 1] * y
        return out.reshape(B, S, H)

    def _L3_gnn_ref(x, edge_index, W, b, gamma, beta):
        import jax, jax.numpy as jnp
        import numpy as np
        N = 3125
        E = 50000
        D = 512

        def _gcn_conv(x, edge_index, W, b):
            n = x.shape[0]
            xw = x @ W.T
            loop = jnp.arange(n, dtype=edge_index.dtype)
            row = jnp.concatenate([edge_index[0], loop])
            col = jnp.concatenate([edge_index[1], loop])
            deg = jax.ops.segment_sum(jnp.ones_like(row, dtype=xw.dtype), col, num_segments=n)
            dinv = jnp.where(deg > 0, jax.lax.rsqrt(deg), 0.0)
            norm = dinv[row] * dinv[col]
            msgs = norm[:, None] * xw[row]
            out = jax.ops.segment_sum(msgs, col, num_segments=n)
            return out + b

        def _batch_norm(h, gamma, beta, eps=1e-05):
            mean = jnp.mean(h, axis=0)
            var = jnp.var(h, axis=0)
            return (h - mean) * jax.lax.rsqrt(var + eps) * gamma + beta
        identity = x
        h = _gcn_conv(x, edge_index, W, b)
        h = _batch_norm(h, gamma, beta)
        h = jax.nn.gelu(h, approximate=False)
        return h + identity

    def _L3_ffn_ref(x, router_w, w1, wgate, w2):
        import jax, jax.numpy as jnp
        import numpy as np
        B, T, C = (8, 256, 512)
        E, K = (8, 2)
        H = 1536
        b, t, c = x.shape
        x_flat = x.reshape(b * t, c)
        logits = x_flat @ router_w.T
        probs = jax.nn.softmax(logits, axis=-1)
        gates, idx = jax.lax.top_k(probs, K)
        gates = gates / jnp.sum(gates, axis=-1, keepdims=True)
        combine = jnp.sum(jax.nn.one_hot(idx, E, dtype=x.dtype) * gates[..., None], axis=1)
        out = jnp.zeros_like(x_flat)
        for e in range(E):
            h = jax.nn.silu(x_flat @ w1[e].T) * (x_flat @ wgate[e].T)
            out = out + combine[:, e:e + 1] * (h @ w2[e].T)
        return out.reshape(b, t, c)
    edge_index = jnp.stack([src, dst])
    x = x + _L0_gnn_ref(_layernorm(x, axis=-1), edge_index, L0_gnn_W_l, L0_gnn_b_l, L0_gnn_W_r, L0_gnn_gamma, L0_gnn_beta)
    x = x + _L0_ffn_ref(_layernorm(x, axis=-1)[None], L0_ffn_ln_g, L0_ffn_ln_b, L0_ffn_Wq, L0_ffn_Wk, L0_ffn_Wv, L0_ffn_Wo, L0_ffn_qn_g, L0_ffn_kn_g, L0_ffn_gate_W, L0_ffn_gate_b, L0_ffn_W1, L0_ffn_b1, L0_ffn_W2, L0_ffn_b2)[0]
    x = x + _L1_gnn_ref(_layernorm(x, axis=-1), edge_index, L1_gnn_Wq, L1_gnn_bq, L1_gnn_Wk, L1_gnn_Wv, L1_gnn_Wo, L1_gnn_bo, L1_gnn_W1, L1_gnn_b1, L1_gnn_W2, L1_gnn_b2, L1_gnn_g1, L1_gnn_beta1, L1_gnn_g2, L1_gnn_beta2, L1_gnn_ln_g, L1_gnn_ln_b)
    x = x + _L1_ffn_ref(_layernorm(x, axis=-1)[None], L1_ffn_gate_w, L1_ffn_gate_b, L1_ffn_w1, L1_ffn_b1, L1_ffn_w2, L1_ffn_b2)[0]
    x = x + _L2_gnn_ref(_layernorm(x, axis=-1), edge_index, L2_gnn_W_bases, L2_gnn_W_comb, L2_gnn_b_comb, L2_gnn_conv_bias, L2_gnn_W_res, L2_gnn_b_res, L2_gnn_gamma, L2_gnn_beta)
    x = x + _L2_ffn_ref(_layernorm(x, axis=-1)[None], L2_ffn_Wg, L2_ffn_bg, L2_ffn_W1, L2_ffn_b1, L2_ffn_W2, L2_ffn_b2)[0]
    x = x + _L3_gnn_ref(_layernorm(x, axis=-1), edge_index, L3_gnn_W, L3_gnn_b, L3_gnn_gamma, L3_gnn_beta)
    x = x + _L3_ffn_ref(_layernorm(x, axis=-1)[None], L3_ffn_router_w, L3_ffn_w1, L3_ffn_wgate, L3_ffn_w2)[0]
    return x

_drawn_inputs = setup_inputs


def setup_inputs(seed=0):
    import zlib

    import numpy as np

    out = dict(_drawn_inputs(seed))
    spreads = {'L0_gnn_b_l': (0.0, 2.0),
     'L0_gnn_gamma': (1.0, 0.2),
     'L0_gnn_beta': (0.0, 0.1),
     'L0_ffn_ln_g': (1.0, 0.6),
     'L0_ffn_ln_b': (0.0, 0.8),
     'L0_ffn_qn_g': (1.0, 0.6),
     'L0_ffn_kn_g': (1.0, 0.6),
     'L0_ffn_gate_b': (0.0, 0.8),
     'L0_ffn_b1': (0.0, 2.0),
     'L0_ffn_b2': (0.0, 2.0),
     'L1_gnn_bq': (0.0, 2.0),
     'L1_gnn_bo': (0.0, 2.0),
     'L1_gnn_b1': (0.0, 2.0),
     'L1_gnn_b2': (0.0, 2.0),
     'L1_gnn_g1': (1.0, 0.6),
     'L1_gnn_beta1': (0.0, 2.0),
     'L1_gnn_g2': (1.0, 0.6),
     'L1_gnn_beta2': (0.0, 0.8),
     'L1_gnn_ln_g': (1.0, 0.6),
     'L1_gnn_ln_b': (0.0, 0.8),
     'L2_gnn_b_comb': (0.0, 2.0),
     'L2_gnn_conv_bias': (0.0, 2.0),
     'L2_gnn_b_res': (0.0, 2.0),
     'L2_gnn_gamma': (1.0, 0.6),
     'L2_gnn_beta': (0.0, 2.0),
     'L2_ffn_bg': (0.0, 2.0),
     'L2_ffn_b1': (0.0, 2.0),
     'L2_ffn_b2': (0.0, 2.0),
     'L3_gnn_b': (0.0, 2.0),
     'L3_gnn_gamma': (1.0, 0.6),
     'L3_gnn_beta': (0.0, 2.0)}
    factors = {'L0_ffn_Wq': 8.0,
     'L0_ffn_Wk': 8.0,
     'L0_ffn_Wv': 8.0,
     'L0_ffn_Wo': 8.0,
     'L0_ffn_gate_W': 8.0,
     'L0_ffn_W1': 8.0,
     'L0_ffn_W2': 8.0,
     'L1_ffn_gate_b': 45.704,
     'L1_ffn_b1': 64.0,
     'L1_ffn_b2': 64.0,
     'L3_ffn_router_w': 6.269,
     'L3_ffn_w1': 5.562,
     'L3_ffn_wgate': 5.435,
     'L3_ffn_w2': 5.425,
     'L1_gnn_Wq': 4.171,
     'L1_gnn_Wk': 4.295,
     'L1_gnn_Wv': 3.191,
     'L1_gnn_Wo': 3.296,
     'L1_gnn_W1': 3.547,
     'L1_gnn_W2': 3.43,
     'L1_ffn_gate_w': 7.742,
     'L1_ffn_w1': 8.0,
     'L1_ffn_w2': 7.961,
     'L2_gnn_W_bases': 4.794,
     'L2_gnn_W_comb': 4.6,
     'L2_gnn_W_res': 4.838,
     'L2_ffn_Wg': 5.668,
     'L2_ffn_W1': 7.599,
     'L2_ffn_W2': 4.226,
     'L3_gnn_W': 4.192}
    for name, (base, spread) in spreads.items():
        noise = np.random.default_rng([zlib.crc32(name.encode()), seed]).standard_normal(out[name].shape)
        drawn = base * np.exp(spread * noise) if base else spread * noise
        out[name] = jnp.asarray(drawn.astype(out[name].dtype))
    for name, factor in factors.items():
        out[name] = (out[name] * factor).astype(out[name].dtype)
    return out
```

```python
from contextlib import ExitStack

import numpy as np

import concourse.bass as bass
from concourse import mybir

ALU = mybir.AluOpType
ACT = mybir.ActivationFunctionType
AX = mybir.AxisListType
F32 = mybir.dt.float32
BF16 = mybir.dt.bfloat16
F16 = mybir.dt.float16
I32 = mybir.dt.int32
U32 = mybir.dt.uint32

P = 128
N = 625
R = 125
T = N // R
D = 512
C = D // P
EDGES = 10000
ET = EDGES // R
H = 8
DH = D // H
E = 8
LAYERS = 2
F1 = 1024
F3 = 1536
BASES = 256
NB = 4
HALVES = ((0, 3 * R), (3 * R, N))
NEG = -1e30
EPS = 1e-5

FV = {}
_at = 0
for _n, _w in (("l0_b", 4), ("l0_g", 4), ("l0_be", 4), ("ln_g", 4), ("ln_b", 4), ("qn", 1), ("kn", 1),
               ("m0_b1", 8), ("m1_b1", 64), ("m2_b1", 8), ("l3_b", 4), ("l3_g", 4), ("l3_be", 4)):
    FV[_n] = _at
    _at += _w
FVW = _at
LV = {}
_at = 0
for _n, _w in (("bq", 4), ("bo", 4), ("b1", 1), ("b2", 4), ("g1", 4), ("be1", 4), ("g2", 4), ("be2", 4)):
    LV[_n] = _at
    _at += _w
LVW = _at
GW = {0: 0, 1: 8, 2: 16, 3: 24, "comb": 32}
GWW = 64
RB = {0: 0, 1: 8, 2: 16, "comb": 24}
RBW = 56


class Chain:

    def __init__(self, eng, sem, base=0):
        self.eng, self.sem, self.n = eng, sem, base

    def __call__(self, ins):
        ins.then_inc(self.sem, 1)
        self.n = self.n + 1

    def sync(self):
        self.eng.wait_ge(self.sem, self.n)


def graph_network(nc, A, out):
    ctx = ExitStack()
    with ctx:
        sems = {}

        def S(name):
            if name not in sems:
                sems[name] = ctx.enter_context(nc.semaphore(name))
            return sems[name]

        def sb(name, shape, dt=F32):
            return ctx.enter_context(nc.sbuf_tensor("sb_" + name, shape, dt))

        bank = ctx.enter_context(nc.psum_tensor("bank", [P, 8, 512], F32))

        X = sb("X", [R, T, D])
        XN = sb("XN", [R, T, D])
        XT = sb("XT", [P, C, N])
        AT = sb("AT", [R, T, N])
        ident = sb("ident", [P, P])
        ones = sb("ones", [P, P])
        SEL = sb("SEL", [E, E, P])
        zeros = sb("zeros", [E, P])
        nop = sb("nop", [1, 48])
        iota8 = sb("iota8", [R, E])
        fvec = sb("fvec", [P, FVW])
        lvec = sb("lvec", [P, LVW])
        rvec = sb("rvec", [P, 4, D])
        rbias = sb("rbias", [P, RBW])
        gw = sb("gw", [P, C, GWW])
        b2 = sb("b2", [E, D])
        rcntb = sb("rcntb", [P, N])
        dinvb = sb("dinvb", [P, N])
        dinvr = sb("dinvr", [R, T])
        half8 = sb("half8", [P, 1])
        st = sb("st", [P, 8, 6])
        mv = sb("mv", [P, T, 2])
        ve = sb("ve", [P, T])
        rstd = sb("rstd", [P, T])
        bsc = sb("bsc", [P, C])
        bsh = sb("bsh", [P, C])
        bms = sb("bms", [P, C])
        degr = sb("degr", [R, T])
        gq = sb("gq", [P, 1])
        bq8 = sb("bq8", [P, C])
        ss = sb("ss", [R, 2, T * H])
        ssr = sb("ssr", [R, 2, T * H])
        nmx = sb("nmx", [R, T * H])
        rden = sb("rden", [R, H])
        LG = sb("LG", [R, T, E])
        EX = sb("EX", [R, T, E])
        PR = sb("PR", [R, T, E])
        COMB = sb("COMB", [R, T, E])
        EQ = sb("EQ", [R, 2, T, E])
        red = sb("red", [R, 3, T])
        m8 = sb("m8", [R, T, 8])
        i8 = sb("i8", [R, T, 8], U32)
        if8 = sb("if8", [R, T, 8])
        m1b = sb("m1b", [P, F1 // P])
        WGT = sb("WGT", [R, T, H * NB])

        W = sb("W", [P, 17408])
        rA = sb("rA", [P, T * D])
        rB = sb("rB", [P, T * D])
        rC = sb("rC", [P, C * N])
        rDE = sb("rDE", [P, C * N + T * H * (DH + 1)])
        rF = sb("rF", [P, 4 * N])
        rG = sb("rG", [P, T * N])

        def rows(r):
            return r[0:R, 0:T * D].rearrange("p (t d) -> p t d", t=T)

        def feats(r, at=0):
            return r[:, at:at + C * N].rearrange("p (c n) -> p c n", c=C)

        QR, KR, OR = rows(rA), rows(rB), rows(rA)
        QT, KT = feats(rC), feats(rDE)
        V = rDE[0:R, C * N:].rearrange("p (t h d) -> p t h d", t=T, h=H)
        OT = feats(rB)
        YT = feats(rC)
        MT, HB = feats(rA), feats(rB)
        HC, X1T = feats(rC), feats(rDE)
        SM = rF[0:R, 0:2 * N].rearrange("p (b n) -> p b n", b=2)
        PT = rF[0:R, 2 * N:4 * N].rearrange("p (b t n) -> p b t n", b=2, t=T)
        RT = rF[:, 0:N]
        hs = rF[:, 0:2 * 375].rearrange("p (b n) -> p b n", b=2)
        hg = rF[:, 750:2 * 750].rearrange("p (b n) -> p b n", b=2)
        combT = rF[0:E, 1500:1500 + N]
        CB = rDE[:, 0:E * N].rearrange("p (e n) -> p e n", e=E)
        MASK = rG[0:R, :].rearrange("p (t n) -> p t n", t=T)
        CM = rG[0:R, 0:N]
        OH = rA[0:R, 0:4 * 640].bitcast(BF16).rearrange("p (s k n) -> p s k n", s=4, k=2)
        iota16 = rB[0:R, 0:320].bitcast(F16)
        idxi = rB[0:R, 320:320 + 2 * ET].bitcast(I32)
        idxf = rB[0:R, 480:480 + 2 * ET]
        diag = rB[0:R, 640:640 + N].rearrange("p (t n) -> p t n", t=T)
        cmx = rB[:, 1280:1280 + N]
        SQ = rF[0:R, 0:2 * D].rearrange("p (b n) -> p b n", b=2)
        BS = rA[0:R, 0:T * BASES].rearrange("p (t n) -> p t n", t=T)
        XW = rows(rA)
        AG = rB[0:R, 0:T * BASES].rearrange("p (t n) -> p t n", t=T)
        CV = rC[0:R, 0:4 * D].rearrange("p (b n) -> p b n", b=4)

        def mat(at, k, n):
            return W[:, at:at + k * n].rearrange("p (c n) -> p c n", c=k)

        Wl, Wr = mat(0, C, D), mat(2048, C, D)
        Wq, Wk, Wv, Wo = (mat(4096 + 2048 * i, C, D) for i in range(4))
        Wf1, Wf2 = mat(16384, C, P), W[:, 16896:17408]
        Wb, Wres = mat(14336, C, BASES), mat(15360, C, D)
        W3 = mat(4096, C, D)
        M0 = [12288 + 1024 * e if e < 4 else 1024 * (e - 4) for e in range(E)]
        M1 = [1024 * s for s in range(4)]
        M2 = [6144 + 1024 * e for e in range(E)]
        M3 = [1536 * s for s in range(4)]

        def bcast(ap, k):
            return ap.unsqueeze(2).broadcast_to([ap.shape[0], ap.shape[1], k])

        GROUPS = [(m, lo, hi) for m in range(C) for lo, hi in HALVES]
        ATT = 5 * 8

        ROUTER_OPS = (6, 24, 21, 24)
        ROUTED = [sum(ROUTER_OPS[:r]) for r in range(4)]
        UNITS = [2 * E * j for j in (1, F1 // P, 1, F3 // P)]
        UB = [sum(UNITS[:r]) for r in range(4)]

        block = ctx.enter_context(nc.Block())

        def with_layers(sp):
            names = ("g_q_full", "g_k_full", "g_v_full", "g_wo_full")
            counts = (8, 8, 5, 8)
            with sp.Fori(0, LAYERS) as layer:
                sp.wait_ge(S("g_x2"), layer * 4)
                sp.dma_start(lvec[:], A["lvec"][bass.ds(layer, 1)].rearrange("l p n -> (l p) n")).then_inc(S("ld_lvec"), 16)
                for i in range(4):
                    sp.wait_ge(S(names[i]), layer * counts[i])
                    sp.dma_start(W[:, 4096 + 2048 * i:6144 + 2048 * i],
                                 A["w_g"][bass.ds(layer, 1), :, i].rearrange("l p n -> (l p) n")).then_inc(S(f"ld_g{i}"), 16)
                sp.wait_ge(S("g_w2_full"), layer * 8)
                sp.dma_start(W[:, 16384:17408], A["w_gf"][bass.ds(layer, 1)].rearrange("l p n -> (l p) n")).then_inc(S("ld_gf"), 16)

        def stream(sp, r, J, slots, width, src):
            for j in range(4):
                sp.dma_start(W[:, slots[j]:slots[j] + width], src[0, j]).then_inc(S(f"ld_m{r}_{j}"), 16)
            with sp.Fori(0, E - 1) as e:
                for j in range(4, J + 4):
                    sp.wait_ge(S("mo_used"), e * (2 * J) + (UB[r] + 2 * (j - 4) + 2))
                    piece = src[e, j] if j < J else src[e + 1, j - J]
                    sp.dma_start(W[:, slots[j % 4]:slots[j % 4] + width], piece).then_inc(S(f"ld_m{r}_{j % 4}"), 16)
            for j in range(4, J):
                sp.wait_ge(S("mo_used"), (E - 1) * 2 * J + UB[r] + 2 * (j - 4) + 2)
                sp.dma_start(W[:, slots[j % 4]:slots[j % 4] + width], src[E - 1, j]).then_inc(S(f"ld_m{r}_{j % 4}"), 16)

        @block.sync
        def _(sp):
            sp.dma_start(idxi, A["edges"]).then_inc(S("ld_idx"), 16)
            sp.dma_start(X[:], A["x"]).then_inc(S("ld_x"), 16)
            sp.dma_start(fvec[:], A["fvec"]).then_inc(S("ld_small"), 16)
            sp.dma_start(W[:, 0:4096], A["w_l0"]).then_inc(S("ld_l0"), 16)
            sp.dma_start(gw[:], A["gw"]).then_inc(S("ld_small"), 16)
            sp.dma_start(rbias[:], A["rbias"].to_broadcast([P, RBW])).then_inc(S("ld_small"), 16)
            sp.dma_start(b2[:], A["b2"][0]).then_inc(S("ld_b2"), 16)
            for i in range(4):
                sp.dma_start(W[:, 4096 + 2048 * i:6144 + 2048 * i], A["w_a0"][:, i]).then_inc(S(f"ld_a0_{i}"), 16)
            sp.dma_start(W[:, 12288:16384].rearrange("p (e n) -> p e n", e=4),
                         A["w_m0"][0:4].rearrange("e p n -> p e n")).then_inc(S("ld_m0a"), 16)
            sp.wait_ge(S("h0_full"), 8)
            sp.dma_start(W[:, 0:4096].rearrange("p (e n) -> p e n", e=4),
                         A["w_m0"][4:8].rearrange("e p n -> p e n")).then_inc(S("ld_m0b"), 16)
            sp.wait_ge(S("kvq_full"), 15)
            sp.wait_ge(S("wo0_full"), 8)
            sp.dma_start(rvec[:, 0:2], A["rvec1"].rearrange("a k d -> a k d").to_broadcast([P, 2, D])).then_inc(S("ld_rvec1"), 16)
            with_layers(sp)
            J = F1 // P
            sp.wait_ge(S("mo_out"), 5)
            sp.dma_start(b2[:], A["b2"][1]).then_inc(S("ld_b2"), 16)
            stream(sp, 1, J, M1, 1024, A["w_m1"])
            sp.wait_ge(S("lf_vec"), 26)
            sp.dma_start(rvec[:], A["rvec2"].to_broadcast([P, 4, D])).then_inc(S("ld_rvec2"), 16)
            sp.dma_start(W[:, 14336:17408], A["w_l2"]).then_inc(S("ld_l2"), 16)
            sp.dma_start(W[:, 6144:14336].rearrange("p (e n) -> p e n", e=8),
                         A["w_m2"].rearrange("e p n -> p e n")).then_inc(S("ld_m2"), 16)
            sp.wait_ge(S("mo_out"), 10)
            sp.dma_start(b2[:], A["b2"][2]).then_inc(S("ld_b2"), 16)
            sp.dma_start(W[:, 4096:6144], A["w_l3"]).then_inc(S("ld_l3"), 16)
            sp.wait_ge(S("mo_out"), 15)
            sp.dma_start(b2[:], A["b2"][3]).then_inc(S("ld_b2"), 16)
            sp.wait_ge(S("xw_full"), 5)
            stream(sp, 3, F3 // P, M3, 1536, A["w_m3"])
            for t in range(T):
                sp.wait_ge(S("mo_out"), 3 * T + t + 1)
                sp.dma_start(out[:, t], X[:, t]).then_inc(S("stored"), 16)
            sp.wait_ge(S("stored"), 16 * T)

        @block.gpsimd
        def _(pool):
            c = Chain(pool, S("consts"))
            c(pool.iota(iota16[:, 0:N], [[1, N]], base=0, channel_multiplier=0, allow_small_or_imprecise_dtypes=True))
            c(pool.memset(ident[:], 0.0))
            c(pool.memset(ones[:], 1.0))
            c(pool.memset(zeros[:], 0.0))
            c(pool.memset(half8[:], -0.5))
            c(pool.memset(SEL[:], 0.0))
            c(pool.memset(CM, 0.0))
            c(pool.iota(iota8[:], [[1, E]], base=0, channel_multiplier=0, allow_small_or_imprecise_dtypes=True))
            c.sync()
            c(pool.affine_select(out=ident[:], in_=ident[:], compare_op=ALU.not_equal, fill=1.0,
                                 base=0, pattern=[[-1, P]], channel_multiplier=1))
            c(pool.affine_select(out=SEL[:], in_=SEL[:], compare_op=ALU.not_equal, fill=1.0,
                                 base=0, pattern=[[-1, E], [0, P]], channel_multiplier=1))
            c(pool.affine_select(out=CM[:, N - R:N], in_=CM[:, N - R:N], compare_op=ALU.is_ge, fill=NEG,
                                 base=0, pattern=[[-1, R]], channel_multiplier=1))
            assert c.n == 11

            def power(dst, src, k, ready, count, done):
                pool.wait_ge(ready, count)
                pool.tensor_tensor(dst, src, half8[0:src.shape[0], :].broadcast_to([src.shape[0], k]), ALU.pow).then_inc(done, 1)

            def ln(k):
                power(rstd[0:R, :], ve[0:R, :], T, S("ln_vec"), 16 * k + 11, S("ln_pow"))

            ln(0)
            power(dinvr[:], degr[:], T, S("deg_vec"), 5, S("deg_pow"))
            power(rstd[:, 0:C], ve[:, 0:C], C, S("bn0_vec"), 13, S("bn0_pow"))
            ln(1)
            ln(2)
            for i in range(2):
                power(ssr[:, i], ss[:, i], T * H, S("qk_vec"), 11 * (i + 1), S("qk_pow"))
            ln(3)
            with pool.Fori(0, LAYERS) as layer:
                for b in (1, 2):
                    power(rstd[:, 0:C], ve[:, 0:C], C, S(f"g_bn{b}_vec"), layer * 17 + 14, S(f"g_bn{b}_pow"))
            power(rstd[0:R, :], ve[0:R, :], T, S("lf_vec"), 11, S("lf_pow"))
            ln(4)
            ln(5)
            power(rstd[0:R, :], ve[0:R, :], T, S("l2_vec"), 52 + 11, S("l2_pow"))
            ln(6)
            ln(7)
            power(rstd[:, 0:C], ve[:, 0:C], C, S("bn3_vec"), 13, S("bn3_pow"))
            ln(8)

        @block.tensor
        def _(pe):
            def to_feats(src, full, base=0):
                for t in range(T):
                    for c in range(C):
                        mm = pe.transpose(bank[:, t, c * R:(c + 1) * R], src[:, t, c * P:(c + 1) * P], ident[0:R, 0:R])
                    mm.then_inc(full, 1)

            def feats_ready(k):
                pe.wait_ge(S("tr_v"), 3 * (k + 1))
                pe.wait_ge(S("tr_a"), 2 * (k + 1))

            def to_rows(src, full):
                for t in range(T):
                    for c in range(C):
                        mm = pe.transpose(bank[0:R, t, c * P:(c + 1) * P], src[:, c, t * R:(t + 1) * R], ident[:])
                    mm.then_inc(full, 1)

            def project(pairs, full, before=None, base=0):
                for j, (m, lo, hi) in enumerate(GROUPS):
                    if before is not None:
                        pe.wait_ge(before, base + j + 1)
                    steps = [(w, x, c) for w, x in pairs for c in range(x.shape[1])]
                    for n, (w, x, c) in enumerate(steps):
                        mm = pe.matmul(bank[:, j, 0:hi - lo], w[:, c, m * P:(m + 1) * P], x[:, c, lo:hi],
                                       start=(n == 0), stop=(n == len(steps) - 1))
                    mm.then_inc(full, 1)

            def row_group(b, x, t, w, full, cols=D):
                for c in range(C):
                    mm = pe.matmul(bank[0:R, b, 0:cols], x[:, c, t * R:(t + 1) * R], w[:, c, 0:cols],
                                   start=(c == 0), stop=(c == C - 1))
                if full is not None:
                    mm.then_inc(full, 1)

            def attention(a, base, causal):
                for s in range(ATT + 2):
                    if s < ATT:
                        t, h = divmod(s, H)
                        kn = (t + 1) * R if causal else N
                        if s >= 2:
                            pe.wait_ge(S(f"{a}_mask"), base(ATT) + s - 1)
                        hp = slice((h % 2) * DH, (h % 2) * DH + DH)
                        for lo, hi in ((0, min(kn, 512)), (512, kn)):
                            if lo < hi:
                                mm = pe.matmul(bank[0:R, 2 * (s % 2) + lo // 512, 0:hi - lo],
                                               QT[hp, h // 2, t * R:(t + 1) * R], KT[hp, h // 2, lo:hi], start=True, stop=True)
                        mm.then_inc(S(f"{a}_s"), 1)
                    if 1 <= s <= ATT:
                        u = s - 1
                        t, h = divmod(u, H)
                        pe.wait_ge(S(f"{a}_exp"), base(ATT) + u + 1)
                        if u >= 1:
                            pe.wait_ge(S(f"{a}_pt"), base(ATT) + u)
                        for kb in range(t + 1 if causal else T):
                            mm = pe.transpose(bank[0:R, 4 + kb // 4, (kb % 4) * P:(kb % 4) * P + R],
                                              SM[:, u % 2, kb * R:(kb + 1) * R], ident[0:R, 0:R])
                        mm.then_inc(S(f"{a}_tr"), 1)
                    if s >= 2:
                        u = s - 2
                        t, h = divmod(u, H)
                        pe.wait_ge(S(f"{a}_pt"), base(ATT) + u + 1)
                        if h == 0 and t >= 1:
                            pe.wait_ge(S(f"{a}_norm"), base(3 * T) + 3 * t)
                        last = t if causal else T - 1
                        for kb in range(last + 1):
                            mm = pe.matmul(bank[0:R, 6 + h // 4, (h % 4) * (DH + 1):(h % 4 + 1) * (DH + 1)],
                                           PT[:, u % 2, kb, :], V[:, kb, h, :], start=(kb == 0), stop=(kb == last))
                        mm.then_inc(S(f"{a}_av"), 1)

            def router(r, xt):
                for t in range(T):
                    for c in range(C):
                        mm = pe.matmul(bank[0:R, 0, t * E:(t + 1) * E], xt[:, c, t * R:(t + 1) * R],
                                       gw[:, c, GW[r]:GW[r] + E], start=(c == 0), stop=(c == C - 1))
                mm.then_inc(S("rt_pe"), 1)
                pe.wait_ge(S("rt_vec"), ROUTED[r] + ROUTER_OPS[r])
                for t in range(T):
                    mm = pe.transpose(bank[0:E, 1 + t // 4, (t % 4) * R:(t % 4 + 1) * R], COMB[:, t], ident[0:R, 0:R])
                mm.then_inc(S("rt_pe"), 1)
                pe.wait_ge(S("rt_act"), 3 * r + 3)
                for e in range(E):
                    for i, (lo, hi) in enumerate(HALVES):
                        g = 2 * e + i
                        if g >= 5:
                            pe.wait_ge(S("rt_cb"), 2 * E * r + g - 4)
                        pe.matmul(bank[:, 3 + g % 5, 0:hi - lo], SEL[:, e], combT[:, lo:hi],
                                  start=True, stop=True).then_inc(S("rt_spread"), 1)

            def mixture(r, xt, J, slots, width, glu):
                pe.wait_ge(S("rt_cb"), 2 * E * (r + 1))
                pe.wait_ge(S("ld_b2"), 16 * (r + 1))
                for t in range(T):
                    pe.matmul(bank[0:R, t, :], combT[:, t * R:(t + 1) * R], b2[:], start=True, stop=False, skip_group_check=True)

                def first(u, e):
                    j, i = divmod(u, 2)
                    lo, hi = HALVES[i]
                    w = W[:, slots[j % len(slots)]:slots[j % len(slots)] + width].rearrange("p (k c n) -> p k c n", c=C, n=P)
                    if i == 0 and J == 1:
                        pe.wait_ge(S("ld_m2" if r == 2 else "ld_m0a" if j < 4 else "ld_m0b"), 16)
                    elif i == 0:
                        pe.wait_ge(S(f"ld_m{r}_{j % 4}"), e * (16 * (J // 4)) + 16 * (j // 4 + 1))
                    for k in range(2 if glu else 1):
                        if k == 1 and u >= 1:
                            pe.wait_ge(S("mo_act"), e * (2 * J) + (UB[r] + u))
                        b = 5 + ((2 * u + k) % 3 if glu else u % 3)
                        for c in range(C):
                            mm = pe.matmul(bank[:, b, 0:hi - lo], w[:, k, c], xt[:, c, lo:hi], start=(c == 0), stop=(c == C - 1))
                        mm.then_inc(S("mo_h"), 1)

                def second(u, e, last):
                    j, i = divmod(u, 2)
                    at = slots[j % len(slots)] + (2 if glu else 1) * D
                    pe.wait_ge(S("mo_hs"), (e * (2 * J) + u + 1) * (2 if glu else 1) + UB[r])
                    for t in range(3 * i, 3 + 2 * i):
                        k = t - 3 * i
                        mm = pe.matmul(bank[0:R, t, :], hs[:, u % 2, k * R:(k + 1) * R], W[:, at:at + D],
                                       start=False, stop=last, skip_group_check=True)
                    mm.then_inc(S("mo_used"), 1)

                if J == 1:
                    for u in range(2 * E + 1):
                        if u < 2 * E:
                            first(u, 0)
                        if u >= 1:
                            second(u - 1, 0, u >= 2 * E - 1)
                else:
                    with pe.Fori(0, E) as e:
                        for u in range(2 * J + 1):
                            if u < 2 * J:
                                first(u, e)
                            if u >= 1:
                                second(u - 1, e, False)
                    for t in range(T):
                        mm = pe.matmul(bank[0:R, t, :], zeros[:, 0:R], b2[:], start=False, stop=True, skip_group_check=True)
                    mm.then_inc(S("mo_closed"), 1)

            def edge_tile(s, ready, first, last=False):
                pe.wait_ge(S("oh_ready"), ready)
                for k in range(T):
                    pe.matmul(bank[0:R, k, :], OH[:, s, 0, k * R:(k + 1) * R], OH[:, s, 1, 0:512],
                              start=first, stop=last, skip_group_check=True)
                for k in range(T):
                    mm = pe.matmul(bank[0:R, 5 + k // 4, (k % 4) * (N - 512):(k % 4 + 1) * (N - 512)],
                                   OH[:, s, 0, k * R:(k + 1) * R], OH[:, s, 1, 512:N],
                                   start=first and k % 4 == 0, stop=last, skip_group_check=True)
                mm.then_inc(S("oh_used"), 1)

            for s in range(4):
                edge_tile(s, 2 * s + 2, s == 0)
            with pe.Fori(1, ET // 4 - 1) as i:
                for s in range(4):
                    edge_tile(s, i * 8 + 2 * s + 2, False)
            for s in range(4):
                edge_tile(s, 2 * (ET - 4 + s) + 2, False, s == 3)
            pe.wait_ge(S("consts"), 11)
            pe.wait_ge(S("at_a"), 5)
            pe.wait_ge(S("at_v"), 2)
            for i, (lo, hi) in enumerate(HALVES):
                for k in range(T):
                    mm = pe.matmul(bank[:, 5 + i, 0:hi - lo], ones[0:R, :], AT[:, k, lo:hi], start=(k == 0), stop=(k == T - 1))
                mm.then_inc(S("deg_pe"), 1)
            for t in range(T):
                for k in range(T):
                    mm = pe.matmul(bank[0:R, 7, t:t + 1], AT[:, k, t * R:(t + 1) * R], ones[0:R, 0:1], start=(k == 0), stop=(k == T - 1))
            mm.then_inc(S("deg_pe"), 1)
            pe.wait_ge(S("ln_vec"), 16)
            to_feats(XN, S("tr_full"))
            pe.wait_ge(S("deg_vec"), 10)
            for i, tiles in enumerate(((0, 1, 2), (3, 4))):
                for k, t in enumerate(tiles):
                    mm = pe.matmul(bank[:, 5 + i, k * R:(k + 1) * R], ones[0:R, :], diag[:, t, :], start=True, stop=True)
                mm.then_inc(S("deg_pe"), 1)
            feats_ready(0)
            pe.wait_ge(S("deg_vec"), 12)
            for j, (m, lo, hi) in enumerate(GROUPS):
                for k in range(T):
                    mm = pe.matmul(bank[:, j, 0:hi - lo], XN[:, k, m * P:(m + 1) * P], AT[:, k, lo:hi], start=(k == 0), stop=(k == T - 1))
                mm.then_inc(S("agg_full"), 1)
            pe.wait_ge(S("ld_l0"), 16)
            pe.wait_ge(S("agg_done"), 8)
            project([(Wl, MT), (Wr, XT[:])], S("h0_full"))
            pe.wait_ge(S("bn0_out"), 4)
            to_rows(HB, S("rows0_full"))

            pe.wait_ge(S("ln_vec"), 48)
            to_feats(XN, S("tr_full"))
            pe.wait_ge(S("aff_done"), 4)
            for g in range(3 * T):
                i, t = divmod(g, T)
                if t == 0:
                    pe.wait_ge(S(f"ld_a0_{i}"), 16)
                if g >= 8:
                    pe.wait_ge(S("kvq_done"), g - 7)
                row_group(g % 8, XT, t, (Wq, Wk, Wv)[i], S("kvq_full"))
            pe.wait_ge(S("kvq_done"), 15)
            pe.wait_ge(S("qk_vec"), 27)
            to_feats(QR, S("tr_full"))
            feats_ready(2)
            pe.wait_ge(S("qk_vec"), 32)
            to_feats(KR, S("tr_full"))
            feats_ready(3)
            attention("a0", lambda k: 0, True)
            pe.wait_ge(S("a0_norm"), 3 * T)
            to_feats(OR, S("tr_full"))
            feats_ready(4)
            pe.wait_ge(S("ld_a0_3"), 16)
            project([(Wo, OT)], S("wo0_full"))
            pe.wait_ge(S("wo0_done"), 8)
            pe.wait_ge(S("ld_small"), 48)
            router(0, YT)
            mixture(0, YT, 1, M0, 1024 - D, False)

            for t in range(T):
                if t == 0:
                    pe.wait_ge(S("mo_out"), 5)
                for k in range(T):
                    mm = pe.transpose(bank[0:R, t, 0 + k % 4 * P:k % 4 * P + R] if k < 4 else bank[0:R, 5 + t // 4, t % 4 * P:t % 4 * P + R],
                                      AT[:, k, t * R:(t + 1) * R], ident[0:R, 0:R])
                mm.then_inc(S("msk_pe"), 1)
            pe.wait_ge(S("msk_done"), 10)
            pe.wait_ge(S("ln_vec"), 64)
            to_feats(XN, S("tr_full"))
            feats_ready(5)
            with pe.Fori(0, LAYERS) as layer:
                pe.wait_ge(S("g_x2"), layer * 4)
                pe.wait_ge(S("ld_g0"), layer * 16 + 16)
                project([(Wq, XT[:])], S("g_q_full"))
                pe.wait_ge(S("ld_g1"), layer * 16 + 16)
                project([(Wk, XT[:])], S("g_k_full"), S("g_q_done"), layer * 8)
                pe.wait_ge(S("ld_g2"), layer * 16 + 16)
                for t in range(T):
                    pe.wait_ge(S("g_k_done"), layer * 8 + t + 1)
                    row_group(t, XT, t, Wv, S("g_v_full"))
                pe.wait_ge(S("g_k_done"), layer * 8 + 8)
                pe.wait_ge(S("g_v_done"), layer * 5 + 5)
                attention("g", lambda k: layer * k, False)
                pe.wait_ge(S("g_norm"), layer * (3 * T) + 3 * T)
                to_feats(OR, S("g_tr_full"))
                pe.wait_ge(S("g_tr_v"), layer * 3 + 3)
                pe.wait_ge(S("g_tr_a"), layer * 2 + 2)
                pe.wait_ge(S("ld_g3"), layer * 16 + 16)
                project([(Wo, OT)], S("g_wo_full"))
                pe.wait_ge(S("g_x1"), layer * 4 + 4)
                pe.wait_ge(S("ld_gf"), layer * 16 + 16)
                for i, (lo, hi) in enumerate(HALVES):
                    for c in range(C):
                        mm = pe.matmul(bank[:, i, 0:hi - lo], Wf1[:, c], X1T[:, c, lo:hi], start=(c == 0), stop=(c == C - 1))
                    mm.then_inc(S("g_f1_full"), 1)
                pe.wait_ge(S("g_f1_done"), layer * 2 + 2)
                for j, (m, lo, hi) in enumerate(GROUPS):
                    pe.matmul(bank[:, j, 0:hi - lo], Wf2[:, m * P:(m + 1) * P], RT[:, lo:hi],
                              start=True, stop=True).then_inc(S("g_w2_full"), 1)
            pe.wait_ge(S("g_x2"), 4 * LAYERS)
            to_rows(XT, S("lf_full"))

            pe.wait_ge(S("ln_vec"), 80)
            to_feats(XN, S("tr_full"))
            feats_ready(6)
            router(1, XT)
            mixture(1, XT, F1 // P, M1, 1024 - D, False)

            pe.wait_ge(S("ln_vec"), 96)
            pe.wait_ge(S("mo_out"), 10)
            to_feats(XN, S("tr_full"))
            feats_ready(7)
            pe.wait_ge(S("ld_l2"), 16)
            for t in range(T):
                row_group(t, XT, t, Wb, None, BASES)
                for c in range(C):
                    mm = pe.matmul(bank[0:R, 5, t * 32:(t + 1) * 32], XT[:, c, t * R:(t + 1) * R],
                                   gw[:, c, GW["comb"]:GW["comb"] + 32], start=(c == 0), stop=(c == C - 1))
                mm.then_inc(S("bs_full"), 1)
            pe.wait_ge(S("bs_done"), 5)
            pe.wait_ge(S("self_loops"), 5)
            for t in range(T):
                b = (6, 7, 0, 1, 2)[t]
                for k in range(T):
                    mm = pe.matmul(bank[0:R, b, 0:BASES], AT[:, k, t * R:(t + 1) * R], BS[:, k], start=(k == 0), stop=(k == T - 1))
                mm.then_inc(S("ag_full"), 1)
            for t in range(T):
                b = (3, 4, 5, 6, 7)[t]
                if b >= 5:
                    pe.wait_ge(S("l2_vec"), 5)
                row_group(b, XT, t, Wres, S("res_full"))

            pe.wait_ge(S("ln_vec"), 112)
            to_feats(XN, S("tr_full"))
            feats_ready(8)
            router(2, XT)
            mixture(2, XT, 1, M2, 1024 - D, False)

            pe.wait_ge(S("ln_vec"), 128)
            pe.wait_ge(S("mo_out"), 15)
            to_feats(XN, S("tr_full"))
            feats_ready(9)
            pe.wait_ge(S("ld_l3"), 16)
            for t in range(T):
                row_group(t, XT, t, W3, S("xw_full"))
            pe.wait_ge(S("xw_done"), 5)
            for j, (m, lo, hi) in enumerate(GROUPS):
                for k in range(T):
                    mm = pe.matmul(bank[:, j, 0:hi - lo], XW[:, k, m * P:(m + 1) * P], AT[:, k, lo:hi], start=(k == 0), stop=(k == T - 1))
                mm.then_inc(S("h3_full"), 1)
            pe.wait_ge(S("bn3_out"), 4)
            to_rows(HB, S("rows3_full"))

            pe.wait_ge(S("ln_vec"), 144)
            to_feats(XN, S("tr_full"))
            feats_ready(10)
            router(3, XT)
            mixture(3, XT, F3 // P, M3, 1536 - D, True)

        @block.scalar
        def _(act):
            def copy_feats(dst, full, done, fbase, dbase, scale=None):
                for t in (1, 3):
                    act.wait_ge(full, fbase + t + 1)
                    act.activation(dst[:, :, t * R:(t + 1) * R], bank[:, t, 0:C * R].rearrange("p (c n) -> p c n", c=C),
                                   ACT.Copy, scale=1.0 if scale is None else scale).then_inc(done, 1)

            def feats(k, dst, scale=None):
                copy_feats(dst, S("tr_full"), S("tr_a"), T * k, 2 * k, scale)

            def bn_apply(src, dst, func, ready, count, done):
                act.wait_ge(ready, count)
                for m in range(C):
                    act.activation(dst[:, m], src[:, m], func, scale=bsc[:, m:m + 1], bias=bsh[:, m:m + 1]).then_inc(done, 1)

            def exps(a, base, causal):
                for s in range(ATT + (2 if causal else 0)):
                    if s < ATT:
                        kn = (s // H + 1) * R if causal else N
                        act.wait_ge(S(f"{a}_mask"), base(ATT) + s + 1)
                        act.activation(SM[:, s % 2, 0:kn], SM[:, s % 2, 0:kn], ACT.Exp, scale=-1.0,
                                       bias=nmx[:, s:s + 1]).then_inc(S(f"{a}_exp"), 1)
                    if causal and s >= 1 and s <= ATT:
                        u = s - 1
                        act.wait_ge(S(f"{a}_tr"), u + 1)
                        if u >= 2:
                            act.wait_ge(S(f"{a}_av"), u - 1)
                        nb = u // H + 1
                        n4 = min(nb, 4)
                        ins = act.activation(PT[:, u % 2, 0:n4, :],
                                             bank[0:R, 4, :].rearrange("p (k n) -> p k n", k=4)[:, 0:n4, 0:R], ACT.Copy)
                        if nb > 4:
                            ins = act.activation(PT[:, u % 2, 4, :], bank[0:R, 5, 0:R], ACT.Copy)
                        ins.then_inc(S(f"{a}_pt"), 1)

            def router(r):
                act.wait_ge(S("rt_vec"), ROUTED[r] + 3)
                act.activation(EX[:], LG[:], ACT.Exp).then_inc(S("rt_act"), 1)
                act.wait_ge(S("rt_pe"), 2 * r + 2)
                act.activation(combT[:, 0:500], bank[0:E, 1, 0:500], ACT.Copy).then_inc(S("rt_act"), 1)
                act.activation(combT[:, 500:N], bank[0:E, 2, 0:R], ACT.Copy).then_inc(S("rt_act"), 1)
                for e in range(E):
                    for i, (lo, hi) in enumerate(HALVES):
                        g = 2 * e + i
                        act.wait_ge(S("rt_spread"), 2 * E * r + g + 1)
                        act.activation(CB[:, e, lo:hi], bank[:, 3 + g % 5, 0:hi - lo], ACT.Copy).then_inc(S("rt_cb"), 1)

            def mixture(r, J, glu, func, bcol):
                k = 2 if glu else 1

                def unit(u, e, column):
                    i = u % 2
                    lo, hi = HALVES[i]
                    act.wait_ge(S("mo_h"), (e * (2 * J) + u) * k + (UB[r] + 1))
                    if not (isinstance(e, int) and u < 2):
                        act.wait_ge(S("mo_used"), e * (2 * J) + (UB[r] + max(u - 1, 0)))
                    b = 5 + ((2 * u) % 3 if glu else u % 3)
                    dst = hg[:, u % 2, 0:hi - lo]
                    if column is None:
                        ins = act.activation(dst, bank[:, b, 0:hi - lo], func)
                    else:
                        ins = act.activation(dst, bank[:, b, 0:hi - lo], func, bias=column)
                    ins.then_inc(S("mo_act"), 1)

                if J == 1:
                    for u in range(2 * E):
                        unit(u, 0, fvec[:, bcol + u // 2:bcol + u // 2 + 1])
                else:
                    with act.Fori(0, E) as e:
                        for u in range(2 * J):
                            unit(u, e, None)

            def mixture1_bias(act):
                J = F1 // P
                with act.Fori(0, E) as e:
                    act.wait_ge(S("mo1_bias"), e + 1)
                    for u in range(2 * J):
                        i = u % 2
                        lo, hi = HALVES[i]
                        act.wait_ge(S("mo_h"), e * (2 * J) + (UB[1] + u + 1))
                        act.wait_ge(S("mo_used"), e * (2 * J) + (UB[1] + max(u - 1, 0)))
                        act.activation(hg[:, u % 2, 0:hi - lo], bank[:, 5 + u % 3, 0:hi - lo], ACT.Relu,
                                       bias=m1b[:, u // 2:u // 2 + 1]).then_inc(S("mo_act"), 1)

            act.wait_ge(S("oh_used"), ET)
            for k in range(T):
                act.activation(AT[:, k, 0:512], bank[0:R, k, :], ACT.Copy).then_inc(S("at_a"), 1)
            feats(0, XT)
            act.wait_ge(S("ld_small"), 48)
            for j, (m, lo, hi) in enumerate(GROUPS):
                act.wait_ge(S("h0_full"), j + 1)
                act.activation(HB[:, m, lo:hi], bank[:, j, 0:hi - lo], ACT.Identity,
                               bias=fvec[:, FV["l0_b"] + m:FV["l0_b"] + m + 1]).then_inc(S("h0_done"), 1)
            bn_apply(HB, HB, ACT.Relu, S("bn0_vec"), 16, S("bn0_out"))

            feats(1, XT)
            for g in range(3 * T):
                i, t = divmod(g, T)
                act.wait_ge(S("kvq_full"), g + 1)
                if i < 2:
                    ins = act.activation((QR, KR)[i][:, t], bank[0:R, g % 8, :], ACT.Copy)
                else:
                    ins = act.activation(V[:, t, :, 0:DH], bank[0:R, g % 8, :].rearrange("p (h d) -> p h d", h=H), ACT.Copy)
                ins.then_inc(S("kvq_done"), 1)
            act.wait_ge(S("aff_done"), 6)
            feats(2, QT, gq[:, 0:1])
            feats(3, KT)
            exps("a0", lambda k: 0, True)
            feats(4, OT)
            for j, (m, lo, hi) in enumerate(GROUPS):
                act.wait_ge(S("wo0_full"), j + 1)
                act.activation(YT[:, m, lo:hi], bank[:, j, 0:hi - lo], ACT.Copy).then_inc(S("wo0_done"), 1)
            router(0)
            mixture(0, 1, False, ACT.Gelu_apprx_tanh, FV["m0_b1"])

            feats(5, XT)
            with act.Fori(0, LAYERS) as layer:
                act.wait_ge(S("g_bq"), layer + 1)
                for j, (m, lo, hi) in enumerate(GROUPS):
                    act.wait_ge(S("g_q_full"), layer * 8 + j + 1)
                    act.activation(QT[:, m, lo:hi], bank[:, j, 0:hi - lo], ACT.Identity,
                                   scale=float(DH) ** -0.5, bias=bq8[:, m:m + 1]).then_inc(S("g_q_done"), 1)
                for t in range(T):
                    act.wait_ge(S("g_v_full"), layer * 5 + t + 1)
                    act.activation(V[:, t, :, 0:DH], bank[0:R, t, :].rearrange("p (h d) -> p h d", h=H),
                                   ACT.Copy).then_inc(S("g_v_done"), 1)
                exps("g", lambda k: layer * k, False)
                copy_feats(OT, S("g_tr_full"), S("g_tr_a"), layer * T, 0)
                bn_apply(HC, X1T, ACT.Identity, S("g_bn1_vec"), layer * 17 + 17, S("g_x1"))
                for i, (lo, hi) in enumerate(HALVES):
                    act.wait_ge(S("g_f1_full"), layer * 2 + i + 1)
                    act.activation(RT[:, lo:hi], bank[:, i, 0:hi - lo], ACT.Relu,
                                   bias=lvec[:, LV["b1"]:LV["b1"] + 1]).then_inc(S("g_f1_done"), 1)
                bn_apply(HC, XT, ACT.Identity, S("g_bn2_vec"), layer * 17 + 17, S("g_x2"))

            feats(6, XT)
            router(1)
            mixture1_bias(act)

            feats(7, XT)
            act.wait_ge(S("bs_full"), 5)
            for t in range(T):
                act.activation(BS[:, t], bank[0:R, t, 0:BASES], ACT.Copy, scale=dinvr[:, t:t + 1]).then_inc(S("bs_done"), 1)

            feats(8, XT)
            router(2)
            mixture(2, 1, False, ACT.Gelu_apprx_tanh, FV["m2_b1"])

            feats(9, XT)
            for t in range(T):
                act.wait_ge(S("xw_full"), t + 1)
                act.activation(XW[:, t], bank[0:R, t, :], ACT.Copy, scale=dinvr[:, t:t + 1]).then_inc(S("xw_done"), 1)
            bn_apply(HB, HB, ACT.Gelu, S("bn3_vec"), 16, S("bn3_out"))

            feats(10, XT)
            router(3)
            mixture(3, F3 // P, True, ACT.Silu, None)

        @block.vector
        def _(dve):
            def copy_feats(dst, full, done, fbase, scale=None):
                for t in (0, 2, 4):
                    dve.wait_ge(full, fbase + t + 1)
                    src = bank[:, t, 0:C * R].rearrange("p (c n) -> p c n", c=C)
                    d = dst[:, :, t * R:(t + 1) * R]
                    ins = dve.tensor_copy(d, src) if scale is None else dve.tensor_scalar(d, src, scale, None, ALU.mult)
                    ins.then_inc(done, 1)

            def feats(k, dst, scale=None):
                copy_feats(dst, S("tr_full"), S("tr_v"), T * k, scale)

            def stats_rows(c, src):
                for t in range(T):
                    c(dve.bn_stats(st[0:R, t], src(t)))
                for t in range(T):
                    if t == 0:
                        c.sync()
                    c(dve.bn_aggr(mv[0:R, t], st[0:R, t]))
                c.sync()
                c(dve.tensor_scalar(ve[0:R, :], mv[0:R, :, 1], EPS, None, ALU.add))

            def ln(k, src=X):
                c = Chain(dve, S("ln_vec"), 16 * k)
                stats_rows(c, lambda t: src[:, t])
                dve.wait_ge(S("ln_pow"), k + 1)
                for t in range(T):
                    c(dve.tensor_scalar(XN[:, t], src[:, t], mv[0:R, t, 0:1], rstd[0:R, t:t + 1], ALU.subtract, ALU.mult))

            def bn(src, done, vec, pow_, gamma, beta, dbase=0, vbase=0, pbase=0):
                c = Chain(dve, vec, vbase)
                for j, (m, lo, hi) in enumerate(GROUPS):
                    dve.wait_ge(done, dbase + j + 1)
                    c(dve.bn_stats(st[:, j], src[:, m, lo:hi]))
                c.sync()
                if not isinstance(vbase, int):
                    c(dve.memset(nop[:, 47:48], 0.0))
                for m in range(C):
                    c(dve.bn_aggr(mv[:, m], st[:, 2 * m:2 * m + 2]))
                c.sync()
                c(dve.tensor_scalar(ve[:, 0:C], mv[:, 0:C, 1], EPS, None, ALU.add))
                dve.wait_ge(pow_, pbase + 1)
                c(dve.tensor_tensor(bsc[:], gamma, rstd[:, 0:C], ALU.mult))
                c.sync()
                c(dve.tensor_tensor(bms[:], mv[:, 0:C, 0], bsc[:], ALU.mult))
                c.sync()
                c(dve.tensor_tensor(bsh[:], beta, bms[:], ALU.subtract))

            def add_rows(full, vec):
                c = Chain(dve, vec)
                for t in range(T):
                    dve.wait_ge(full, t + 1)
                    c(dve.tensor_tensor(XN[:, t], bank[0:R, t, :], XN[:, t], ALU.add))
                    c.sync()
                    c(dve.tensor_tensor(X[:, t], X[:, t], XN[:, t], ALU.add))
                c.sync()

            def attention(a, base, mask, causal):
                cn = Chain(dve, S(f"{a}_norm"), base(3 * T))
                for s in range(ATT + 2):
                    if s < ATT:
                        t = s // H
                        kn = (t + 1) * R if causal else N
                        dve.wait_ge(S(f"{a}_s"), base(ATT) + s + 1)
                        if s >= 2:
                            dve.wait_ge(S(f"{a}_tr"), base(ATT) + s - 1)
                        if not causal:
                            dve.memset(nop[:, s:s + 1], 0.0)
                        scores = bank[0:R, 2 * (s % 2):2 * (s % 2) + 2, :].rearrange("p b n -> p (b n)")[:, 0:kn]
                        dve.tensor_tensor_reduce(out=SM[:, s % 2, 0:kn], in0=scores, in1=mask(t), scale=-1.0, scalar=3e38,
                                                 op0=ALU.add, op1=ALU.min, accum_out=nmx[:, s:s + 1]).then_inc(S(f"{a}_mask"), 1)
                    if not causal and 1 <= s <= ATT:
                        u = s - 1
                        t = u // H
                        dve.wait_ge(S(f"{a}_tr"), base(ATT) + u + 1)
                        if u >= 2:
                            dve.wait_ge(S(f"{a}_av"), base(ATT) + u - 1)
                        at = AT[:, :, t * R:(t + 1) * R]
                        pt = bank[0:R, 4:6, :].rearrange("p b (k n) -> p (b k) n", n=P)[:, 0:T, 0:R]
                        dve.tensor_tensor(PT[:, u % 2], pt, at, ALU.mult).then_inc(S(f"{a}_pt"), 1)
                    if s >= 2 and (s - 2) % H == H - 1:
                        t = (s - 2) // H
                        dve.wait_ge(S(f"{a}_av"), base(ATT) + (t + 1) * H)
                        o = bank[0:R, 6:8, 0:4 * (DH + 1)].rearrange("p b (h d) -> p b h d", h=4)
                        cn(dve.tensor_scalar(rden[:].rearrange("p (b h) -> p b h", b=2), o[:, :, :, DH], 1e-16, None, ALU.add))
                        cn.sync()
                        cn(dve.reciprocal(rden[:], rden[:]))
                        cn.sync()
                        for b in range(2):
                            ins = dve.tensor_tensor(OR[:, t, b * 256:(b + 1) * 256].rearrange("p (h d) -> p h d", h=4),
                                                    o[:, b, :, 0:DH], bcast(rden[:, 4 * b:4 * b + 4], DH), ALU.mult)
                            if b == 1:
                                cn(ins)

            def router(r):
                c = Chain(dve, S("rt_vec"), ROUTED[r])
                dve.wait_ge(S("rt_pe"), 2 * r + 1)
                logits = bank[0:R, 0, 0:T * E].rearrange("p (t e) -> p t e", t=T)
                if r in RB:
                    bias = rbias[0:R, RB[r]:RB[r] + E].unsqueeze(1).broadcast_to([R, T, E])
                    c(dve.tensor_tensor(LG[:], logits, bias, ALU.add))
                else:
                    c(dve.tensor_copy(LG[:], logits))
                c.sync()
                c(dve.tensor_reduce(red[:, 0], LG[:], AX.X, ALU.max))
                c.sync()
                c(dve.tensor_tensor(LG[:], LG[:], bcast(red[:, 0], E), ALU.subtract))
                dve.wait_ge(S("rt_act"), 3 * r + 1)
                c(dve.tensor_reduce(red[:, 1], EX[:], AX.X, ALU.add))
                c.sync()
                c(dve.reciprocal(red[:, 1], red[:, 1]))
                c.sync()
                c(dve.tensor_tensor(COMB[:] if r == 0 else PR[:], EX[:], bcast(red[:, 1], E), ALU.mult))
                if r > 0:
                    c.sync()
                    best = LG if r == 1 else PR
                    for t in range(T):
                        c(dve.max(m8[:, t], best[:, t]))
                    c.sync()
                    for t in range(T):
                        c(dve.max_index(i8[:, t], m8[:, t], best[:, t]))
                    c.sync()
                    c(dve.tensor_copy(if8[:], i8[:]))
                    c.sync()
                    for k in range(2):
                        c(dve.tensor_tensor(EQ[:, k], iota8[:].unsqueeze(1).broadcast_to([R, T, E]),
                                            if8[:, :, k:k + 1].broadcast_to([R, T, E]), ALU.is_equal))
                    c.sync()
                    c(dve.tensor_tensor(EQ[:, 0], EQ[:, 0], EQ[:, 1], ALU.add))
                    c.sync()
                    c(dve.tensor_tensor(COMB[:], PR[:], EQ[:, 0], ALU.mult))
                if r in (1, 3):
                    c.sync()
                    c(dve.tensor_reduce(red[:, 2], COMB[:], AX.X, ALU.add))
                    c.sync()
                    c(dve.reciprocal(red[:, 2], red[:, 2]))
                    c.sync()
                    c(dve.tensor_tensor(COMB[:], COMB[:], bcast(red[:, 2], E), ALU.mult))
                assert c.n == ROUTED[r] + ROUTER_OPS[r]

            def mixture(r, J, glu):
                k = 2 if glu else 1

                def unit(u, e, weights):
                    lo, hi = HALVES[u % 2]
                    n = hi - lo
                    if glu:
                        dve.wait_ge(S("mo_h"), (e * (2 * J) + u) * 2 + (UB[r] + 2))
                    dve.wait_ge(S("mo_act"), e * (2 * J) + (UB[r] + u + 1))
                    if glu:
                        dve.tensor_tensor(hg[:, u % 2, 0:n], hg[:, u % 2, 0:n], bank[:, 5 + (2 * u + 1) % 3, 0:n],
                                          ALU.mult).then_inc(S("mo_hs"), 1)
                        dve.wait_ge(S("mo_hs"), (e * (2 * J) + u) * 2 + (UB[r] + 1))
                    dve.tensor_tensor(hs[:, u % 2, 0:n], hg[:, u % 2, 0:n], weights(lo, hi), ALU.mult).then_inc(S("mo_hs"), 1)

                dve.wait_ge(S("rt_cb"), 2 * E * (r + 1))
                if J == 1:
                    for u in range(2 * E):
                        unit(u, 0, lambda lo, hi: CB[:, u // 2, lo:hi])
                else:
                    with dve.Fori(0, E) as e:
                        if r == 1:
                            dve.wait_ge(S("mo_act"), e * (2 * J) + UB[1])
                            dve.tensor_copy(m1b[:], fvec[:, bass.ds(e * J + FV["m1_b1"], J)]).then_inc(S("mo1_bias"), 1)
                        for u in range(2 * J):
                            unit(u, e, lambda lo, hi: CB[:, bass.ds(e, 1), lo:hi].rearrange("p a n -> p (a n)"))
                c = Chain(dve, S("mo_out"), T * r)
                dve.wait_ge(S("mo_used"), UB[r] + UNITS[r])
                if J > 1:
                    dve.wait_ge(S("mo_closed"), (r + 1) // 2)
                for t in range(T):
                    c(dve.tensor_tensor(X[:, t], X[:, t], bank[0:R, t, :], ALU.add))
                c.sync()

            c = Chain(dve, S("oh_idx"))
            dve.wait_ge(S("ld_idx"), 16)
            c(dve.tensor_copy(idxf, idxi))
            c.sync()
            dve.wait_ge(S("consts"), 11)

            def one_hots(s, at):
                for k in range(2):
                    dve.tensor_scalar(OH[:, s, k, 0:N], iota16[:, 0:N], at(k), None, ALU.is_equal).then_inc(S("oh_ready"), 1)

            for s in range(4):
                one_hots(s, lambda k: idxf[:, k * ET + s:k * ET + s + 1])
            with dve.Fori(1, ET // 4) as i:
                for s in range(4):
                    dve.wait_ge(S("oh_used"), i * 4 + s - 3)
                    one_hots(s, lambda k: idxf[:, bass.ds(i * 4 + (k * ET + s), 1)])
            dve.wait_ge(S("ld_x"), 16)
            ln(0)
            dve.wait_ge(S("oh_used"), ET)
            c = Chain(dve, S("at_v"))
            c(dve.tensor_copy(AT[:, 0:4, 512:N], bank[0:R, 5, 0:4 * (N - 512)].rearrange("p (k n) -> p k n", k=4)))
            c(dve.tensor_copy(AT[:, 4, 512:N], bank[0:R, 6, 0:N - 512]))
            c = Chain(dve, S("deg_vec"))
            for i, (lo, hi) in enumerate(HALVES):
                dve.wait_ge(S("deg_pe"), i + 1)
                c(dve.tensor_scalar(cmx[:, lo:hi], bank[:, 5 + i, 0:hi - lo], 1.0, None, ALU.max))
                c.sync()
                c(dve.reciprocal(rcntb[:, lo:hi], cmx[:, lo:hi]))
            dve.wait_ge(S("deg_pe"), 3)
            c(dve.tensor_scalar(degr[:], bank[0:R, 7, 0:T], 1.0, None, ALU.add))
            feats(0, XT)
            dve.wait_ge(S("deg_pow"), 1)
            for t in range(T):
                c(dve.tensor_scalar(diag[:, t], ident[0:R, 0:R], dinvr[:, t:t + 1], None, ALU.mult))
            for i, (lo, hi) in enumerate(HALVES):
                dve.wait_ge(S("deg_pe"), 4 + i)
                c(dve.tensor_copy(dinvb[:, lo:hi], bank[:, 5 + i, 0:hi - lo]))
            assert c.n == 12
            for j, (m, lo, hi) in enumerate(GROUPS):
                dve.wait_ge(S("agg_full"), j + 1)
                dve.tensor_tensor(MT[:, m, lo:hi], bank[:, j, 0:hi - lo], rcntb[:, lo:hi], ALU.mult).then_inc(S("agg_done"), 1)
            dve.wait_ge(S("ld_small"), 48)
            bn(HB, S("h0_done"), S("bn0_vec"), S("bn0_pow"), fvec[:, FV["l0_g"]:FV["l0_g"] + C], fvec[:, FV["l0_be"]:FV["l0_be"] + C])
            add_rows(S("rows0_full"), S("rows0_vec"))

            ln(1)
            dve.wait_ge(S("ln_vec"), 32)
            ln(2, XN)
            feats(1, XT)
            c = Chain(dve, S("aff_done"))
            dve.wait_ge(S("tr_v"), 6)
            dve.wait_ge(S("tr_a"), 4)
            for k in range(C):
                c(dve.tensor_scalar(XT[:, k], XT[:, k], fvec[:, FV["ln_g"] + k:FV["ln_g"] + k + 1],
                                    fvec[:, FV["ln_b"] + k:FV["ln_b"] + k + 1], ALU.mult, ALU.add))
            c(dve.tensor_scalar(gq[:], fvec[:, FV["qn"]:FV["qn"] + 1], float(DH) ** 0.5, None, ALU.mult))
            c.sync()
            c(dve.tensor_tensor(gq[:], gq[:], fvec[:, FV["kn"]:FV["kn"] + 1], ALU.mult))
            dve.memset(V[:, :, :, DH:DH + 1], 1.0).then_inc(S("v_ones"), 1)
            c = Chain(dve, S("qk_vec"))
            for i, dst in enumerate((QR, KR)):
                for t in range(T):
                    dve.wait_ge(S("kvq_done"), i * T + t + 1)
                    c(dve.tensor_tensor(SQ[:, t % 2], dst[:, t], dst[:, t], ALU.mult))
                    c.sync()
                    c(dve.tensor_reduce(ss[:, i, t * H:(t + 1) * H], SQ[:, t % 2].rearrange("p (h d) -> p h d", h=H), AX.X, ALU.add))
                c.sync()
                c(dve.tensor_scalar(ss[:, i], ss[:, i], 1e-12, None, ALU.add))
            for i, dst in enumerate((QR, KR)):
                dve.wait_ge(S("qk_pow"), i + 1)
                for t in range(T):
                    d = dst[:, t].rearrange("p (h d) -> p h d", h=H)
                    c(dve.tensor_tensor(d, d, bcast(ssr[:, i, t * H:(t + 1) * H], DH), ALU.mult))
            assert c.n == 32
            dve.wait_ge(S("aff_done"), 6)
            feats(2, QT, gq[:, 0:1])
            feats(3, KT)
            attention("a0", lambda k: 0, lambda t: CM[:, N - (t + 1) * R:N], True)
            feats(4, OT)
            dve.wait_ge(S("ld_small"), 48)
            router(0)
            mixture(0, 1, False)

            c = Chain(dve, S("msk_done"))
            for t in range(T):
                dve.wait_ge(S("msk_pe"), T)
                c(dve.tensor_scalar(MASK[:, t, 0:4 * R].rearrange("p (k n) -> p k n", k=4),
                                    bank[0:R, t, :].rearrange("p (k n) -> p k n", k=4)[:, :, 0:R], 0.0, NEG, ALU.is_equal, ALU.mult))
                c(dve.tensor_scalar(MASK[:, t, 4 * R:N], bank[0:R, 5 + t // 4, t % 4 * P:t % 4 * P + R], 0.0, NEG, ALU.is_equal, ALU.mult))
            ln(3)
            dve.memset(V[:, :, :, DH:DH + 1], 1.0).then_inc(S("v_ones"), 1)
            feats(5, XT)
            dve.wait_ge(S("msk_done"), 10)
            with dve.Fori(0, LAYERS) as layer:
                dve.wait_ge(S("ld_lvec"), layer * 16 + 16)
                dve.tensor_scalar(bq8[:], lvec[:, LV["bq"]:LV["bq"] + C], float(DH) ** -0.5, None, ALU.mult).then_inc(S("g_bq"), 1)
                for j, (m, lo, hi) in enumerate(GROUPS):
                    dve.wait_ge(S("g_k_full"), layer * 8 + j + 1)
                    dve.tensor_copy(KT[:, m, lo:hi], bank[:, j, 0:hi - lo]).then_inc(S("g_k_done"), 1)
                attention("g", lambda k: layer * k, lambda t: MASK[:, t], False)
                copy_feats(OT, S("g_tr_full"), S("g_tr_v"), layer * T)
                for name, full, bias, res, base in (("1", "g_wo_full", "bo", XT, 8), ("2", "g_w2_full", "b2", X1T, 8)):
                    for j, (m, lo, hi) in enumerate(GROUPS):
                        dve.wait_ge(S(full), layer * 8 + j + 1)
                        dve.scalar_tensor_tensor(out=HC[:, m, lo:hi], in0=bank[:, j, 0:hi - lo],
                                                 scalar=lvec[:, LV[bias] + m:LV[bias] + m + 1], in1=res[:, m, lo:hi],
                                                 op0=ALU.add, op1=ALU.add).then_inc(S(f"g_res{name}"), 1)
                    bn(HC, S(f"g_res{name}"), S(f"g_bn{name}_vec"), S(f"g_bn{name}_pow"),
                       lvec[:, LV["g" + name]:LV["g" + name] + C], lvec[:, LV["be" + name]:LV["be" + name] + C],
                       layer * 8, layer * 17, layer)

            c = Chain(dve, S("lf_vec"))
            dve.wait_ge(S("lf_full"), 5)
            stats_rows(c, lambda t: bank[0:R, t, :])
            dve.wait_ge(S("lf_pow"), 1)
            dve.wait_ge(S("ld_rvec1"), 16)
            for t in range(T):
                c(dve.tensor_scalar(XN[:, t], bank[0:R, t, :], mv[0:R, t, 0:1], rstd[0:R, t:t + 1], ALU.subtract, ALU.mult))
            c.sync()
            for t in range(T):
                c(dve.tensor_tensor(XN[:, t], XN[:, t], rvec[0:R, 0], ALU.mult))
            c.sync()
            for t in range(T):
                c(dve.tensor_tensor(XN[:, t], XN[:, t], rvec[0:R, 1], ALU.add))
            c.sync()
            for t in range(T):
                c(dve.tensor_tensor(X[:, t], X[:, t], XN[:, t], ALU.add))
            c.sync()

            ln(4)
            feats(6, XT)
            router(1)
            mixture(1, F1 // P, False)

            ln(5)
            for t in range(T):
                d = AT[:, t, t * R:(t + 1) * R]
                dve.tensor_tensor(d, d, ident[0:R, 0:R], ALU.add).then_inc(S("self_loops"), 1)
            feats(7, XT)
            c = Chain(dve, S("l2_vec"))
            dve.wait_ge(S("bs_full"), 5)
            c(dve.tensor_tensor(WGT[:], bank[0:R, 5, 0:T * 32].rearrange("p (t n) -> p t n", t=T),
                                rbias[0:R, RB["comb"]:RB["comb"] + 32].unsqueeze(1).broadcast_to([R, T, 32]), ALU.add))
            for t in range(T):
                dve.wait_ge(S("ag_full"), t + 1)
                c(dve.tensor_scalar(AG[:, t], bank[0:R, (6, 7, 0, 1, 2)[t], 0:BASES], dinvr[:, t:t + 1], None, ALU.mult))
            c.sync()
            dve.wait_ge(S("ld_rvec2"), 16)
            c(dve.tensor_tensor(rvec[0:R, 0], rvec[0:R, 0], rvec[0:R, 1], ALU.add))
            c.sync()
            for t in range(T):
                w = WGT[:, t].rearrange("p (h b) -> p h b", h=H)
                for b in range(NB):
                    c(dve.tensor_tensor(CV[:, b].rearrange("p (h f) -> p h f", h=H),
                                        AG[:, t, b * DH:(b + 1) * DH].unsqueeze(1).broadcast_to([R, H, DH]),
                                        w[:, :, b:b + 1].broadcast_to([R, H, DH]), ALU.mult))
                c.sync()
                c(dve.tensor_tensor(CV[:, 0], CV[:, 0], CV[:, 1], ALU.add))
                c(dve.tensor_tensor(CV[:, 2], CV[:, 2], CV[:, 3], ALU.add))
                c.sync()
                c(dve.tensor_tensor(CV[:, 0], CV[:, 0], CV[:, 2], ALU.add))
                c.sync()
                c(dve.tensor_tensor(CV[:, 0], CV[:, 0], rvec[0:R, 0], ALU.add))
                c.sync()
                dve.wait_ge(S("res_full"), t + 1)
                c(dve.tensor_tensor(XN[:, t], CV[:, 0], bank[0:R, 3 + t, :], ALU.add))
                c.sync()
            assert c.n == 52
            stats_rows(c, lambda t: XN[:, t])
            dve.wait_ge(S("l2_pow"), 1)
            for t in range(T):
                c(dve.tensor_scalar(XN[:, t], XN[:, t], mv[0:R, t, 0:1], rstd[0:R, t:t + 1], ALU.subtract, ALU.mult))
            c.sync()
            for t in range(T):
                c(dve.tensor_tensor(XN[:, t], XN[:, t], rvec[0:R, 2], ALU.mult))
            c.sync()
            for t in range(T):
                c(dve.tensor_tensor(XN[:, t], XN[:, t], rvec[0:R, 3], ALU.add))
            c.sync()
            for t in range(T):
                c(dve.scalar_tensor_tensor(out=X[:, t], in0=XN[:, t], scalar=0.0, in1=X[:, t], op0=ALU.max, op1=ALU.add))
            c.sync()

            ln(6)
            feats(8, XT)
            router(2)
            mixture(2, 1, False)

            ln(7)
            feats(9, XT)
            c = Chain(dve, S("h3_scaled"))
            for j, (m, lo, hi) in enumerate(GROUPS):
                dve.wait_ge(S("h3_full"), j + 1)
                c(dve.tensor_tensor(HB[:, m, lo:hi], bank[:, j, 0:hi - lo], dinvb[:, lo:hi], ALU.mult))
                c.sync()
                dve.tensor_scalar(HB[:, m, lo:hi], HB[:, m, lo:hi], fvec[:, FV["l3_b"] + m:FV["l3_b"] + m + 1], None,
                                  ALU.add).then_inc(S("h3_done"), 1)
            bn(HB, S("h3_done"), S("bn3_vec"), S("bn3_pow"), fvec[:, FV["l3_g"]:FV["l3_g"] + C], fvec[:, FV["l3_be"]:FV["l3_be"] + C])
            add_rows(S("rows3_full"), S("rows3_vec"))

            ln(8)
            feats(10, XT)
            router(3)
            mixture(3, F3 // P, True)


def _by_feature(v):
    return np.asarray(v).reshape(-1, P).T


def _rhs(w):
    w = np.asarray(w)
    return w.reshape(-1, P, w.shape[1]).transpose(1, 0, 2)


def kernel(**inputs):
    import concourse.bacc as bacc
    from concourse.bass_utils import run_bass_kernel_spmd

    g = {k: np.asarray(v) for k, v in inputs.items()}
    cat = np.concatenate
    L = {}
    L["x"] = g["x"].reshape(T, R, D).transpose(1, 0, 2)
    L["edges"] = cat([g["src"].reshape(ET, R).T, g["dst"].reshape(ET, R).T], 1)
    f = _by_feature
    L["fvec"] = cat([f(g["L0_gnn_b_l"]), f(g["L0_gnn_gamma"]), f(g["L0_gnn_beta"]), f(g["L0_ffn_ln_g"]), f(g["L0_ffn_ln_b"]),
                     f(cat([g["L0_ffn_qn_g"]] * 2)), f(cat([g["L0_ffn_kn_g"]] * 2)), f(g["L0_ffn_b1"]), f(g["L1_ffn_b1"]),
                     f(g["L2_ffn_b1"]), f(g["L3_gnn_b"]), f(g["L3_gnn_gamma"]), f(g["L3_gnn_beta"])], 1)
    L["lvec"] = np.stack([cat([f(g["L1_gnn_" + n][l]) for n in ("bq", "bo", "b1", "b2", "g1", "beta1", "g2", "beta2")], 1)
                          for l in range(LAYERS)])
    L["gw"] = _rhs(cat([g["L0_ffn_gate_W"], g["L1_ffn_gate_w"], g["L2_ffn_Wg"], g["L3_ffn_router_w"].T, g["L2_gnn_W_comb"]], 1))
    L["rbias"] = cat([g["L0_ffn_gate_b"], g["L1_ffn_gate_b"], g["L2_ffn_bg"], g["L2_gnn_b_comb"]])[None]
    L["rvec1"] = np.stack([g["L1_gnn_ln_g"], g["L1_gnn_ln_b"]])[None]
    L["rvec2"] = np.stack([g["L2_gnn_conv_bias"], g["L2_gnn_b_res"], g["L2_gnn_gamma"], g["L2_gnn_beta"]])[None]
    L["b2"] = np.stack([g["L0_ffn_b2"], g["L1_ffn_b2"], g["L2_ffn_b2"], np.zeros((E, D), np.float32)])
    L["w_l0"] = cat([_rhs(g["L0_gnn_W_l"].T), _rhs(g["L0_gnn_W_r"].T)], 1).reshape(P, -1)
    L["w_a0"] = np.stack([_rhs(g["L0_ffn_" + n]).reshape(P, -1) for n in ("Wq", "Wk", "Wv", "Wo")], 1)
    L["w_g"] = np.stack([np.stack([_rhs(g["L1_gnn_" + n][l].T).reshape(P, -1) for n in ("Wq", "Wk", "Wv", "Wo")], 1) for l in range(LAYERS)])
    L["w_gf"] = np.stack([cat([_rhs(g["L1_gnn_W1"][l].T).reshape(P, -1), g["L1_gnn_W2"][l].T], 1) for l in range(LAYERS)])
    L["w_l2"] = cat([_rhs(g["L2_gnn_W_bases"]).reshape(P, -1), _rhs(g["L2_gnn_W_res"]).reshape(P, -1)], 1)
    L["w_l3"] = _rhs(g["L3_gnn_W"].T).reshape(P, -1)

    def chunks(ins, w2):
        J = w2.shape[1] // P
        first = [w.reshape(E, C, P, J, P).transpose(0, 3, 2, 1, 4).reshape(E, J, P, C * P) for w in ins]
        return cat(first + [w2.reshape(E, J, P, D)], 3)

    L["w_m0"] = chunks([g["L0_ffn_W1"]], g["L0_ffn_W2"])[:, 0]
    L["w_m1"] = chunks([g["L1_ffn_w1"]], g["L1_ffn_w2"])
    L["w_m2"] = chunks([g["L2_ffn_W1"]], g["L2_ffn_W2"])[:, 0]
    L["w_m3"] = chunks([g["L3_ffn_w1"].transpose(0, 2, 1), g["L3_ffn_wgate"].transpose(0, 2, 1)], g["L3_ffn_w2"].transpose(0, 2, 1))

    nc = bacc.Bacc("TRN2", target_bir_lowering=False, num_devices=1)
    arrays, aps = {}, {}
    for name, a in L.items():
        a = np.ascontiguousarray(a)
        arrays["in_" + name] = a
        aps[name] = nc.dram_tensor("in_" + name, a.shape, mybir.dt.from_np(a.dtype), kind="ExternalInput").ap()
    out = nc.dram_tensor("out_x", (R, T, D), F32, kind="ExternalOutput").ap()
    graph_network(nc, aps, out)
    r = run_bass_kernel_spmd(nc, [arrays], core_ids=[0])
    return np.asarray(r.results[0]["out_x"]).transpose(1, 0, 2).reshape(N, D)
```

```python
from contextlib import ExitStack

import numpy as np

import concourse.bass as bass
from concourse import mybir

ALU = mybir.AluOpType
ACT = mybir.ActivationFunctionType
AX = mybir.AxisListType
F32 = mybir.dt.float32
BF16 = mybir.dt.bfloat16
F16 = mybir.dt.float16
I32 = mybir.dt.int32
U32 = mybir.dt.uint32

P = 128
N = 625
R = 125
T = N // R
D = 512
C = D // P
EDGES = 10000
ET = EDGES // R
H = 8
DH = D // H
E = 8
LAYERS = 2
F1 = 1024
F3 = 1536
BASES = 256
NB = 4
BLOCKS = (2 * N - E) // P + E
PER = -(-N // P)
HALVES = ((0, 3 * R), (3 * R, N))
NEG = -1e30
EPS = 1e-5

FV = {}
_at = 0
for _n, _w in (("l0_b", 4), ("l0_g", 4), ("l0_be", 4), ("ln_g", 4), ("ln_b", 4), ("qn", 1), ("kn", 1),
               ("m0_b1", 8), ("m2_b1", 8), ("l3_b", 4), ("l3_g", 4), ("l3_be", 4)):
    FV[_n] = _at
    _at += _w
FVW = _at
LV = {}
_at = 0
for _n, _w in (("bq", 4), ("bo", 4), ("b1", 1), ("b2", 4), ("g1", 4), ("be1", 4), ("g2", 4), ("be2", 4)):
    LV[_n] = _at
    _at += _w
LVW = _at
GW = {0: 0, 1: 8, 2: 16, 3: 24, "comb": 32}
GWW = 64
RB = {0: 0, 1: 8, 2: 16, "comb": 24}
RBW = 56


CH = {1: F1 // D, 3: F3 // D}
PARTS = {1: (("a", 0), ("a", 1), ("y", 0), ("y", 1)),
         3: (("a", 0), ("g", 0), ("a", 1), ("g", 1), ("y", 0), ("a", 2), ("g", 2), ("y", 1), ("y", 2))}


class Chain:

    def __init__(self, eng, sem, base=0):
        self.eng, self.sem, self.n = eng, sem, base

    def __call__(self, ins):
        ins.then_inc(self.sem, 1)
        self.n = self.n + 1

    def sync(self):
        self.eng.wait_ge(self.sem, self.n)


def graph_network(nc, A, out):
    ctx = ExitStack()
    with ctx:
        sems = {}

        def S(name):
            if name not in sems:
                sems[name] = ctx.enter_context(nc.semaphore(name))
            return sems[name]

        def sb(name, shape, dt=F32):
            return ctx.enter_context(nc.sbuf_tensor("sb_" + name, shape, dt))

        bank = ctx.enter_context(nc.psum_tensor("bank", [P, 8, 512], F32))

        X = sb("X", [R, T, D])
        XN = sb("XN", [R, T, D])
        XT = sb("XT", [P, C, N])
        AT = sb("AT", [R, T, N])
        ident = sb("ident", [P, P])
        ones = sb("ones", [P, P])
        SEL = sb("SEL", [E, E, P])
        TRI = sb("TRI", [R, R])
        LT = sb("LT", [R, E, E])
        THR = sb("THR", [R, E, PER])
        iota_b = sb("iota_b", [1, BLOCKS])
        nop = sb("nop", [1, 48])
        iota8 = sb("iota8", [R, E])
        fvec = sb("fvec", [P, FVW])
        lvec = sb("lvec", [P, LVW])
        rvec = sb("rvec", [P, 4, D])
        rbias = sb("rbias", [P, RBW])
        gw = sb("gw", [P, C, GWW])
        b2 = sb("b2", [E, D])
        dinvb = sb("dinvb", [P, N])
        dinvr = sb("dinvr", [R, T])
        half8 = sb("half8", [P, 1])
        st = sb("st", [P, 8, 6])
        mv = sb("mv", [P, T, 2])
        ve = sb("ve", [P, T])
        rstd = sb("rstd", [P, T])
        bsc = sb("bsc", [P, C])
        bsh = sb("bsh", [P, C])
        bms = sb("bms", [P, C])
        degr = sb("degr", [R, T])
        gq = sb("gq", [P, 1])
        bq8 = sb("bq8", [P, C])
        ss = sb("ss", [R, 2, T * H])
        ssr = sb("ssr", [R, 2, T * H])
        nmx = sb("nmx", [R, T * H])
        rden = sb("rden", [R, H])
        LG = sb("LG", [R, T, E])
        EX = sb("EX", [R, T, E])
        PR = sb("PR", [R, T, E])
        COMB = sb("COMB", [R, T, E])
        EQ = sb("EQ", [R, 2, T, E])
        MK = sb("MK", [R, T, E])
        nblk = sb("nblk", [R, 3, E])
        slot = sb("slot", [R, T, E])
        sl = sb("sl", [R, 2, T])
        slu = sb("slu", [R, 2, T], U32)
        wk = sb("wk", [R, 2, T])
        eb = sb("eb", [1, 2, BLOCKS])
        ebi = sb("ebi", [1, 2, BLOCKS], I32)
        red = sb("red", [R, 3, T])
        m8 = sb("m8", [R, T, 8])
        i8 = sb("i8", [R, T, 8], U32)
        if8 = sb("if8", [R, T, 8])
        m1b = sb("m1b", [P, F1 // P])
        WGT = sb("WGT", [R, T, H * NB])

        W = sb("W", [P, 17408])
        rA = sb("rA", [P, T * D])
        rB = sb("rB", [P, T * D])
        rC = sb("rC", [P, C * N])
        rDE = sb("rDE", [P, C * N + T * H * (DH + 1)])
        rF = sb("rF", [P, 4 * N])
        rG = sb("rG", [P, T * N])

        def rows(r):
            return r[0:R, 0:T * D].rearrange("p (t d) -> p t d", t=T)

        def feats(r, at=0):
            return r[:, at:at + C * N].rearrange("p (c n) -> p c n", c=C)

        QR, KR, OR = rows(rA), rows(rB), rows(rA)
        QT, KT = feats(rC), feats(rDE)
        V = rDE[0:R, C * N:].rearrange("p (t h d) -> p t h d", t=T, h=H)
        OT = feats(rB)
        YT = feats(rC)
        MT, HB = feats(rA), feats(rB)
        HC, X1T = feats(rC), feats(rDE)
        SM = rF[0:R, 0:2 * N].rearrange("p (b n) -> p b n", b=2)
        PT = rF[0:R, 2 * N:4 * N].rearrange("p (b t n) -> p b t n", b=2, t=T)
        RT = rF[:, 0:N]
        hs = rF[:, 0:2 * 375].rearrange("p (b n) -> p b n", b=2)
        hg = rF[:, 750:2 * 750].rearrange("p (b n) -> p b n", b=2)
        combT = rF[0:E, 1500:1500 + N]
        CB = rDE[:, 0:E * N].rearrange("p (e n) -> p e n", e=E)
        MASK = rG[0:R, :].rearrange("p (t n) -> p t n", t=T)
        CM = rG[0:R, 0:N]
        OH = rA[0:R, 0:4 * 640].bitcast(BF16).rearrange("p (s k n) -> p s k n", s=4, k=2)
        iota16 = rB[0:R, 0:320].bitcast(F16)
        idxi = rB[0:R, 320:320 + 2 * ET].bitcast(I32)
        idxf = rB[0:R, 480:480 + 2 * ET]
        diag = rB[0:R, 640:640 + N].rearrange("p (t n) -> p t n", t=T)
        cmx = rB[:, 1280:1280 + N]
        rcntb = rG[:, 700:700 + N]
        SQ = rF[0:R, 0:2 * D].rearrange("p (b n) -> p b n", b=2)
        BS = rA[0:R, 0:T * BASES].rearrange("p (t n) -> p t n", t=T)
        XW = rows(rA)
        AG = rB[0:R, 0:T * BASES].rearrange("p (t n) -> p t n", t=T)
        CV = rC[0:R, 0:4 * D].rearrange("p (b n) -> p b n", b=4)

        def mat(at, k, n):
            return W[:, at:at + k * n].rearrange("p (c n) -> p c n", c=k)

        Wl, Wr = mat(0, C, D), mat(2048, C, D)
        Wq, Wk, Wv, Wo = (mat(4096 + 2048 * i, C, D) for i in range(4))
        Wf1, Wf2 = mat(16384, C, P), W[:, 16896:17408]
        Wb, Wres = mat(0, C, BASES), mat(1024, C, D)
        W3 = mat(3072, C, D)
        M0 = [12288 + 1024 * e if e < 4 else 1024 * (e - 4) for e in range(E)]
        M2 = [8192 + 1024 * e for e in range(E)]
        XS = nc.dram_tensor("slots_in", (P * (BLOCKS + 1), D), F32).ap()
        YS = nc.dram_tensor("slots_out", (P * BLOCKS, D), F32).ap()
        fill = rC[:, 0:D]
        xblk = rC[:, 0:D]
        xbT = rC[:, D:2 * D].rearrange("p (c n) -> p c n", c=C)
        yblk = rC[:, 2 * D:3 * D]
        act_s = rF[:, 0:2 * D].rearrange("p (b n) -> p b n", b=2)
        hrow = rF[:, 2 * D:4 * D].rearrange("p (b n) -> p b n", b=2)
        hT = rG[:, 0:2 * D].rearrange("p (b c n) -> p b c n", b=2, c=4)
        G = (rows(rA), rows(rB))
        gtmp = rDE[0:R, 0:E * E]
        btmp = rDE[0:1, 256:256 + BLOCKS * E].rearrange("p (b e) -> p b e", e=E)
        etmp = rDE[0:R, 512:512 + 2 * T * E]

        def part(i):
            return W[:, 2048 * i:2048 * (i + 1)] if i < 8 else rDE[:, 2560:2560 + 2048]

        def bcast(ap, k):
            return ap.unsqueeze(2).broadcast_to([ap.shape[0], ap.shape[1], k])

        GROUPS = [(m, lo, hi) for m in range(C) for lo, hi in HALVES]
        ATT = 5 * 8

        CONSTS = 16
        ROUTER_OPS = (6, 24, 21, 24)
        SLOT_OPS = 16
        ROUTED = [sum(ROUTER_OPS[:r]) for r in range(4)]
        UNITS = 2 * E
        UB = {0: 0, 2: UNITS}
        PLACE = {r: {p: i + (4 if r == 1 else 0) for i, p in enumerate(PARTS[r])} for r in PARTS}

        block = ctx.enter_context(nc.Block())

        def with_layers(sp):
            names = ("g_q_full", "g_k_full", "g_v_full", "g_wo_full")
            counts = (8, 8, 5, 8)

            def load(layer, after_first):
                if after_first:
                    sp.wait_ge(S("g_x2"), layer * 4)
                sp.dma_start(lvec[:], A["lvec"][bass.ds(layer, 1)].rearrange("l p n -> (l p) n")).then_inc(S("ld_lvec"), 16)
                for i in range(4):
                    if after_first:
                        sp.wait_ge(S(names[i]), layer * counts[i])
                    sp.dma_start(W[:, 4096 + 2048 * i:6144 + 2048 * i],
                                 A["w_g"][bass.ds(layer, 1), :, i].rearrange("l p n -> (l p) n")).then_inc(S(f"ld_g{i}"), 16)
                if after_first:
                    sp.wait_ge(S("g_w2_full"), layer * 8)
                sp.dma_start(W[:, 16384:17408], A["w_gf"][bass.ds(layer, 1)].rearrange("l p n -> (l p) n")).then_inc(S("ld_gf"), 16)

            load(0, False)
            with sp.Fori(1, LAYERS) as layer:
                load(layer, True)

        def blocks(sp, r, src):
            n = CH[r]
            sp.wait_ge(S(f"sl{r}_vec"), SLOT_OPS)
            sp.wait_ge(S(f"sc{r}"), 16 * 2 * T)
            sp.dma_start(xblk, XS[0:P]).then_inc(S(f"ld_x{r}"), 16)
            e = sp.value_load(ebi[0:1, 0, 0:1], min_val=0, max_val=E - 1)
            if r == 1:
                sp.dma_start(m1b[:], A["m1_b1"][e]).then_inc(S("ld_m1b"), 16)
            for i, p in enumerate(PARTS[r]):
                sp.dma_start(part(PLACE[r][p]), src[e, i]).then_inc(S(f"ld{r}_{p[0]}{p[1]}"), 16)
            sp.wait_ge(S(f"b{r}_xt"), 1)
            sp.dma_start(xblk, XS[P:2 * P]).then_inc(S(f"ld_x{r}"), 16)
            with sp.Fori(1, BLOCKS) as b:
                e = sp.value_load(ebi[0:1, 0, bass.ds(b, 1)], min_val=0, max_val=E - 1)
                new = sp.value_load(ebi[0:1, 1, bass.ds(b, 1)], min_val=0, max_val=1)
                for i, p in enumerate(PARTS[r]):
                    if r == 1 and p == ("y", 1):
                        sp.wait_ge(S("b1_ht"), b * (4 * n))
                        sp.dma_start(m1b[:], A["m1_b1"][e]).then_inc(S("ld_m1b"), 16)
                    if i == len(PARTS[r]) - 1:
                        sp.wait_ge(S(f"b{r}_xt"), b + 1)
                        sp.dma_start(xblk, XS[bass.ds(b * P + P, P)]).then_inc(S(f"ld_x{r}"), 16)
                    sp.wait_ge(S(f"b{r}_{p[0]}"), b * n + (p[1] + 1 - n))
                    sp.dma_start(part(PLACE[r][p]), src[e, i], cond=new > 0).then_inc(S(f"ld{r}_{p[0]}{p[1]}"), 16)

        @block.sync
        def _(sp):
            sp.dma_start(idxi, A["edges"]).then_inc(S("ld_idx"), 16)
            sp.wait_ge(S("fill"), 1)
            sp.dma_start(XS.rearrange("(b p) d -> p b d", p=P), fill.unsqueeze(1).broadcast_to([P, BLOCKS + 1, D])).then_inc(S("filled"), 16)
            sp.dma_start(X[:], A["x"]).then_inc(S("ld_x"), 16)
            sp.dma_start(fvec[:], A["fvec"]).then_inc(S("ld_small"), 16)
            sp.dma_start(W[:, 0:4096], A["w_l0"]).then_inc(S("ld_l0"), 16)
            sp.dma_start(gw[:], A["gw"]).then_inc(S("ld_small"), 16)
            sp.dma_start(rbias[:], A["rbias"].to_broadcast([P, RBW])).then_inc(S("ld_small"), 16)
            sp.dma_start(b2[:], A["b2"][0]).then_inc(S("ld_b2"), 16)
            for i in range(4):
                sp.dma_start(W[:, 4096 + 2048 * i:6144 + 2048 * i], A["w_a0"][:, i]).then_inc(S(f"ld_a0_{i}"), 16)
            sp.dma_start(W[:, 12288:16384].rearrange("p (e n) -> p e n", e=4),
                         A["w_m0"][0:4].rearrange("e p n -> p e n")).then_inc(S("ld_m0a"), 16)
            sp.wait_ge(S("h_full"), 8)
            sp.dma_start(W[:, 0:4096].rearrange("p (e n) -> p e n", e=4),
                         A["w_m0"][4:8].rearrange("e p n -> p e n")).then_inc(S("ld_m0b"), 16)
            sp.wait_ge(S("kvq_full"), 15)
            sp.wait_ge(S("wo0_full"), 8)
            sp.dma_start(rvec[:, 0:2], A["rvec1"].rearrange("a k d -> a k d").to_broadcast([P, 2, D])).then_inc(S("ld_rvec1"), 16)
            sp.wait_ge(S("mo_out"), 5)
            sp.dma_start(b2[:], A["b2"][1]).then_inc(S("ld_b2"), 16)
            with_layers(sp)
            blocks(sp, 1, A["w_m1"])
            sp.dma_start(rvec[:], A["rvec2"].to_broadcast([P, 4, D])).then_inc(S("ld_rvec2"), 16)
            sp.dma_start(W[:, 0:3072], A["w_l2"]).then_inc(S("ld_l2"), 16)
            sp.dma_start(W[:, 3072:5120], A["w_l3"]).then_inc(S("ld_l3"), 16)
            sp.wait_ge(S("b1_y"), BLOCKS * CH[1])
            sp.dma_start(W[:, 8192:16384].rearrange("p (e n) -> p e n", e=8),
                         A["w_m2"].rearrange("e p n -> p e n")).then_inc(S("ld_m2"), 16)
            sp.dma_start(b2[:], A["b2"][2]).then_inc(S("ld_b2"), 16)
            blocks(sp, 3, A["w_m3"])
            for t in range(T):
                sp.wait_ge(S("mo_out"), 3 * T + t + 1)
                sp.dma_start(out[:, t], X[:, t]).then_inc(S("stored"), 16)
            sp.wait_ge(S("stored"), 16 * T)

        @block.gpsimd
        def _(pool):
            pool.memset(fill, 0.0).then_inc(S("fill"), 1)
            c = Chain(pool, S("consts"))
            c(pool.iota(iota16[:, 0:N], [[1, N]], base=0, channel_multiplier=0, allow_small_or_imprecise_dtypes=True))
            c(pool.memset(ident[:], 0.0))
            c(pool.memset(ones[:], 1.0))
            c(pool.memset(TRI[:], 1.0))
            c(pool.memset(LT[:], 1.0))
            c(pool.iota(THR[:], [[0, E], [P, PER]], base=0, channel_multiplier=0, allow_small_or_imprecise_dtypes=True))
            c(pool.iota(iota_b[:], [[1, BLOCKS]], base=0, channel_multiplier=0, allow_small_or_imprecise_dtypes=True))
            c(pool.memset(half8[:], -0.5))
            c(pool.memset(SEL[:], 0.0))
            c(pool.memset(CM, 0.0))
            c(pool.iota(iota8[:], [[1, E]], base=0, channel_multiplier=0, allow_small_or_imprecise_dtypes=True))
            c.sync()
            c(pool.affine_select(out=ident[:], in_=ident[:], compare_op=ALU.not_equal, fill=1.0,
                                 base=0, pattern=[[-1, P]], channel_multiplier=1))
            c(pool.affine_select(out=SEL[:], in_=SEL[:], compare_op=ALU.not_equal, fill=1.0,
                                 base=0, pattern=[[-1, E], [0, P]], channel_multiplier=1))
            c(pool.affine_select(out=CM[:, N - R:N], in_=CM[:, N - R:N], compare_op=ALU.is_ge, fill=NEG,
                                 base=0, pattern=[[-1, R]], channel_multiplier=1))
            c(pool.affine_select(out=TRI[:], in_=TRI[:], compare_op=ALU.is_gt, fill=0.0,
                                 base=0, pattern=[[1, R]], channel_multiplier=-1))
            c(pool.affine_select(out=LT[:], in_=LT[:], compare_op=ALU.is_gt, fill=0.0,
                                 base=0, pattern=[[1, E], [-1, E]], channel_multiplier=0))
            assert c.n == CONSTS

            def power(dst, src, k, ready, count, done):
                pool.wait_ge(ready, count)
                pool.tensor_tensor(dst, src, half8[0:src.shape[0], :].broadcast_to([src.shape[0], k]), ALU.pow).then_inc(done, 1)

            def ln(k):
                power(rstd[0:R, :], ve[0:R, :], T, S("ln_vec"), 16 * k + 11, S("ln_pow"))

            def scatter(r):
                pool.wait_ge(S("ln_vec"), 16 * (4 if r == 1 else 8) + 16)
                pool.wait_ge(S(f"sl{r}_vec"), 8)
                pool.wait_ge(S("filled"), 16)
                for k in range(2):
                    for t in range(T):
                        pool.indirect_dma_start(out=XS, out_offset=bass.IndirectOffsetOnAxis(ap=slu[:, k, t:t + 1], axis=0),
                                                in_=XN[:, t], in_offset=None).then_inc(S(f"sc{r}"), 16)
                pool.wait_ge(S(f"st{r}"), 16 * BLOCKS)
                for k in range(2):
                    for t in range(T):
                        pool.indirect_dma_start(out=G[k][:, t], out_offset=None, in_=YS,
                                                in_offset=bass.IndirectOffsetOnAxis(ap=slu[:, k, t:t + 1], axis=0)).then_inc(S(f"gathered{k}"), 16)

            ln(0)
            power(dinvr[:], degr[:], T, S("deg_vec"), 5, S("deg_pow"))
            power(rstd[:, 0:C], ve[:, 0:C], C, S("bn_vec"), 13, S("bn_pow"))
            ln(1)
            ln(2)
            for i in range(2):
                power(ssr[:, i], ss[:, i], T * H, S("qk_vec"), 11 * (i + 1), S("qk_pow"))
            ln(3)
            with pool.Fori(0, LAYERS) as layer:
                for b in (1, 2):
                    power(rstd[:, 0:C], ve[:, 0:C], C, S(f"g_bn{b}_vec"), layer * 17 + 14, S(f"g_bn{b}_pow"))
            power(rstd[0:R, :], ve[0:R, :], T, S("lf_vec"), 11, S("lf_pow"))
            ln(4)
            scatter(1)
            ln(5)
            power(rstd[0:R, :], ve[0:R, :], T, S("l2_vec"), 52 + 11, S("l2_pow"))
            ln(6)
            ln(7)
            power(rstd[:, 0:C], ve[:, 0:C], C, S("bn_vec"), 29, S("bn_pow"))
            ln(8)
            scatter(3)

        @block.tensor
        def _(pe):
            def to_feats(src, full, base=0):
                for t in range(T):
                    for c in range(C):
                        mm = pe.transpose(bank[:, t, c * R:(c + 1) * R], src[:, t, c * P:(c + 1) * P], ident[0:R, 0:R])
                    mm.then_inc(full, 1)

            def feats_ready(k):
                pe.wait_ge(S("tr_v"), 3 * (k + 1))
                pe.wait_ge(S("tr_a"), 2 * (k + 1))

            def to_rows(src, full):
                for t in range(T):
                    for c in range(C):
                        mm = pe.transpose(bank[0:R, t, c * P:(c + 1) * P], src[:, c, t * R:(t + 1) * R], ident[:])
                    mm.then_inc(full, 1)

            def project(pairs, full, before=None, base=0):
                for j, (m, lo, hi) in enumerate(GROUPS):
                    if before is not None:
                        pe.wait_ge(before, base + j + 1)
                    steps = [(w, x, c) for w, x in pairs for c in range(x.shape[1])]
                    for n, (w, x, c) in enumerate(steps):
                        mm = pe.matmul(bank[:, j, 0:hi - lo], w[:, c, m * P:(m + 1) * P], x[:, c, lo:hi],
                                       start=(n == 0), stop=(n == len(steps) - 1))
                    mm.then_inc(full, 1)

            def row_group(b, x, t, w, full, cols=D):
                for c in range(C):
                    mm = pe.matmul(bank[0:R, b, 0:cols], x[:, c, t * R:(t + 1) * R], w[:, c, 0:cols],
                                   start=(c == 0), stop=(c == C - 1))
                if full is not None:
                    mm.then_inc(full, 1)

            def attention(base, causal):
                for s in range(ATT + 2):
                    if s < ATT:
                        t, h = divmod(s, H)
                        kn = (t + 1) * R if causal else N
                        if s >= 2:
                            pe.wait_ge(S("at_mask"), base(ATT) + s - 1)
                        hp = slice((h % 2) * DH, (h % 2) * DH + DH)
                        for lo, hi in ((0, min(kn, 512)), (512, kn)):
                            if lo < hi:
                                mm = pe.matmul(bank[0:R, 2 * (s % 2) + lo // 512, 0:hi - lo],
                                               QT[hp, h // 2, t * R:(t + 1) * R], KT[hp, h // 2, lo:hi], start=True, stop=True)
                        mm.then_inc(S("at_s"), 1)
                    if 1 <= s <= ATT:
                        u = s - 1
                        t, h = divmod(u, H)
                        pe.wait_ge(S("at_exp"), base(ATT) + u + 1)
                        if u >= 1:
                            pe.wait_ge(S("at_pt"), base(ATT) + u)
                        for kb in range(t + 1 if causal else T):
                            mm = pe.transpose(bank[0:R, 4 + kb // 4, (kb % 4) * P:(kb % 4) * P + R],
                                              SM[:, u % 2, kb * R:(kb + 1) * R], ident[0:R, 0:R])
                        mm.then_inc(S("at_tr"), 1)
                    if s >= 2:
                        u = s - 2
                        t, h = divmod(u, H)
                        pe.wait_ge(S("at_pt"), base(ATT) + u + 1)
                        if h == 0 and t >= 1:
                            pe.wait_ge(S("at_norm"), base(3 * T) + 3 * t)
                        last = t if causal else T - 1
                        for kb in range(last + 1):
                            mm = pe.matmul(bank[0:R, 6 + h // 4, (h % 4) * (DH + 1):(h % 4 + 1) * (DH + 1)],
                                           PT[:, u % 2, kb, :], V[:, kb, h, :], start=(kb == 0), stop=(kb == last))
                        mm.then_inc(S("at_av"), 1)

            def router(r, xt):
                for t in range(T):
                    for c in range(C):
                        mm = pe.matmul(bank[0:R, 0, t * E:(t + 1) * E], xt[:, c, t * R:(t + 1) * R],
                                       gw[:, c, GW[r]:GW[r] + E], start=(c == 0), stop=(c == C - 1))
                mm.then_inc(S("rt_pe"), 1)
                if r in (1, 3):
                    return
                pe.wait_ge(S("rt_vec"), ROUTED[r] + ROUTER_OPS[r])
                for t in range(T):
                    mm = pe.transpose(bank[0:E, 1 + t // 4, (t % 4) * R:(t % 4 + 1) * R], COMB[:, t], ident[0:R, 0:R])
                mm.then_inc(S("rt_pe"), 1)
                pe.wait_ge(S("rt_act"), 3 * r + 3)
                for e in range(E):
                    for i, (lo, hi) in enumerate(HALVES):
                        g = 2 * e + i
                        if g >= 5:
                            pe.wait_ge(S("rt_cb"), 2 * E * (r // 2) + g - 4)
                        pe.matmul(bank[:, 3 + g % 5, 0:hi - lo], SEL[:, e], combT[:, lo:hi],
                                  start=True, stop=True).then_inc(S("rt_spread"), 1)

            def mixture(r, xt, slots):
                pe.wait_ge(S("rt_cb"), 2 * E * (r // 2 + 1))
                pe.wait_ge(S("ld_b2"), 16 * (r + 1))
                for t in range(T):
                    pe.matmul(bank[0:R, t, :], combT[:, t * R:(t + 1) * R], b2[:], start=True, stop=False, skip_group_check=True)

                def first(u):
                    e, i = divmod(u, 2)
                    lo, hi = HALVES[i]
                    w = W[:, slots[e]:slots[e] + D].rearrange("p (c n) -> p c n", c=C)
                    if i == 0:
                        pe.wait_ge(S("ld_m2" if r == 2 else "ld_m0a" if e < 4 else "ld_m0b"), 16)
                    for c in range(C):
                        mm = pe.matmul(bank[:, 5 + u % 3, 0:hi - lo], w[:, c], xt[:, c, lo:hi], start=(c == 0), stop=(c == C - 1))
                    mm.then_inc(S("mo_h"), 1)

                def second(u):
                    e, i = divmod(u, 2)
                    at = slots[e] + D
                    pe.wait_ge(S("mo_hs"), UB[r] + u + 1)
                    for t in range(3 * i, 3 + 2 * i):
                        k = t - 3 * i
                        mm = pe.matmul(bank[0:R, t, :], hs[:, u % 2, k * R:(k + 1) * R], W[:, at:at + D],
                                       start=False, stop=(e == E - 1), skip_group_check=True)
                    mm.then_inc(S("mo_used"), 1)

                for u in range(UNITS + 1):
                    if u < UNITS:
                        first(u)
                    if u >= 1:
                        second(u - 1)

            def slots(r):
                pe.wait_ge(S("rt_vec"), ROUTED[r] + ROUTER_OPS[r])
                for t in range(T):
                    for k in range(t + 1):
                        pe.matmul(bank[0:R, 0, 64 + t * E:64 + (t + 1) * E], (ones[0:R, 0:R] if k < t else TRI[:]), MK[:, k],
                                  start=(k == 0), stop=(k == t))
                for k in range(T):
                    mm = pe.matmul(bank[0:R, 0, 128:128 + E], ones[0:R, 0:R], MK[:, k], start=(k == 0), stop=(k == T - 1))
                mm.then_inc(S(f"sl{r}_pe"), 1)

            def second_biases():
                for t in range(T):
                    mm = pe.transpose(bank[0:E, 1 + t // 4, (t % 4) * R:(t % 4 + 1) * R], COMB[:, t], ident[0:R, 0:R])
                mm.then_inc(S("rt_pe"), 1)
                pe.wait_ge(S("rt_act"), 6)
                pe.wait_ge(S("ld_b2"), 32)
                for t in range(T):
                    pe.matmul(bank[0:R, 3 + t, :], combT[:, t * R:(t + 1) * R], b2[:], start=True, stop=True).then_inc(S("b2_full"), 1)

            def block_parts(r):
                n = CH[r]
                freed = S("b1_h") if r == 1 else S("b3_s")

                def product(name, bank0, c, j, b, taken):
                    pe.wait_ge(S(f"ld{r}_{name}{j}"), b * 16 + 16)
                    if j == 0:
                        pe.wait_ge(S(f"b{r}_xbt"), b + 1)
                    before = c if j == 0 and n % 2 else c - 1
                    if not (isinstance(before, int) and before <= 0):
                        pe.wait_ge(taken, before)
                    w = part(PLACE[r][(name, j)]).rearrange("p (c n) -> p c n", c=C)
                    for k in range(C):
                        mm = pe.matmul(bank[:, bank0 + j % 2, :], xbT[:, k], w[:, k], start=(k == 0), stop=(k == C - 1))
                    mm.then_inc(S(f"b{r}_{name}"), 1)

                def first(b, j):
                    c = b * n + j
                    product("a", 0, c, j, b, freed)
                    if r == 3:
                        product("g", 2, c, j, b, S("b3_h"))

                def second(b, j):
                    c = b * n + j
                    k = 4 if r == 1 else 1
                    pe.wait_ge(S(f"b{r}_h"), c + 1)
                    for i in range(4):
                        mm = pe.transpose(bank[:, 4 + j % 2, i * P:(i + 1) * P], hrow[:, j % 2, i * P:(i + 1) * P], ident[:])
                    mm.then_inc(S(f"b{r}_tr"), 1)
                    pe.wait_ge(S(f"ld{r}_y{j}"), b * 16 + 16)
                    if j == 0 and not isinstance(b, int):
                        pe.wait_ge(S(f"st_y{r}"), b)
                    pe.wait_ge(S(f"b{r}_ht"), (c + 1) * k)
                    w = part(PLACE[r][("y", j)]).rearrange("p (c n) -> p c n", c=4)
                    for i in range(4):
                        mm = pe.matmul(bank[:, 7, :], hT[:, j % 2, i], w[:, i], start=(j == 0 and i == 0), stop=(j == n - 1 and i == 3))
                    mm.then_inc(S(f"b{r}_y"), 1)

                def nodes(b):
                    pe.wait_ge(S(f"ld_x{r}"), b * 16 + 16)
                    if not isinstance(b, int):
                        pe.wait_ge(S(f"b{r}_xbt"), b)
                    for k in range(C):
                        mm = pe.transpose(bank[:, 6, k * P:(k + 1) * P], xblk[:, k * P:(k + 1) * P], ident[:])
                    mm.then_inc(S(f"b{r}_xt"), 1)

                return first, second, nodes

            def block_loop(r):
                n = CH[r]
                first, second, nodes = block_parts(r)

                def body(b, before):
                    for j in range(n):
                        first(b, j)
                        if j == n - 1:
                            nodes(b + 1)
                        if j >= 1:
                            second(b, j - 1)
                        elif before is not None:
                            second(before, n - 1)

                nodes(0)
                body(0, None)
                with pe.Fori(1, BLOCKS) as b:
                    body(b, b - 1)
                second(BLOCKS - 1, n - 1)

            def edge_tile(s, ready, first, last=False):
                pe.wait_ge(S("oh_ready"), ready)
                for k in range(T):
                    pe.matmul(bank[0:R, k, :], OH[:, s, 0, k * R:(k + 1) * R], OH[:, s, 1, 0:512],
                              start=first, stop=last, skip_group_check=True)
                for k in range(T):
                    mm = pe.matmul(bank[0:R, 5 + k // 4, (k % 4) * (N - 512):(k % 4 + 1) * (N - 512)],
                                   OH[:, s, 0, k * R:(k + 1) * R], OH[:, s, 1, 512:N],
                                   start=first and k % 4 == 0, stop=last, skip_group_check=True)
                mm.then_inc(S("oh_used"), 1)

            for s in range(4):
                edge_tile(s, 2 * s + 2, s == 0)
            with pe.Fori(1, ET // 4 - 1) as i:
                for s in range(4):
                    edge_tile(s, i * 8 + 2 * s + 2, False)
            for s in range(4):
                edge_tile(s, 2 * (ET - 4 + s) + 2, False, s == 3)
            pe.wait_ge(S("consts"), CONSTS)
            pe.wait_ge(S("cnt_a"), 5)
            pe.wait_ge(S("cnt_v"), 2)
            for i, (lo, hi) in enumerate(HALVES):
                for k in range(T):
                    mm = pe.matmul(bank[:, 5 + i, 0:hi - lo], ones[0:R, :], AT[:, k, lo:hi], start=(k == 0), stop=(k == T - 1))
                mm.then_inc(S("deg_pe"), 1)
            for t in range(T):
                for k in range(T):
                    mm = pe.matmul(bank[0:R, 7, t:t + 1], AT[:, k, t * R:(t + 1) * R], ones[0:R, 0:1], start=(k == 0), stop=(k == T - 1))
            mm.then_inc(S("deg_pe"), 1)
            pe.wait_ge(S("ln_vec"), 16)
            to_feats(XN, S("tr_full"))
            pe.wait_ge(S("deg_vec"), 10)
            for i, tiles in enumerate(((0, 1, 2), (3, 4))):
                for k, t in enumerate(tiles):
                    mm = pe.matmul(bank[:, 5 + i, k * R:(k + 1) * R], ones[0:R, :], diag[:, t, :], start=True, stop=True)
                mm.then_inc(S("deg_pe"), 1)
            feats_ready(0)
            pe.wait_ge(S("deg_vec"), 12)
            for j, (m, lo, hi) in enumerate(GROUPS):
                for k in range(T):
                    mm = pe.matmul(bank[:, j, 0:hi - lo], XN[:, k, m * P:(m + 1) * P], AT[:, k, lo:hi], start=(k == 0), stop=(k == T - 1))
                mm.then_inc(S("agg_full"), 1)
            pe.wait_ge(S("ld_l0"), 16)
            pe.wait_ge(S("agg_done"), 8)
            project([(Wl, MT), (Wr, XT[:])], S("h_full"))
            pe.wait_ge(S("bn_out"), 4)
            to_rows(HB, S("rows_full"))

            pe.wait_ge(S("ln_vec"), 48)
            to_feats(XN, S("tr_full"))
            pe.wait_ge(S("aff_done"), 4)
            for g in range(3 * T):
                i, t = divmod(g, T)
                if t == 0:
                    pe.wait_ge(S(f"ld_a0_{i}"), 16)
                if g >= 8:
                    pe.wait_ge(S("kvq_done"), g - 7)
                row_group(g % 8, XT, t, (Wq, Wk, Wv)[i], S("kvq_full"))
            pe.wait_ge(S("kvq_done"), 15)
            pe.wait_ge(S("qk_vec"), 27)
            to_feats(QR, S("tr_full"))
            feats_ready(2)
            pe.wait_ge(S("qk_vec"), 32)
            to_feats(KR, S("tr_full"))
            feats_ready(3)
            attention(lambda k: 0, True)
            pe.wait_ge(S("at_norm"), 3 * T)
            to_feats(OR, S("tr_full"))
            feats_ready(4)
            pe.wait_ge(S("ld_a0_3"), 16)
            project([(Wo, OT)], S("wo0_full"))
            pe.wait_ge(S("wo0_done"), 8)
            pe.wait_ge(S("ld_small"), 48)
            router(0, YT)
            mixture(0, YT, M0)

            for t in range(T):
                if t == 0:
                    pe.wait_ge(S("mo_out"), 5)
                for k in range(T):
                    mm = pe.transpose(bank[0:R, t, 0 + k % 4 * P:k % 4 * P + R] if k < 4 else bank[0:R, 5 + t // 4, t % 4 * P:t % 4 * P + R],
                                      AT[:, k, t * R:(t + 1) * R], ident[0:R, 0:R])
                mm.then_inc(S("msk_pe"), 1)
            pe.wait_ge(S("msk_done"), 10)
            pe.wait_ge(S("ln_vec"), 64)
            to_feats(XN, S("tr_full"))
            feats_ready(5)
            with pe.Fori(0, LAYERS) as layer:
                pe.wait_ge(S("ld_g0"), layer * 16 + 16)
                project([(Wq, XT[:])], S("g_q_full"))
                pe.wait_ge(S("ld_g1"), layer * 16 + 16)
                project([(Wk, XT[:])], S("g_k_full"), S("g_q_done"), layer * 8)
                pe.wait_ge(S("ld_g2"), layer * 16 + 16)
                for t in range(T):
                    pe.wait_ge(S("g_k_done"), layer * 8 + t + 1)
                    row_group(t, XT, t, Wv, S("g_v_full"))
                pe.wait_ge(S("g_k_done"), layer * 8 + 8)
                pe.wait_ge(S("g_v_done"), layer * 5 + 5)
                attention(lambda k: layer * k + k, False)
                pe.wait_ge(S("at_norm"), layer * (3 * T) + 6 * T)
                to_feats(OR, S("g_tr_full"))
                pe.wait_ge(S("g_tr_v"), layer * 3 + 3)
                pe.wait_ge(S("g_tr_a"), layer * 2 + 2)
                pe.wait_ge(S("ld_g3"), layer * 16 + 16)
                project([(Wo, OT)], S("g_wo_full"))
                pe.wait_ge(S("g_x1"), layer * 4 + 4)
                pe.wait_ge(S("ld_gf"), layer * 16 + 16)
                for i, (lo, hi) in enumerate(HALVES):
                    for c in range(C):
                        mm = pe.matmul(bank[:, i, 0:hi - lo], Wf1[:, c], X1T[:, c, lo:hi], start=(c == 0), stop=(c == C - 1))
                    mm.then_inc(S("g_f1_full"), 1)
                pe.wait_ge(S("g_f1_done"), layer * 2 + 2)
                for j, (m, lo, hi) in enumerate(GROUPS):
                    pe.matmul(bank[:, j, 0:hi - lo], Wf2[:, m * P:(m + 1) * P], RT[:, lo:hi],
                              start=True, stop=True).then_inc(S("g_w2_full"), 1)
                pe.wait_ge(S("g_x2"), layer * 4 + 4)
            to_rows(XT, S("rows_full"))

            pe.wait_ge(S("ln_vec"), 80)
            to_feats(XN, S("tr_full"))
            feats_ready(6)
            router(1, XT)
            slots(1)
            second_biases()
            pe.wait_ge(S("b2_done"), 5)
            block_loop(1)

            pe.wait_ge(S("ln_vec"), 96)
            pe.wait_ge(S("mo_out"), 10)
            to_feats(XN, S("tr_full"))
            feats_ready(7)
            pe.wait_ge(S("ld_l2"), 16)
            for t in range(T):
                row_group(t, XT, t, Wb, None, BASES)
                for c in range(C):
                    mm = pe.matmul(bank[0:R, 5, t * 32:(t + 1) * 32], XT[:, c, t * R:(t + 1) * R],
                                   gw[:, c, GW["comb"]:GW["comb"] + 32], start=(c == 0), stop=(c == C - 1))
                mm.then_inc(S("bs_full"), 1)
            pe.wait_ge(S("bs_done"), 5)
            pe.wait_ge(S("self_loops"), 5)
            for t in range(T):
                b = (6, 7, 0, 1, 2)[t]
                for k in range(T):
                    mm = pe.matmul(bank[0:R, b, 0:BASES], AT[:, k, t * R:(t + 1) * R], BS[:, k], start=(k == 0), stop=(k == T - 1))
                mm.then_inc(S("ag_full"), 1)
            for t in range(T):
                b = (3, 4, 5, 6, 7)[t]
                if b >= 5:
                    pe.wait_ge(S("l2_vec"), 5)
                row_group(b, XT, t, Wres, S("res_full"))

            pe.wait_ge(S("ln_vec"), 112)
            to_feats(XN, S("tr_full"))
            feats_ready(8)
            router(2, XT)
            mixture(2, XT, M2)

            pe.wait_ge(S("ln_vec"), 128)
            pe.wait_ge(S("mo_out"), 15)
            to_feats(XN, S("tr_full"))
            feats_ready(9)
            pe.wait_ge(S("ld_l3"), 16)
            for t in range(T):
                row_group(t, XT, t, W3, S("xw_full"))
            pe.wait_ge(S("xw_done"), 5)
            for j, (m, lo, hi) in enumerate(GROUPS):
                for k in range(T):
                    mm = pe.matmul(bank[:, j, 0:hi - lo], XW[:, k, m * P:(m + 1) * P], AT[:, k, lo:hi], start=(k == 0), stop=(k == T - 1))
                mm.then_inc(S("h_full"), 1)
            pe.wait_ge(S("bn_out"), 8)
            to_rows(HB, S("rows_full"))

            pe.wait_ge(S("ln_vec"), 144)
            to_feats(XN, S("tr_full"))
            feats_ready(10)
            router(3, XT)
            slots(3)
            block_loop(3)

        @block.scalar
        def _(act):
            def copy_feats(dst, full, done, fbase, dbase, scale=None):
                for t in (1, 3):
                    act.wait_ge(full, fbase + t + 1)
                    act.activation(dst[:, :, t * R:(t + 1) * R], bank[:, t, 0:C * R].rearrange("p (c n) -> p c n", c=C),
                                   ACT.Copy, scale=1.0 if scale is None else scale).then_inc(done, 1)

            def feats(k, dst, scale=None):
                copy_feats(dst, S("tr_full"), S("tr_a"), T * k, 2 * k, scale)

            def bn_apply(src, dst, func, ready, count, done):
                act.wait_ge(ready, count)
                for m in range(C):
                    act.activation(dst[:, m], src[:, m], func, scale=bsc[:, m:m + 1], bias=bsh[:, m:m + 1]).then_inc(done, 1)

            def exps(base, causal):
                for s in range(ATT + (2 if causal else 0)):
                    if s < ATT:
                        kn = (s // H + 1) * R if causal else N
                        act.wait_ge(S("at_mask"), base(ATT) + s + 1)
                        act.activation(SM[:, s % 2, 0:kn], SM[:, s % 2, 0:kn], ACT.Exp, scale=-1.0,
                                       bias=nmx[:, s:s + 1]).then_inc(S("at_exp"), 1)
                    if causal and s >= 1 and s <= ATT:
                        u = s - 1
                        act.wait_ge(S("at_tr"), u + 1)
                        if u >= 2:
                            act.wait_ge(S("at_av"), u - 1)
                        nb = u // H + 1
                        n4 = min(nb, 4)
                        ins = act.activation(PT[:, u % 2, 0:n4, :],
                                             bank[0:R, 4, :].rearrange("p (k n) -> p k n", k=4)[:, 0:n4, 0:R], ACT.Copy)
                        if nb > 4:
                            ins = act.activation(PT[:, u % 2, 4, :], bank[0:R, 5, 0:R], ACT.Copy)
                        ins.then_inc(S("at_pt"), 1)

            def router(r):
                act.wait_ge(S("rt_vec"), ROUTED[r] + 3)
                act.activation(EX[:], LG[:], ACT.Exp).then_inc(S("rt_act"), 1)
                if r == 3:
                    return
                act.wait_ge(S("rt_pe"), 2 * r + 2)
                act.activation(combT[:, 0:500], bank[0:E, 1, 0:500], ACT.Copy).then_inc(S("rt_act"), 1)
                act.activation(combT[:, 500:N], bank[0:E, 2, 0:R], ACT.Copy).then_inc(S("rt_act"), 1)
                if r == 1:
                    return
                for e in range(E):
                    for i, (lo, hi) in enumerate(HALVES):
                        g = 2 * e + i
                        act.wait_ge(S("rt_spread"), 2 * E * (r // 2) + g + 1)
                        act.activation(CB[:, e, lo:hi], bank[:, 3 + g % 5, 0:hi - lo], ACT.Copy).then_inc(S("rt_cb"), 1)

            def mixture(r, bcol):
                for u in range(UNITS):
                    lo, hi = HALVES[u % 2]
                    act.wait_ge(S("mo_h"), UB[r] + u + 1)
                    if u >= 2:
                        act.wait_ge(S("mo_used"), UB[r] + u - 1)
                    act.activation(hg[:, u % 2, 0:hi - lo], bank[:, 5 + u % 3, 0:hi - lo], ACT.Gelu_apprx_tanh,
                                   bias=fvec[:, bcol + u // 2:bcol + u // 2 + 1]).then_inc(S("mo_act"), 1)

            def block_loop(r):
                n = CH[r]

                def silu(b, j):
                    c = b * n + j
                    act.wait_ge(S("b3_a"), c + 1)
                    before = c if j == 0 else c - 1
                    if not (isinstance(before, int) and before <= 0):
                        act.wait_ge(S("b3_h"), before)
                    act.activation(act_s[:, j % 2], bank[:, j % 2, :], ACT.Silu).then_inc(S("b3_s"), 1)

                def hidden(b, j):
                    c = b * n + j
                    act.wait_ge(S(f"b{r}_tr"), c + 1)
                    if r == 3:
                        act.activation(hT[:, j % 2].rearrange("p c n -> p (c n)"), bank[:, 4 + j % 2, :], ACT.Copy).then_inc(S("b3_ht"), 1)
                        return
                    act.wait_ge(S("ld_m1b"), b * 16 + 16)
                    for i in range(4):
                        act.activation(hT[:, j % 2, i], bank[:, 4 + j % 2, i * P:(i + 1) * P], ACT.Relu,
                                       bias=m1b[:, 4 * j + i:4 * j + i + 1]).then_inc(S("b1_ht"), 1)

                def output(b):
                    act.wait_ge(S(f"b{r}_y"), b * n + n)
                    if not (isinstance(b, int) and b == 0):
                        act.wait_ge(S(f"st{r}"), b * 16)
                    act.activation(yblk, bank[:, 7, :], ACT.Copy).then_inc(S(f"st_y{r}"), 1)
                    act.wait_ge(S(f"st_y{r}"), b + 1)
                    act.dma_start(YS[b * P:(b + 1) * P] if isinstance(b, int) else YS[bass.ds(b * P, P)], yblk).then_inc(S(f"st{r}"), 16)

                def body(b, before):
                    for j in range(n):
                        if r == 3:
                            silu(b, j)
                        if j >= 1:
                            hidden(b, j - 1)
                        elif before is not None:
                            hidden(before, n - 1)
                            output(before)

                body(0, None)
                with act.Fori(1, BLOCKS) as b:
                    body(b, b - 1)
                hidden(BLOCKS - 1, n - 1)
                output(BLOCKS - 1)

            act.wait_ge(S("oh_used"), ET)
            for k in range(T):
                act.activation(AT[:, k, 0:512], bank[0:R, k, :], ACT.Copy).then_inc(S("cnt_a"), 1)
            feats(0, XT)
            act.wait_ge(S("ld_small"), 48)
            for j, (m, lo, hi) in enumerate(GROUPS):
                act.wait_ge(S("h_full"), j + 1)
                act.activation(HB[:, m, lo:hi], bank[:, j, 0:hi - lo], ACT.Identity,
                               bias=fvec[:, FV["l0_b"] + m:FV["l0_b"] + m + 1]).then_inc(S("h_done"), 1)
            bn_apply(HB, HB, ACT.Relu, S("bn_vec"), 16, S("bn_out"))

            feats(1, XT)
            for g in range(3 * T):
                i, t = divmod(g, T)
                act.wait_ge(S("kvq_full"), g + 1)
                if i < 2:
                    ins = act.activation((QR, KR)[i][:, t], bank[0:R, g % 8, :], ACT.Copy)
                else:
                    ins = act.activation(V[:, t, :, 0:DH], bank[0:R, g % 8, :].rearrange("p (h d) -> p h d", h=H), ACT.Copy)
                ins.then_inc(S("kvq_done"), 1)
            act.wait_ge(S("aff_done"), 6)
            feats(2, QT, gq[:, 0:1])
            feats(3, KT)
            exps(lambda k: 0, True)
            feats(4, OT)
            for j, (m, lo, hi) in enumerate(GROUPS):
                act.wait_ge(S("wo0_full"), j + 1)
                act.activation(YT[:, m, lo:hi], bank[:, j, 0:hi - lo], ACT.Copy).then_inc(S("wo0_done"), 1)
            router(0)
            mixture(0, FV["m0_b1"])

            feats(5, XT)
            with act.Fori(0, LAYERS) as layer:
                act.wait_ge(S("g_bq"), layer + 1)
                for j, (m, lo, hi) in enumerate(GROUPS):
                    act.wait_ge(S("g_q_full"), layer * 8 + j + 1)
                    act.activation(QT[:, m, lo:hi], bank[:, j, 0:hi - lo], ACT.Identity,
                                   scale=float(DH) ** -0.5, bias=bq8[:, m:m + 1]).then_inc(S("g_q_done"), 1)
                for t in range(T):
                    act.wait_ge(S("g_v_full"), layer * 5 + t + 1)
                    act.activation(V[:, t, :, 0:DH], bank[0:R, t, :].rearrange("p (h d) -> p h d", h=H),
                                   ACT.Copy).then_inc(S("g_v_done"), 1)
                exps(lambda k: layer * k + k, False)
                copy_feats(OT, S("g_tr_full"), S("g_tr_a"), layer * T, 0)
                bn_apply(HC, X1T, ACT.Identity, S("g_bn1_vec"), layer * 17 + 17, S("g_x1"))
                for i, (lo, hi) in enumerate(HALVES):
                    act.wait_ge(S("g_f1_full"), layer * 2 + i + 1)
                    act.activation(RT[:, lo:hi], bank[:, i, 0:hi - lo], ACT.Relu,
                                   bias=lvec[:, LV["b1"]:LV["b1"] + 1]).then_inc(S("g_f1_done"), 1)
                bn_apply(HC, XT, ACT.Identity, S("g_bn2_vec"), layer * 17 + 17, S("g_x2"))

            feats(6, XT)
            router(1)
            block_loop(1)

            feats(7, XT)
            act.wait_ge(S("bs_full"), 5)
            for t in range(T):
                act.activation(BS[:, t], bank[0:R, t, 0:BASES], ACT.Copy, scale=dinvr[:, t:t + 1]).then_inc(S("bs_done"), 1)

            feats(8, XT)
            router(2)
            mixture(2, FV["m2_b1"])

            feats(9, XT)
            for t in range(T):
                act.wait_ge(S("xw_full"), t + 1)
                act.activation(XW[:, t], bank[0:R, t, :], ACT.Copy, scale=dinvr[:, t:t + 1]).then_inc(S("xw_done"), 1)
            bn_apply(HB, HB, ACT.Gelu, S("bn_vec"), 32, S("bn_out"))

            feats(10, XT)
            router(3)
            block_loop(3)

        @block.vector
        def _(dve):
            def copy_feats(dst, full, done, fbase, scale=None):
                for t in (0, 2, 4):
                    dve.wait_ge(full, fbase + t + 1)
                    src = bank[:, t, 0:C * R].rearrange("p (c n) -> p c n", c=C)
                    d = dst[:, :, t * R:(t + 1) * R]
                    ins = dve.tensor_copy(d, src) if scale is None else dve.tensor_scalar(d, src, scale, None, ALU.mult)
                    ins.then_inc(done, 1)

            def feats(k, dst, scale=None):
                copy_feats(dst, S("tr_full"), S("tr_v"), T * k, scale)

            def stats_rows(c, src):
                for t in range(T):
                    c(dve.bn_stats(st[0:R, t], src(t)))
                for t in range(T):
                    if t == 0:
                        c.sync()
                    c(dve.bn_aggr(mv[0:R, t], st[0:R, t]))
                c.sync()
                c(dve.tensor_scalar(ve[0:R, :], mv[0:R, :, 1], EPS, None, ALU.add))

            def ln(k, src=X):
                c = Chain(dve, S("ln_vec"), 16 * k)
                stats_rows(c, lambda t: src[:, t])
                dve.wait_ge(S("ln_pow"), k + 1)
                for t in range(T):
                    c(dve.tensor_scalar(XN[:, t], src[:, t], mv[0:R, t, 0:1], rstd[0:R, t:t + 1], ALU.subtract, ALU.mult))

            def bn(src, done, vec, pow_, gamma, beta, dbase=0, vbase=0, pbase=0):
                c = Chain(dve, vec, vbase)
                for j, (m, lo, hi) in enumerate(GROUPS):
                    dve.wait_ge(done, dbase + j + 1)
                    c(dve.bn_stats(st[:, j], src[:, m, lo:hi]))
                c.sync()
                if not isinstance(vbase, int):
                    c(dve.memset(nop[:, 47:48], 0.0))
                for m in range(C):
                    c(dve.bn_aggr(mv[:, m], st[:, 2 * m:2 * m + 2]))
                c.sync()
                c(dve.tensor_scalar(ve[:, 0:C], mv[:, 0:C, 1], EPS, None, ALU.add))
                dve.wait_ge(pow_, pbase + 1)
                c(dve.tensor_tensor(bsc[:], gamma, rstd[:, 0:C], ALU.mult))
                c.sync()
                c(dve.tensor_tensor(bms[:], mv[:, 0:C, 0], bsc[:], ALU.mult))
                c.sync()
                c(dve.tensor_tensor(bsh[:], beta, bms[:], ALU.subtract))

            def add_rows(before, base):
                c = Chain(dve, S("rows_vec"), base)
                for t in range(T):
                    dve.wait_ge(S("rows_full"), before + t + 1)
                    c(dve.tensor_tensor(XN[:, t], bank[0:R, t, :], XN[:, t], ALU.add))
                    c.sync()
                    c(dve.tensor_tensor(X[:, t], X[:, t], XN[:, t], ALU.add))
                c.sync()

            def attention(base, mask, causal):
                cn = Chain(dve, S("at_norm"), base(3 * T))
                for s in range(ATT + 2):
                    if s < ATT:
                        t = s // H
                        kn = (t + 1) * R if causal else N
                        dve.wait_ge(S("at_s"), base(ATT) + s + 1)
                        if s >= 2:
                            dve.wait_ge(S("at_tr"), base(ATT) + s - 1)
                        if not causal:
                            dve.memset(nop[:, s:s + 1], 0.0)
                        scores = bank[0:R, 2 * (s % 2):2 * (s % 2) + 2, :].rearrange("p b n -> p (b n)")[:, 0:kn]
                        dve.tensor_tensor_reduce(out=SM[:, s % 2, 0:kn], in0=scores, in1=mask(t), scale=-1.0, scalar=3e38,
                                                 op0=ALU.add, op1=ALU.min, accum_out=nmx[:, s:s + 1]).then_inc(S("at_mask"), 1)
                    if not causal and 1 <= s <= ATT:
                        u = s - 1
                        t = u // H
                        dve.wait_ge(S("at_tr"), base(ATT) + u + 1)
                        if u >= 2:
                            dve.wait_ge(S("at_av"), base(ATT) + u - 1)
                        at = AT[:, :, t * R:(t + 1) * R]
                        pt = bank[0:R, 4:6, :].rearrange("p b (k n) -> p (b k) n", n=P)[:, 0:T, 0:R]
                        dve.tensor_tensor(PT[:, u % 2], pt, at, ALU.mult).then_inc(S("at_pt"), 1)
                    if s >= 2 and (s - 2) % H == H - 1:
                        t = (s - 2) // H
                        dve.wait_ge(S("at_av"), base(ATT) + (t + 1) * H)
                        o = bank[0:R, 6:8, 0:4 * (DH + 1)].rearrange("p b (h d) -> p b h d", h=4)
                        cn(dve.tensor_scalar(rden[:].rearrange("p (b h) -> p b h", b=2), o[:, :, :, DH], 1e-16, None, ALU.add))
                        cn.sync()
                        cn(dve.reciprocal(rden[:], rden[:]))
                        cn.sync()
                        for b in range(2):
                            ins = dve.tensor_tensor(OR[:, t, b * 256:(b + 1) * 256].rearrange("p (h d) -> p h d", h=4),
                                                    o[:, b, :, 0:DH], bcast(rden[:, 4 * b:4 * b + 4], DH), ALU.mult)
                            if b == 1:
                                cn(ins)

            def router(r):
                c = Chain(dve, S("rt_vec"), ROUTED[r])
                dve.wait_ge(S("rt_pe"), 2 * r + 1)
                logits = bank[0:R, 0, 0:T * E].rearrange("p (t e) -> p t e", t=T)
                if r in RB:
                    bias = rbias[0:R, RB[r]:RB[r] + E].unsqueeze(1).broadcast_to([R, T, E])
                    c(dve.tensor_tensor(LG[:], logits, bias, ALU.add))
                else:
                    c(dve.tensor_copy(LG[:], logits))
                c.sync()
                c(dve.tensor_reduce(red[:, 0], LG[:], AX.X, ALU.max))
                c.sync()
                c(dve.tensor_tensor(LG[:], LG[:], bcast(red[:, 0], E), ALU.subtract))
                dve.wait_ge(S("rt_act"), 3 * r + 1)
                c(dve.tensor_reduce(red[:, 1], EX[:], AX.X, ALU.add))
                c.sync()
                c(dve.reciprocal(red[:, 1], red[:, 1]))
                c.sync()
                c(dve.tensor_tensor(COMB[:] if r == 0 else PR[:], EX[:], bcast(red[:, 1], E), ALU.mult))
                if r > 0:
                    c.sync()
                    best = LG if r == 1 else PR
                    for t in range(T):
                        c(dve.max(m8[:, t], best[:, t]))
                    c.sync()
                    for t in range(T):
                        c(dve.max_index(i8[:, t], m8[:, t], best[:, t]))
                    c.sync()
                    c(dve.tensor_copy(if8[:], i8[:]))
                    c.sync()
                    for k in range(2):
                        c(dve.tensor_tensor(EQ[:, k], iota8[:].unsqueeze(1).broadcast_to([R, T, E]),
                                            if8[:, :, k:k + 1].broadcast_to([R, T, E]), ALU.is_equal))
                    c.sync()
                    c(dve.tensor_tensor(MK[:], EQ[:, 0], EQ[:, 1], ALU.add))
                    c.sync()
                    c(dve.tensor_tensor(COMB[:], PR[:], MK[:], ALU.mult))
                if r in (1, 3):
                    c.sync()
                    c(dve.tensor_reduce(red[:, 2], COMB[:], AX.X, ALU.add))
                    c.sync()
                    c(dve.reciprocal(red[:, 2], red[:, 2]))
                    c.sync()
                    c(dve.tensor_tensor(COMB[:], COMB[:], bcast(red[:, 2], E), ALU.mult))
                assert c.n == ROUTED[r] + ROUTER_OPS[r]

            def slots(r):
                c = Chain(dve, S(f"sl{r}_vec"))
                dve.wait_ge(S(f"sl{r}_pe"), 1)
                rank = bank[0:R, 0, 64:64 + T * E].rearrange("p (t e) -> p t e", t=T)
                chosen = bank[0:R, 0, 128:128 + E]
                more = gtmp[:, 0:E * PER].rearrange("p (e j) -> p e j", e=E)
                sums = gtmp.rearrange("p (e f) -> p e f", e=E)
                pick = etmp.rearrange("p (k t e) -> p k t e", k=2, t=T)
                c(dve.tensor_tensor(more, bcast(chosen, PER), THR[:], ALU.is_gt))
                c.sync()
                c(dve.tensor_reduce(nblk[:, 0], more, AX.X, ALU.add))
                c.sync()
                c(dve.tensor_tensor(sums, nblk[:, 0].unsqueeze(1).broadcast_to([R, E, E]), LT[:], ALU.mult))
                c.sync()
                c(dve.tensor_reduce(nblk[:, 1], sums, AX.X, ALU.add))
                c.sync()
                c(dve.scalar_tensor_tensor(out=slot[:], in0=nblk[:, 1].unsqueeze(1).broadcast_to([R, T, E]), scalar=float(P),
                                           in1=rank, op0=ALU.mult, op1=ALU.add))
                c.sync()
                c(dve.tensor_tensor(pick, EQ[:], slot[:].unsqueeze(1).broadcast_to([R, 2, T, E]), ALU.mult))
                c.sync()
                c(dve.tensor_reduce(sl[:], pick, AX.X, ALU.add))
                c.sync()
                c(dve.tensor_copy(slu[:], sl[:]))
                c(dve.tensor_tensor(nblk[0:1, 2], nblk[0:1, 0], nblk[0:1, 1], ALU.add))
                c.sync()
                c(dve.tensor_tensor(btmp, bcast(iota_b[:], E), nblk[0:1, 2].unsqueeze(1).broadcast_to([1, BLOCKS, E]), ALU.is_ge))
                c.sync()
                c(dve.tensor_reduce(eb[:, 0], btmp, AX.X, ALU.add))
                c.sync()
                c(dve.tensor_scalar(eb[:, 0], eb[:, 0], float(E - 1), None, ALU.min))
                c.sync()
                c(dve.tensor_tensor(eb[:, 1, 1:], eb[:, 0, 1:], eb[:, 0, 0:BLOCKS - 1], ALU.not_equal))
                c.sync()
                c(dve.tensor_copy(ebi[:, 0], eb[:, 0]))
                c(dve.tensor_copy(ebi[:, 1, 1:], eb[:, 1, 1:]))
                c(dve.tensor_tensor(pick, EQ[:], COMB[:].unsqueeze(1).broadcast_to([R, 2, T, E]), ALU.mult))
                assert c.n == SLOT_OPS
                c.sync()
                dve.tensor_reduce(wk[:], pick, AX.X, ALU.add).then_inc(S("wk"), 1)

            def block_loop(r):
                n = CH[r]

                def hidden(b, j):
                    c = b * n + j
                    if r == 1:
                        dve.wait_ge(S("b1_a"), c + 1)
                    else:
                        dve.wait_ge(S("b3_s"), c + 1)
                        dve.wait_ge(S("b3_g"), c + 1)
                    before = c if j == 0 and n % 2 else c - 1
                    if not (isinstance(before, int) and before <= 0):
                        dve.wait_ge(S(f"b{r}_tr"), before)
                    if r == 1:
                        ins = dve.tensor_copy(hrow[:, j % 2], bank[:, j % 2, :])
                    else:
                        ins = dve.tensor_tensor(hrow[:, j % 2], act_s[:, j % 2], bank[:, 2 + j % 2, :], ALU.mult)
                    ins.then_inc(S(f"b{r}_h"), 1)

                def nodes(b):
                    dve.wait_ge(S(f"b{r}_xt"), b + 1)
                    if not (isinstance(b, int) and b == 0):
                        dve.wait_ge(S("b1_a" if r == 1 else "b3_g"), b * n)
                    dve.tensor_copy(xbT.rearrange("p c n -> p (c n)"), bank[:, 6, :]).then_inc(S(f"b{r}_xbt"), 1)

                nodes(0)
                for j in range(n):
                    hidden(0, j)
                nodes(1)
                with dve.Fori(1, BLOCKS) as b:
                    for j in range(n):
                        hidden(b, j)
                    nodes(b + 1)
                dve.wait_ge(S("wk"), 1 + r // 2)
                c = Chain(dve, S("add"), T * (r // 2))
                for k in range(2):
                    dve.wait_ge(S(f"gathered{k}"), 16 * T * (r // 2 + 1))
                    if k == 1:
                        c.sync()
                    for t in range(T):
                        ins = dve.scalar_tensor_tensor(out=X[:, t], in0=G[k][:, t], scalar=wk[:, k, t:t + 1], in1=X[:, t],
                                                       op0=ALU.mult, op1=ALU.add)
                        if k == 0:
                            c(ins)
                        else:
                            ins.then_inc(S("mo_out"), 1)
                dve.wait_ge(S("mo_out"), T * (r + 1))

            def mixture(r):
                dve.wait_ge(S("rt_cb"), 2 * E * (r // 2 + 1))
                for u in range(UNITS):
                    lo, hi = HALVES[u % 2]
                    dve.wait_ge(S("mo_act"), UB[r] + u + 1)
                    dve.tensor_tensor(hs[:, u % 2, 0:hi - lo], hg[:, u % 2, 0:hi - lo], CB[:, u // 2, lo:hi],
                                      ALU.mult).then_inc(S("mo_hs"), 1)
                c = Chain(dve, S("mo_out"), T * r)
                dve.wait_ge(S("mo_used"), UB[r] + UNITS)
                for t in range(T):
                    c(dve.tensor_tensor(X[:, t], X[:, t], bank[0:R, t, :], ALU.add))
                c.sync()

            c = Chain(dve, S("oh_idx"))
            dve.wait_ge(S("ld_idx"), 16)
            c(dve.tensor_copy(idxf, idxi))
            c.sync()
            dve.wait_ge(S("consts"), CONSTS)

            def one_hots(s, at):
                for k in range(2):
                    dve.tensor_scalar(OH[:, s, k, 0:N], iota16[:, 0:N], at(k), None, ALU.is_equal).then_inc(S("oh_ready"), 1)

            for s in range(4):
                one_hots(s, lambda k: idxf[:, k * ET + s:k * ET + s + 1])
            with dve.Fori(1, ET // 4) as i:
                for s in range(4):
                    dve.wait_ge(S("oh_used"), i * 4 + s - 3)
                    one_hots(s, lambda k: idxf[:, bass.ds(i * 4 + (k * ET + s), 1)])
            dve.wait_ge(S("ld_x"), 16)
            ln(0)
            dve.wait_ge(S("oh_used"), ET)
            c = Chain(dve, S("cnt_v"))
            c(dve.tensor_copy(AT[:, 0:4, 512:N], bank[0:R, 5, 0:4 * (N - 512)].rearrange("p (k n) -> p k n", k=4)))
            c(dve.tensor_copy(AT[:, 4, 512:N], bank[0:R, 6, 0:N - 512]))
            c = Chain(dve, S("deg_vec"))
            for i, (lo, hi) in enumerate(HALVES):
                dve.wait_ge(S("deg_pe"), i + 1)
                c(dve.tensor_scalar(cmx[:, lo:hi], bank[:, 5 + i, 0:hi - lo], 1.0, None, ALU.max))
                c.sync()
                c(dve.reciprocal(rcntb[:, lo:hi], cmx[:, lo:hi]))
            dve.wait_ge(S("deg_pe"), 3)
            c(dve.tensor_scalar(degr[:], bank[0:R, 7, 0:T], 1.0, None, ALU.add))
            feats(0, XT)
            dve.wait_ge(S("deg_pow"), 1)
            for t in range(T):
                c(dve.tensor_scalar(diag[:, t], ident[0:R, 0:R], dinvr[:, t:t + 1], None, ALU.mult))
            for i, (lo, hi) in enumerate(HALVES):
                dve.wait_ge(S("deg_pe"), 4 + i)
                c(dve.tensor_copy(dinvb[:, lo:hi], bank[:, 5 + i, 0:hi - lo]))
            assert c.n == 12
            for j, (m, lo, hi) in enumerate(GROUPS):
                dve.wait_ge(S("agg_full"), j + 1)
                dve.tensor_tensor(MT[:, m, lo:hi], bank[:, j, 0:hi - lo], rcntb[:, lo:hi], ALU.mult).then_inc(S("agg_done"), 1)
            dve.wait_ge(S("ld_small"), 48)
            bn(HB, S("h_done"), S("bn_vec"), S("bn_pow"), fvec[:, FV["l0_g"]:FV["l0_g"] + C], fvec[:, FV["l0_be"]:FV["l0_be"] + C])
            add_rows(0, 0)

            ln(1)
            dve.wait_ge(S("ln_vec"), 32)
            ln(2, XN)
            feats(1, XT)
            c = Chain(dve, S("aff_done"))
            dve.wait_ge(S("tr_v"), 6)
            dve.wait_ge(S("tr_a"), 4)
            for k in range(C):
                c(dve.tensor_scalar(XT[:, k], XT[:, k], fvec[:, FV["ln_g"] + k:FV["ln_g"] + k + 1],
                                    fvec[:, FV["ln_b"] + k:FV["ln_b"] + k + 1], ALU.mult, ALU.add))
            c(dve.tensor_scalar(gq[:], fvec[:, FV["qn"]:FV["qn"] + 1], float(DH) ** 0.5, None, ALU.mult))
            c.sync()
            c(dve.tensor_tensor(gq[:], gq[:], fvec[:, FV["kn"]:FV["kn"] + 1], ALU.mult))
            dve.memset(V[:, :, :, DH:DH + 1], 1.0).then_inc(S("v_ones"), 1)
            c = Chain(dve, S("qk_vec"))
            for i, dst in enumerate((QR, KR)):
                for t in range(T):
                    dve.wait_ge(S("kvq_done"), i * T + t + 1)
                    c(dve.tensor_tensor(SQ[:, t % 2], dst[:, t], dst[:, t], ALU.mult))
                    c.sync()
                    c(dve.tensor_reduce(ss[:, i, t * H:(t + 1) * H], SQ[:, t % 2].rearrange("p (h d) -> p h d", h=H), AX.X, ALU.add))
                c.sync()
                c(dve.tensor_scalar(ss[:, i], ss[:, i], 1e-12, None, ALU.add))
            for i, dst in enumerate((QR, KR)):
                dve.wait_ge(S("qk_pow"), i + 1)
                for t in range(T):
                    d = dst[:, t].rearrange("p (h d) -> p h d", h=H)
                    c(dve.tensor_tensor(d, d, bcast(ssr[:, i, t * H:(t + 1) * H], DH), ALU.mult))
            assert c.n == 32
            dve.wait_ge(S("aff_done"), 6)
            feats(2, QT, gq[:, 0:1])
            feats(3, KT)
            attention(lambda k: 0, lambda t: CM[:, N - (t + 1) * R:N], True)
            feats(4, OT)
            dve.wait_ge(S("ld_small"), 48)
            router(0)
            mixture(0)

            c = Chain(dve, S("msk_done"))
            for t in range(T):
                dve.wait_ge(S("msk_pe"), T)
                c(dve.tensor_scalar(MASK[:, t, 0:4 * R].rearrange("p (k n) -> p k n", k=4),
                                    bank[0:R, t, :].rearrange("p (k n) -> p k n", k=4)[:, :, 0:R], 0.0, NEG, ALU.is_equal, ALU.mult))
                c(dve.tensor_scalar(MASK[:, t, 4 * R:N], bank[0:R, 5 + t // 4, t % 4 * P:t % 4 * P + R], 0.0, NEG, ALU.is_equal, ALU.mult))
            ln(3)
            dve.memset(V[:, :, :, DH:DH + 1], 1.0).then_inc(S("v_ones"), 1)
            feats(5, XT)
            dve.wait_ge(S("msk_done"), 10)
            with dve.Fori(0, LAYERS) as layer:
                dve.wait_ge(S("ld_lvec"), layer * 16 + 16)
                dve.tensor_scalar(bq8[:], lvec[:, LV["bq"]:LV["bq"] + C], float(DH) ** -0.5, None, ALU.mult).then_inc(S("g_bq"), 1)
                for j, (m, lo, hi) in enumerate(GROUPS):
                    dve.wait_ge(S("g_k_full"), layer * 8 + j + 1)
                    dve.tensor_copy(KT[:, m, lo:hi], bank[:, j, 0:hi - lo]).then_inc(S("g_k_done"), 1)
                attention(lambda k: layer * k + k, lambda t: MASK[:, t], False)
                copy_feats(OT, S("g_tr_full"), S("g_tr_v"), layer * T)
                for name, full, bias, res, base in (("1", "g_wo_full", "bo", XT, 8), ("2", "g_w2_full", "b2", X1T, 8)):
                    for j, (m, lo, hi) in enumerate(GROUPS):
                        dve.wait_ge(S(full), layer * 8 + j + 1)
                        dve.scalar_tensor_tensor(out=HC[:, m, lo:hi], in0=bank[:, j, 0:hi - lo],
                                                 scalar=lvec[:, LV[bias] + m:LV[bias] + m + 1], in1=res[:, m, lo:hi],
                                                 op0=ALU.add, op1=ALU.add).then_inc(S(f"g_res{name}"), 1)
                    bn(HC, S(f"g_res{name}"), S(f"g_bn{name}_vec"), S(f"g_bn{name}_pow"),
                       lvec[:, LV["g" + name]:LV["g" + name] + C], lvec[:, LV["be" + name]:LV["be" + name] + C],
                       layer * 8, layer * 17, layer)

            c = Chain(dve, S("lf_vec"))
            dve.wait_ge(S("rows_full"), 2 * T)
            stats_rows(c, lambda t: bank[0:R, t, :])
            dve.wait_ge(S("lf_pow"), 1)
            dve.wait_ge(S("ld_rvec1"), 16)
            for t in range(T):
                c(dve.tensor_scalar(XN[:, t], bank[0:R, t, :], mv[0:R, t, 0:1], rstd[0:R, t:t + 1], ALU.subtract, ALU.mult))
            c.sync()
            for t in range(T):
                c(dve.tensor_tensor(XN[:, t], XN[:, t], rvec[0:R, 0], ALU.mult))
            c.sync()
            for t in range(T):
                c(dve.tensor_tensor(XN[:, t], XN[:, t], rvec[0:R, 1], ALU.add))
            c.sync()
            for t in range(T):
                c(dve.tensor_tensor(X[:, t], X[:, t], XN[:, t], ALU.add))
            c.sync()

            ln(4)
            feats(6, XT)
            router(1)
            slots(1)
            c = Chain(dve, S("b2_done"))
            for t in range(T):
                dve.wait_ge(S("b2_full"), t + 1)
                c(dve.tensor_tensor(X[:, t], X[:, t], bank[0:R, 3 + t, :], ALU.add))
            c.sync()
            block_loop(1)

            ln(5)
            for t in range(T):
                d = AT[:, t, t * R:(t + 1) * R]
                dve.tensor_tensor(d, d, ident[0:R, 0:R], ALU.add).then_inc(S("self_loops"), 1)
            feats(7, XT)
            c = Chain(dve, S("l2_vec"))
            dve.wait_ge(S("bs_full"), 5)
            c(dve.tensor_tensor(WGT[:], bank[0:R, 5, 0:T * 32].rearrange("p (t n) -> p t n", t=T),
                                rbias[0:R, RB["comb"]:RB["comb"] + 32].unsqueeze(1).broadcast_to([R, T, 32]), ALU.add))
            for t in range(T):
                dve.wait_ge(S("ag_full"), t + 1)
                c(dve.tensor_scalar(AG[:, t], bank[0:R, (6, 7, 0, 1, 2)[t], 0:BASES], dinvr[:, t:t + 1], None, ALU.mult))
            c.sync()
            dve.wait_ge(S("ld_rvec2"), 16)
            c(dve.tensor_tensor(rvec[0:R, 0], rvec[0:R, 0], rvec[0:R, 1], ALU.add))
            c.sync()
            for t in range(T):
                w = WGT[:, t].rearrange("p (h b) -> p h b", h=H)
                for b in range(NB):
                    c(dve.tensor_tensor(CV[:, b].rearrange("p (h f) -> p h f", h=H),
                                        AG[:, t, b * DH:(b + 1) * DH].unsqueeze(1).broadcast_to([R, H, DH]),
                                        w[:, :, b:b + 1].broadcast_to([R, H, DH]), ALU.mult))
                c.sync()
                c(dve.tensor_tensor(CV[:, 0], CV[:, 0], CV[:, 1], ALU.add))
                c(dve.tensor_tensor(CV[:, 2], CV[:, 2], CV[:, 3], ALU.add))
                c.sync()
                c(dve.tensor_tensor(CV[:, 0], CV[:, 0], CV[:, 2], ALU.add))
                c.sync()
                c(dve.tensor_tensor(CV[:, 0], CV[:, 0], rvec[0:R, 0], ALU.add))
                c.sync()
                dve.wait_ge(S("res_full"), t + 1)
                c(dve.tensor_tensor(XN[:, t], CV[:, 0], bank[0:R, 3 + t, :], ALU.add))
                c.sync()
            assert c.n == 52
            stats_rows(c, lambda t: XN[:, t])
            dve.wait_ge(S("l2_pow"), 1)
            for t in range(T):
                c(dve.tensor_scalar(XN[:, t], XN[:, t], mv[0:R, t, 0:1], rstd[0:R, t:t + 1], ALU.subtract, ALU.mult))
            c.sync()
            for t in range(T):
                c(dve.tensor_tensor(XN[:, t], XN[:, t], rvec[0:R, 2], ALU.mult))
            c.sync()
            for t in range(T):
                c(dve.tensor_tensor(XN[:, t], XN[:, t], rvec[0:R, 3], ALU.add))
            c.sync()
            for t in range(T):
                c(dve.scalar_tensor_tensor(out=X[:, t], in0=XN[:, t], scalar=0.0, in1=X[:, t], op0=ALU.max, op1=ALU.add))
            c.sync()

            ln(6)
            feats(8, XT)
            router(2)
            mixture(2)

            ln(7)
            feats(9, XT)
            c = Chain(dve, S("h3_scaled"))
            for j, (m, lo, hi) in enumerate(GROUPS):
                dve.wait_ge(S("h_full"), 8 + j + 1)
                c(dve.tensor_tensor(HB[:, m, lo:hi], bank[:, j, 0:hi - lo], dinvb[:, lo:hi], ALU.mult))
                c.sync()
                dve.tensor_scalar(HB[:, m, lo:hi], HB[:, m, lo:hi], fvec[:, FV["l3_b"] + m:FV["l3_b"] + m + 1], None,
                                  ALU.add).then_inc(S("h_done"), 1)
            bn(HB, S("h_done"), S("bn_vec"), S("bn_pow"), fvec[:, FV["l3_g"]:FV["l3_g"] + C], fvec[:, FV["l3_be"]:FV["l3_be"] + C], 8, 16, 1)
            add_rows(2 * T, 2 * T)

            ln(8)
            feats(10, XT)
            router(3)
            slots(3)
            block_loop(3)


def _by_feature(v):
    return np.asarray(v).reshape(-1, P).T


def _rhs(w):
    w = np.asarray(w)
    return w.reshape(-1, P, w.shape[1]).transpose(1, 0, 2)


def kernel(**inputs):
    import concourse.bacc as bacc
    from concourse.bass_utils import run_bass_kernel_spmd

    g = {k: np.asarray(v) for k, v in inputs.items()}
    cat = np.concatenate
    L = {}
    L["x"] = g["x"].reshape(T, R, D).transpose(1, 0, 2)
    L["edges"] = cat([g["src"].reshape(ET, R).T, g["dst"].reshape(ET, R).T], 1)
    f = _by_feature
    L["fvec"] = cat([f(g["L0_gnn_b_l"]), f(g["L0_gnn_gamma"]), f(g["L0_gnn_beta"]), f(g["L0_ffn_ln_g"]), f(g["L0_ffn_ln_b"]),
                     f(cat([g["L0_ffn_qn_g"]] * 2)), f(cat([g["L0_ffn_kn_g"]] * 2)), f(g["L0_ffn_b1"]),
                     f(g["L2_ffn_b1"]), f(g["L3_gnn_b"]), f(g["L3_gnn_gamma"]), f(g["L3_gnn_beta"])], 1)
    L["lvec"] = np.stack([cat([f(g["L1_gnn_" + n][l]) for n in ("bq", "bo", "b1", "b2", "g1", "beta1", "g2", "beta2")], 1)
                          for l in range(LAYERS)])
    L["gw"] = _rhs(cat([g["L0_ffn_gate_W"], g["L1_ffn_gate_w"], g["L2_ffn_Wg"], g["L3_ffn_router_w"].T, g["L2_gnn_W_comb"]], 1))
    L["rbias"] = cat([g["L0_ffn_gate_b"], g["L1_ffn_gate_b"], g["L2_ffn_bg"], g["L2_gnn_b_comb"]])[None]
    L["rvec1"] = np.stack([g["L1_gnn_ln_g"], g["L1_gnn_ln_b"]])[None]
    L["rvec2"] = np.stack([g["L2_gnn_conv_bias"], g["L2_gnn_b_res"], g["L2_gnn_gamma"], g["L2_gnn_beta"]])[None]
    L["b2"] = np.stack([g["L0_ffn_b2"], g["L1_ffn_b2"], g["L2_ffn_b2"]])
    L["m1_b1"] = g["L1_ffn_b1"].reshape(E, F1 // P, P).transpose(0, 2, 1)
    L["w_l0"] = cat([_rhs(g["L0_gnn_W_l"].T), _rhs(g["L0_gnn_W_r"].T)], 1).reshape(P, -1)
    L["w_a0"] = np.stack([_rhs(g["L0_ffn_" + n]).reshape(P, -1) for n in ("Wq", "Wk", "Wv", "Wo")], 1)
    L["w_g"] = np.stack([np.stack([_rhs(g["L1_gnn_" + n][l].T).reshape(P, -1) for n in ("Wq", "Wk", "Wv", "Wo")], 1) for l in range(LAYERS)])
    L["w_gf"] = np.stack([cat([_rhs(g["L1_gnn_W1"][l].T).reshape(P, -1), g["L1_gnn_W2"][l].T], 1) for l in range(LAYERS)])
    L["w_l2"] = cat([_rhs(g["L2_gnn_W_bases"]).reshape(P, -1), _rhs(g["L2_gnn_W_res"]).reshape(P, -1)], 1)
    L["w_l3"] = _rhs(g["L3_gnn_W"].T).reshape(P, -1)

    def chunks(ins, w2):
        J = w2.shape[1] // P
        first = [w.reshape(E, C, P, J, P).transpose(0, 3, 2, 1, 4).reshape(E, J, P, C * P) for w in ins]
        return cat(first + [w2.reshape(E, J, P, D)], 3)

    L["w_m0"] = chunks([g["L0_ffn_W1"]], g["L0_ffn_W2"])[:, 0]
    L["w_m2"] = chunks([g["L2_ffn_W1"]], g["L2_ffn_W2"])[:, 0]

    def parts(ins, w2, order):
        at = {}
        for name, w in ins.items():
            for j in range(w.shape[2] // D):
                at[name, j] = w[:, :, j * D:(j + 1) * D].reshape(E, C, P, D).transpose(0, 2, 1, 3)
        for j in range(w2.shape[1] // D):
            at["y", j] = w2[:, j * D:(j + 1) * D].reshape(E, 4, P, D).transpose(0, 2, 1, 3)
        return np.stack([at[p].reshape(E, P, -1) for p in order], 1)

    L["w_m1"] = parts({"a": g["L1_ffn_w1"]}, g["L1_ffn_w2"], PARTS[1])
    L["w_m3"] = parts({"a": g["L3_ffn_w1"].transpose(0, 2, 1), "g": g["L3_ffn_wgate"].transpose(0, 2, 1)},
                      g["L3_ffn_w2"].transpose(0, 2, 1), PARTS[3])

    nc = bacc.Bacc("TRN2", target_bir_lowering=False, num_devices=1)
    arrays, aps = {}, {}
    for name, a in L.items():
        a = np.ascontiguousarray(a)
        arrays["in_" + name] = a
        aps[name] = nc.dram_tensor("in_" + name, a.shape, mybir.dt.from_np(a.dtype), kind="ExternalInput").ap()
    out = nc.dram_tensor("out_x", (R, T, D), F32, kind="ExternalOutput").ap()
    graph_network(nc, aps, out)
    r = run_bass_kernel_spmd(nc, [arrays], core_ids=[0])
    return np.asarray(r.results[0]["out_x"]).transpose(1, 0, 2).reshape(N, D)
```

```python
from contextlib import ExitStack

import numpy as np

import concourse.bass as bass
from concourse import mybir

ALU = mybir.AluOpType
ACT = mybir.ActivationFunctionType
AX = mybir.AxisListType
F32 = mybir.dt.float32
F32R = mybir.dt.float32r
BF16 = mybir.dt.bfloat16
F16 = mybir.dt.float16
I32 = mybir.dt.int32
U32 = mybir.dt.uint32

P = 128
N = 625
R = 125
T = N // R
D = 512
C = D // P
EDGES = 10000
ET = EDGES // R
H = 8
DH = D // H
E = 8
LAYERS = 2
F1 = 1024
F3 = 1536
BASES = 256
NB = 4
BLOCKS = (2 * N - E) // P + E
PER = -(-N // P)
HALVES = ((0, 3 * R), (3 * R, N))
NEG = -1e30
EPS = 1e-5

FV = {}
_at = 0
for _n, _w in (("l0_b", 4), ("l0_g", 4), ("l0_be", 4), ("ln_g", 4), ("ln_b", 4), ("qn", 1), ("kn", 1),
               ("m0_b1", 8), ("m1_b1", 64), ("m2_b1", 8), ("l3_b", 4), ("l3_g", 4), ("l3_be", 4)):
    FV[_n] = _at
    _at += _w
FVW = _at
LV = {}
_at = 0
for _n, _w in (("bq", 4), ("bo", 4), ("b1", 1), ("b2", 4), ("g1", 4), ("be1", 4), ("g2", 4), ("be2", 4)):
    LV[_n] = _at
    _at += _w
LVW = _at
GW = {0: 0, 1: 8, 2: 16, 3: 24, "comb": 32}
GWW = 64
RB = {0: 0, 1: 8, 2: 16, "comb": 24}
RBW = 56


CH = {1: F1 // D, 3: F3 // D}
PARTS = {1: (("a", 0), ("a", 1), ("y", 0), ("y", 1)),
         3: (("a", 0), ("g", 0), ("a", 1), ("g", 1), ("y", 0), ("a", 2), ("g", 2), ("y", 1), ("y", 2))}


STREAMS = {1: {"a": (("a", 0), ("a", 1)), "y": (("y", 0),), "z": (("y", 1),)},
           3: {"a": (("a", 0), ("g", 0), ("a", 1), ("g", 1), ("a", 2), ("g", 2)), "y": (("y", 0), ("y", 1), ("y", 2))}}
SLOTS = {1: {"a": 4, "y": 2, "z": 2}, 3: {"a": 4, "y": 3}}
BY_POOL = {1: "z", 3: "y"}
HALF = 1024
WHERE = {r: {p: (s, 2 * i, 2 * len(ps)) for s, ps in STREAMS[r].items() for i, p in enumerate(ps)} for r in STREAMS}


class Chain:

    def __init__(self, eng, sem, base=0):
        self.eng, self.sem, self.n = eng, sem, base

    def __call__(self, ins):
        ins.then_inc(self.sem, 1)
        self.n = self.n + 1

    def sync(self):
        self.eng.wait_ge(self.sem, self.n)


def graph_network(nc, A, out):
    ctx = ExitStack()
    with ctx:
        sems = {}

        def S(name):
            if name not in sems:
                sems[name] = ctx.enter_context(nc.semaphore(name))
            return sems[name]

        def sb(name, shape, dt=F32):
            t = ctx.enter_context(nc.sbuf_tensor("sb_" + name, shape, dt))
            start[name] = nc.sbuf_base - 4 * int(np.prod(shape[1:]))
            return t

        start = {}

        def rounded(name, at, n):
            return nc.alloc_sbuf_tensor_at(f"sb_{name}_r{at}", [P, n], F32R, offset=start[name] + 4 * at)[:]

        bank = ctx.enter_context(nc.psum_tensor("bank", [P, 8, 512], F32))

        X = sb("X", [R, T, D])
        XNf = sb("XN", [P, T * D])
        XN = XNf[0:R].rearrange("p (t d) -> p t d", t=T)
        XT = sb("XT", [P, C, N])
        ATf = sb("AT", [P, T * N])
        AT = ATf[0:R].rearrange("p (t n) -> p t n", t=T)
        ident = sb("ident", [P, P])
        ones = sb("ones", [P, P])
        SEL = sb("SEL", [E, E, P], F32R)
        TRI = sb("TRI", [R, R])
        LT = sb("LT", [P, E, E])
        THR = sb("THR", [P, E, PER])
        iota_b = sb("iota_b", [P, BLOCKS])
        nop = sb("nop", [1, 48])
        iota8 = sb("iota8", [P, E])
        fvec = sb("fvec", [P, FVW])
        lvec = sb("lvec", [P, LVW])
        rvec = sb("rvec", [P, 4, D])
        rbias = sb("rbias", [P, RBW])
        gw = sb("gw", [P, C, GWW])
        b2 = sb("b2", [E, D])
        dinvb = sb("dinvb", [P, N])
        dinvr = sb("dinvr", [R, T])
        half8 = sb("half8", [P, 1])
        st = sb("st", [P, 8, 6])
        mv = sb("mv", [P, T, 2])
        ve = sb("ve", [P, T])
        rstd = sb("rstd", [P, T])
        nbias = sb("nbias", [R, T])
        rstd2 = sb("rstd2", [R, T])
        rstd3 = sb("rstd3", [R, T])
        bsc = sb("bsc", [P, C])
        bsh = sb("bsh", [P, C])
        bms = sb("bms", [P, C])
        degr = sb("degr", [R, T])
        gq = sb("gq", [P, 1])
        bq8 = sb("bq8", [P, C])
        ss = sb("ss", [R, 2, T * H])
        ssr = sb("ssr", [R, 2, T * H])
        nmx = sb("nmx", [R, T * H])
        rden = sb("rden", [R, H])
        LG = sb("LG", [R, T, E])
        EX = sb("EX", [R, T, E])
        PR = sb("PR", [R, T, E])
        COMB = sb("COMB", [R, T, E])
        EQ = sb("EQ", [R, 2, T, E])
        MK = sb("MK", [R, T, E])
        nblk = sb("nblk", [P, 3, E])
        slot = sb("slot", [R, T, E])
        sl = sb("sl", [R, 2, T])
        slu = sb("slu", [R, 2, T], U32)
        wk = sb("wk", [R, 2, T])
        eb = sb("eb", [P, 2, BLOCKS])
        ebi = sb("ebi", [1, 2, BLOCKS], I32)
        red = sb("red", [R, 3, T])
        m8 = sb("m8", [R, T, 8])
        i8 = sb("i8", [R, T, 8], U32)
        if8 = sb("if8", [R, T, 8])
        m1b = sb("m1b", [P, F1 // P])
        WGT = sb("WGT", [R, T, H * NB])

        W = sb("W", [P, 17408])
        rA = sb("rA", [P, T * D])
        rB = sb("rB", [P, T * D])
        rC = sb("rC", [P, C * N])
        rDE = sb("rDE", [P, C * N + T * H * (DH + 1)])
        rF = sb("rF", [P, 4 * N])
        rG = sb("rG", [P, T * N])

        def rows(r):
            return r[0:R, 0:T * D].rearrange("p (t d) -> p t d", t=T)

        def feats(r, at=0):
            return r[:, at:at + C * N].rearrange("p (c n) -> p c n", c=C)

        QR, KR, OR = rows(rA), rows(rB), rows(rA)
        QT, KT = feats(rC), feats(rDE)
        V = rDE[0:R, C * N:].rearrange("p (t h d) -> p t h d", t=T, h=H)
        OT = feats(rB)
        YT = feats(rC)
        MT, HB = feats(rA), feats(rB)
        HC, X1T = feats(rC), feats(rDE)
        SM = rF[0:R, 0:2 * N].rearrange("p (b n) -> p b n", b=2)
        PT = rF[0:R, 2 * N:4 * N].rearrange("p (b t n) -> p b t n", b=2, t=T)
        RT = rF[:, 0:N]
        hs = rF[:, 0:2 * 375].rearrange("p (b n) -> p b n", b=2)
        hg = rF[:, 750:2 * 750].rearrange("p (b n) -> p b n", b=2)
        combT = rF[0:E, 1500:1500 + N]
        SELf = rDE[0:E, 0:E * P].rearrange("p (e n) -> p e n", e=E)
        combH, combL = (rounded("rB", at, N)[0:E] for at in (0, 632))
        CB = rDE[:, 0:E * N].rearrange("p (e n) -> p e n", e=E)
        MASK = rG[0:R, :].rearrange("p (t n) -> p t n", t=T)
        CM = rvec[0:R].rearrange("p k d -> p (k d)")[:, 0:N]
        OH = rA[0:R, 0:4 * 640].bitcast(BF16).rearrange("p (s k n) -> p s k n", s=4, k=2)
        iota16 = rB[0:R, 0:320].bitcast(F16)
        idxi = rB[0:R, 320:320 + 2 * ET].bitcast(I32)
        idxf = rB[0:R, 480:480 + 2 * ET]
        diag = rB[0:R, 640:640 + N].rearrange("p (t n) -> p t n", t=T)
        cmx = rB[:, 1280:1280 + N]
        rcntb = rG[:, 700:700 + N]
        SQ = rF[0:R, 0:2 * D].rearrange("p (b n) -> p b n", b=2)
        BS = rA[0:R, 0:T * BASES].rearrange("p (t n) -> p t n", t=T)
        XW = rows(rA)
        AG = rB[0:R, 0:T * BASES].rearrange("p (t n) -> p t n", t=T)
        CV = rC[0:R, 0:4 * D].rearrange("p (b n) -> p b n", b=4)

        PV = rDE[0:R, 0:4 * D].rearrange("p (s b n) -> p s b n", s=2, b=2)
        L2_TILE0, L2_TILE = 2 + T, 5
        L2_OPS = L2_TILE0 + L2_TILE * T

        def basis(eng, dst, t, b):
            return eng.tensor_tensor(dst.rearrange("p (h f) -> p h f", h=H),
                                     AG[:, t, b * DH:(b + 1) * DH].unsqueeze(1).broadcast_to([R, H, DH]),
                                     WGT[:, t].rearrange("p (h b) -> p h b", h=H)[:, :, b:b + 1].broadcast_to([R, H, DH]), ALU.mult)

        def mat(at, k, n):
            return W[:, at:at + k * n].rearrange("p (c n) -> p c n", c=k)

        Wl, Wr = mat(0, C, D), mat(2048, C, D)
        Wq, Wk, Wv, Wo = (mat(4096 + 2048 * i, C, D) for i in range(4))
        Wf1, Wf2 = mat(16384, C, P), W[:, 16896:17408]
        Wb, Wres = mat(0, C, BASES), mat(1024, C, D)
        W3 = mat(3072, C, D)
        M0 = [12288 + 1024 * e if e < 4 else 1024 * (e - 4) for e in range(E)]
        M2 = [8192 + 1024 * e for e in range(E)]
        XS = nc.dram_tensor("slots_in", (P * (BLOCKS + 1), D), F32).ap()
        YS = nc.dram_tensor("slots_out", (P * BLOCKS, D), F32).ap()
        fill = rC[:, 0:D]
        xblk = rC[:, 0:D]
        xbh, xbl = (rounded("rC", at, D).rearrange("p (c n) -> p c n", c=C) for at in (D, 3 * D))
        yblk = rC[:, 2 * D:3 * D]
        act_s = rF[:, 0:2 * D].rearrange("p (b n) -> p b n", b=2)
        hrow = rF[:, 2 * D:4 * D].rearrange("p (b n) -> p b n", b=2)
        hTh, hTl = (rounded("rG", at, 2 * D).rearrange("p (b n) -> p b n", b=2) for at in (0, 2 * D))

        B0, X0, C0 = {1: 0, 3: BLOCKS}, {1: 0, 3: BLOCKS + 1}, {1: 0, 3: BLOCKS * CH[1]}

        def pieces(buf, at, n):
            return [rounded(buf, at + HALF * i, HALF) for i in range(n)]

        both = pieces("rA", 0, 2) + pieces("rB", 0, 2) + pieces("XT", 0, 2) + pieces("rG", 4 * D, 1)
        space = {1: both + pieces("rDE", 640, 4) + pieces("W", 5120, 3) + pieces("XN", 0, 2),
                 3: both + pieces("AT", 0, 3) + pieces("rvec", 0, 2) + pieces("XN", 0, 2)}
        ring = {}
        for r in STREAMS:
            at = 0
            for name, k in SLOTS[r].items():
                ring[r, name] = [(space[r][at + 2 * i], space[r][at + 2 * i + 1]) for i in range(k)]
                at += 2 * k

        def half(r, p, h):
            name, i, _ = WHERE[r][p]
            return ring[r, name][(i + h) % SLOTS[r][name]]

        def nth(r, p, h, b):
            _, i, per_block = WHERE[r][p]
            return b * per_block + (i + h + 1)

        def split(r, p, h, b, kind):
            return S(f"w{r}_{kind}_{WHERE[r][p][0]}"), nth(r, p, h, b)

        def used(r, p, b):
            return split(r, p, 1, b, "used")

        def low(eng, r, p, b, src):
            for h in range(2):
                hi, lo = half(r, p, h)
                eng.wait_ge(*split(r, p, h, b, "hi"))
                eng.tensor_tensor(lo, src[:, HALF * h:HALF * (h + 1)], hi.bitcast(F32),
                                  ALU.subtract).then_inc(split(r, p, h, b, "lo")[0], 1)

        G = (rows(rA), rows(rB))
        gtmp = rDE[:, 0:E * E]
        btmp = rDE[:, 256:256 + BLOCKS * E].rearrange("p (b e) -> p b e", e=E)
        etmp = rDE[0:R, 512:512 + 2 * T * E]
        M1 = F1 // P
        biases = rDE[:, 4736:4736 + BLOCKS * M1].rearrange("p (b m) -> p b m", b=BLOCKS)
        bprod = rG[:, 0:BLOCKS * M1 * E].rearrange("p (b m e) -> p b m e", b=BLOCKS, m=M1)

        def part(i):
            return W[:, 2048 * i:2048 * (i + 1)] if i < 8 else rDE[:, 2560:2560 + 2048]

        def bcast(ap, k):
            return ap.unsqueeze(2).broadcast_to([ap.shape[0], ap.shape[1], k])

        GROUPS = [(m, lo, hi) for m in range(C) for lo, hi in HALVES]
        ATT = T * H

        def step(s, causal):
            t, h = divmod(s, H)
            return (T - 1 - t, h, (T - t) * R) if causal else (t, h, N)

        CONSTS = 17
        NORMS = 8 + 2 * LAYERS
        POW = {"ln0": 1, "deg": 2, "bn0": 3, "ln1": 4, "ln2": 5, "q": 6, "k": 7, "ln3": 8, "lf": NORMS + 1, "ln4": NORMS + 2,
               "ln5": NORMS + 3, "l2": NORMS + 4, "ln6": NORMS + 5, "ln7": NORMS + 6, "bn3": NORMS + 7, "ln8": NORMS + 8}
        LN = [16 * k if k < 2 else 16 * (k - 1) + 4 for k in range(9)]
        RT_ACT = {0: 0, 1: 5, 2: 8, 3: 13}
        LAST_BN = 16 + 34 * LAYERS
        ROUTER_OPS = (6, 24, 21, 24)
        SLOT_OPS = 17
        ROUTED = [sum(ROUTER_OPS[:r]) for r in range(4)]
        UNITS = 2 * E
        UB = {0: 0, 2: UNITS}
        PLACE = {r: {p: i + (4 if r == 1 else 0) for i, p in enumerate(PARTS[r])} for r in PARTS}

        block = ctx.enter_context(nc.Block())

        def with_layers(sp):
            names = ("g_q_full", "g_k_full", "g_v_full", "g_wo_full")
            counts = (8, 8, 5, 8)

            def load(layer, after_first):
                for i in range(4):
                    if after_first:
                        sp.wait_ge(S(names[i]), layer * counts[i])
                    sp.dma_start(W[:, 4096 + 2048 * i:6144 + 2048 * i],
                                 A["w_g"][bass.ds(layer, 1), :, i].rearrange("l p n -> (l p) n")).then_inc(S(f"ld_g{i}"), 16)
                if after_first:
                    sp.wait_ge(S("g_w2_full"), layer * 8)
                sp.dma_start(W[:, 16384:17408], A["w_gf"][bass.ds(layer, 1)].rearrange("l p n -> (l p) n")).then_inc(S("ld_gf"), 16)
                if after_first:
                    sp.wait_ge(S("g_x2"), layer * 2)
                    sp.wait_ge(S("g_x2v"), layer * 2)
                sp.dma_start(lvec[:], A["lvec"][bass.ds(layer, 1)].rearrange("l p n -> (l p) n")).then_inc(S("ld_lvec"), 16)

            load(0, False)
            with sp.Fori(1, LAYERS) as layer:
                load(layer, True)

        def blocks(sp, r, src):

            def weights(p, b, e, new):
                if new is not None:
                    sp.wait_ge(*split(r, p, 1, b - 1, "lo"))
                sp.dma_start(part(PLACE[r][p]), src[e, PARTS[r].index(p)],
                             cond=None if new is None else new > 0).then_inc(S(f"ld{r}_{p[0]}{p[1]}"), 16)

            def nodes(b):
                if not (isinstance(b, int) and b == 0):
                    sp.wait_ge(S("b_xt"), b + X0[r])
                sp.dma_start(xblk, XS[b * P:(b + 1) * P] if isinstance(b, int) else XS[bass.ds(b * P, P)]).then_inc(S("ld_xb"), 16)

            def expert(b):
                at = slice(b, b + 1) if isinstance(b, int) else bass.ds(b, 1)
                return sp.value_load(ebi[0:1, 0, at], min_val=0, max_val=E - 1)

            def changed(b):
                if isinstance(b, int) and b == 0:
                    return None
                at = slice(b, b + 1) if isinstance(b, int) else bass.ds(b, 1)
                return sp.value_load(ebi[0:1, 1, at], min_val=0, max_val=1)

            def body1(b, e0, new0):
                e, new = expert(b), changed(b)
                weights(("a", 0), b, e, new)
                weights(("a", 1), b, e, new)
                weights(("y", 1), b - 1, e0, new0)
                nodes(b + 1)
                weights(("y", 0), b, e, new)
                return e, new

            sp.wait_ge(S("sl_vec"), SLOT_OPS * (r // 2 + 1))
            e = expert(0)
            for p in PARTS[r][:1]:
                weights(p, 0, e, None)
            sp.wait_ge(S("sc"), 16 * 2 * T * (r // 2 + 1))
            nodes(0)
            if r == 1:
                for p in PARTS[1][1:3]:
                    weights(p, 0, e, None)
                nodes(1)
                body1(1, e, None)
                with sp.Fori(2, BLOCKS) as b:
                    body1(b, expert(b - 1), changed(b - 1))
                weights(("y", 1), BLOCKS - 1, expert(BLOCKS - 1), changed(BLOCKS - 1))
                return
            for p in PARTS[3][1:]:
                weights(p, 0, e, None)
            nodes(1)
            with sp.Fori(1, BLOCKS) as b:
                e, new = expert(b), changed(b)
                for p in PARTS[3]:
                    if p == PARTS[3][-1]:
                        nodes(b + 1)
                    weights(p, b, e, new)

        @block.sync
        def _(sp):
            sp.dma_start(idxi, A["edges"]).then_inc(S("ld_idx"), 16)
            sp.wait_ge(S("fill"), 1)
            sp.dma_start(XS.rearrange("(b p) d -> p b d", p=P), fill.unsqueeze(1).broadcast_to([P, BLOCKS + 1, D])).then_inc(S("filled"), 16)
            sp.dma_start(X[:], A["x"]).then_inc(S("ld_x"), 16)
            sp.dma_start(fvec[:], A["fvec"]).then_inc(S("ld_small"), 16)
            sp.dma_start(W[:, 0:4096], A["w_l0"]).then_inc(S("ld_l0"), 16)
            sp.dma_start(gw[:], A["gw"]).then_inc(S("ld_small"), 16)
            sp.dma_start(rbias[:], A["rbias"].to_broadcast([P, RBW])).then_inc(S("ld_small"), 16)
            sp.dma_start(b2[:], A["b2"][0]).then_inc(S("ld_b2"), 16)
            for i in range(4):
                sp.dma_start(W[:, 4096 + 2048 * i:6144 + 2048 * i], A["w_a0"][:, i]).then_inc(S(f"ld_a0_{i}"), 16)
            sp.dma_start(W[:, 12288:16384].rearrange("p (e n) -> p e n", e=4),
                         A["w_m0"][0:4].rearrange("e p n -> p e n")).then_inc(S("ld_m0a"), 16)
            sp.wait_ge(S("h_full"), 8)
            sp.dma_start(W[:, 0:4096].rearrange("p (e n) -> p e n", e=4),
                         A["w_m0"][4:8].rearrange("e p n -> p e n")).then_inc(S("ld_m0b"), 16)
            sp.wait_ge(S("kvq_full"), 15)
            sp.wait_ge(S("wo0_full"), 8)
            sp.dma_start(rvec[:, 0:2], A["rvec1"].rearrange("a k d -> a k d").to_broadcast([P, 2, D])).then_inc(S("ld_rvec"), 16)
            sp.wait_ge(S("mo_out"), 5)
            sp.dma_start(b2[:], A["b2"][1]).then_inc(S("ld_b2"), 16)
            with_layers(sp)
            sp.wait_ge(S("g_q_full"), 8 * LAYERS)
            sp.dma_start(W[:, 0:3072], A["w_l2"]).then_inc(S("ld_l23"), 16)
            sp.dma_start(W[:, 3072:5120], A["w_l3"]).then_inc(S("ld_l23"), 16)
            sp.wait_ge(S("lf_vec"), 12 + T)
            sp.dma_start(rvec[:], A["rvec2"].to_broadcast([P, 4, D])).then_inc(S("ld_rvec"), 16)
            blocks(sp, 1, A["w_m1"])
            sp.wait_ge(S(f"gathered{T - 1}"), 32)
            sp.dma_start(W[:, 8192:16384].rearrange("p (e n) -> p e n", e=8),
                         A["w_m2"].rearrange("e p n -> p e n")).then_inc(S("ld_m2"), 16)
            sp.dma_start(b2[:], A["b2"][2]).then_inc(S("ld_b2"), 16)
            blocks(sp, 3, A["w_m3"])
            for t in range(T):
                sp.wait_ge(S("add"), 2 * T + 2 * t + 2)
                sp.dma_start(out[:, t], X[:, t]).then_inc(S("stored"), 16)
            sp.wait_ge(S("stored"), 16 * T)

        @block.gpsimd
        def _(pool):
            pool.memset(fill, 0.0).then_inc(S("fill"), 1)
            c = Chain(pool, S("consts"))
            c(pool.iota(iota16[:, 0:N], [[1, N]], base=0, channel_multiplier=0, allow_small_or_imprecise_dtypes=True))
            c(pool.memset(ident[:], 0.0))
            c(pool.memset(ones[:], 1.0))
            c(pool.memset(TRI[:], 1.0))
            c(pool.memset(LT[:], 1.0))
            c(pool.iota(THR[:], [[0, E], [P, PER]], base=0, channel_multiplier=0, allow_small_or_imprecise_dtypes=True))
            c(pool.iota(iota_b[:], [[1, BLOCKS]], base=0, channel_multiplier=0, allow_small_or_imprecise_dtypes=True))
            c(pool.memset(half8[:], -0.5))
            c(pool.memset(SELf, 0.0))
            c(pool.memset(CM, 0.0))
            c(pool.iota(iota8[:], [[1, E]], base=0, channel_multiplier=0, allow_small_or_imprecise_dtypes=True))
            c.sync()
            c(pool.affine_select(out=ident[:], in_=ident[:], compare_op=ALU.not_equal, fill=1.0,
                                 base=0, pattern=[[-1, P]], channel_multiplier=1))
            c(pool.affine_select(out=SELf, in_=SELf, compare_op=ALU.not_equal, fill=1.0,
                                 base=0, pattern=[[-1, E], [0, P]], channel_multiplier=1))
            c(pool.affine_select(out=CM[:, N - R:N], in_=CM[:, N - R:N], compare_op=ALU.is_ge, fill=NEG,
                                 base=0, pattern=[[-1, R]], channel_multiplier=1))
            c(pool.affine_select(out=TRI[:], in_=TRI[:], compare_op=ALU.is_gt, fill=0.0,
                                 base=0, pattern=[[1, R]], channel_multiplier=-1))
            c(pool.affine_select(out=LT[:], in_=LT[:], compare_op=ALU.is_gt, fill=0.0,
                                 base=0, pattern=[[1, E], [-1, E]], channel_multiplier=0))
            c.sync()
            c(pool.tensor_copy(SEL[:], SELf))
            assert c.n == CONSTS

            def power(dst, src, k, ready, count):
                pool.wait_ge(ready, count)
                pool.tensor_tensor(dst, src, half8[0:src.shape[0], :].broadcast_to([src.shape[0], k]), ALU.pow).then_inc(S("pow"), 1)

            def ln(k):
                power(rstd3[:] if k == 2 else rstd[0:R, :], ve[0:R, :], T, S("ln_vec"), LN[k] + 11 if k != 2 else LN[1] + 14)

            def scatter(r):
                pool.wait_ge(S("ln_vec"), LN[4 if r == 1 else 8] + 16)
                pool.wait_ge(S("sl_vec"), SLOT_OPS * (r // 2) + 9)
                pool.wait_ge(S("filled"), 16)
                for k in range(2):
                    for t in range(T):
                        pool.indirect_dma_start(out=XS, out_offset=bass.IndirectOffsetOnAxis(ap=slu[:, k, t:t + 1], axis=0),
                                                in_=XN[:, t], in_offset=None).then_inc(S("sc"), 16)
                with pool.Fori(0, BLOCKS) as b:
                    for p in STREAMS[r][BY_POOL[r]]:
                        low(pool, r, p, b, part(PLACE[r][p]))
                pool.wait_ge(S("st"), 16 * (B0[r] + BLOCKS))
                for t in range(T):
                    for k in range(2):
                        pool.indirect_dma_start(out=G[k][:, t], out_offset=None, in_=YS,
                                                in_offset=bass.IndirectOffsetOnAxis(ap=slu[:, k, t:t + 1], axis=0)).then_inc(S(f"gathered{t}"), 16)

            ln(0)
            power(dinvr[:], degr[:], T, S("deg_vec"), 5)
            power(rstd[:, 0:C], ve[:, 0:C], C, S("bn_vec"), 13)
            ln(1)
            ln(2)
            for t in range(T):
                pool.wait_ge(S("msk_act"), 2 * T)
                pool.tensor_scalar(MASK[:, t], MASK[:, t], 0.0, NEG, ALU.is_equal, ALU.mult).then_inc(S("msk_done"), 1)
            for i in range(2):
                power(ssr[:, i], ss[:, i], T * H, S("qk_vec"), 11 * (i + 1))
            ln(3)
            pool.wait_ge(S("ln_vec"), LN[3] + 16)
            pool.wait_ge(S("ld_rvec"), 16)
            for t in range(T):
                pool.tensor_tensor(X[:, t], X[:, t], rvec[0:R, 1], ALU.add).then_inc(S("lf_beta"), 1)
            with pool.Fori(0, LAYERS) as layer:
                for b in range(2):
                    power(rstd[:, 0:C], ve[:, 0:C], C, S("bn_vec"), layer * 34 + (16 + 17 * b + 14))
            power(rstd[0:R, :], ve[0:R, :], T, S("lf_vec"), 11)
            ln(4)
            scatter(1)
            ln(5)
            for t in range(T):
                c = Chain(pool, S("l2_half"), 3 * t)
                if t == 0:
                    pool.wait_ge(S("l2_vec"), 2 + T)
                if t >= 2:
                    pool.wait_ge(S("l2_vec"), L2_TILE0 + L2_TILE * (t - 1))
                for b in (2, 3):
                    c(basis(pool, PV[:, t % 2, b - 2], t, b))
                c.sync()
                c(pool.tensor_tensor(PV[:, t % 2, 0], PV[:, t % 2, 0], PV[:, t % 2, 1], ALU.add))
            power(rstd[0:R, :], ve[0:R, :], T, S("l2_vec"), L2_OPS + 11)
            ln(6)
            ln(7)
            power(rstd[:, 0:C], ve[:, 0:C], C, S("bn_vec"), LAST_BN + 13)
            ln(8)
            scatter(3)

        @block.tensor
        def _(pe):
            def to_feats(src, full, ready=None, base=0, every=0, behind=None):
                for t in range(T):
                    if ready is not None:
                        pe.wait_ge(ready, base + every * (t + 1))
                    for c in range(C):
                        mm = pe.transpose(bank[:, t, c * R:(c + 1) * R], src[:, t, c * P:(c + 1) * P], ident[0:R, 0:R])
                    mm.then_inc(full, 1)
                    if behind is not None and t >= 2:
                        behind(t - 2)
                if behind is not None:
                    behind(T - 2)
                    behind(T - 1)

            def ln_to_feats(k, behind=None):
                to_feats(XN, S("tr_full"), S("ln_vec"), LN[k] + 11 if k != 2 else LN[1] + 15, 1, behind)

            def routed_feats(k, u, r):
                def logits(t):
                    pe.wait_ge(S("tr_a" if t % 2 else "tr_v"), (2 if t % 2 else 3) * u + t // 2 + 1)
                    gate(r, XT, t)
                ln_to_feats(k, logits)

            def feats_ready(k):
                pe.wait_ge(S("tr_v"), 3 * (k + 1))
                pe.wait_ge(S("tr_a"), 2 * (k + 1))

            def to_rows(src, full, ready=None, base=0):
                for t in range(T):
                    for c in range(C):
                        if t == 0 and ready is not None:
                            pe.wait_ge(ready, base + c + 1)
                        mm = pe.transpose(bank[0:R, t, c * P:(c + 1) * P], src[:, c, t * R:(t + 1) * R], ident[:])
                    mm.then_inc(full, 1)

            def project(pairs, full, before=None, base=0):
                for j, (m, lo, hi) in enumerate(GROUPS):
                    if before is not None:
                        pe.wait_ge(before, base + j + 1)
                    steps = [(w, x, c) for w, x in pairs for c in range(x.shape[1])]
                    for n, (w, x, c) in enumerate(steps):
                        mm = pe.matmul(bank[:, j, 0:hi - lo], w[:, c, m * P:(m + 1) * P], x[:, c, lo:hi],
                                       start=(n == 0), stop=(n == len(steps) - 1))
                    mm.then_inc(full, 1)

            def row_group(b, x, t, w, full, cols=D, last=True):
                for c in range(C):
                    mm = pe.matmul(bank[0:R, b, 0:cols], x[:, c, t * R:(t + 1) * R], w[:, c, 0:cols],
                                   start=(c == 0), stop=(last and c == C - 1))
                if full is not None:
                    mm.then_inc(full, 1)

            def scores(s, causal):
                t, h, kn = step(s, causal)
                hp = slice((h % 2) * DH, (h % 2) * DH + DH)
                for lo, hi in ((0, min(kn, 512)), (512, kn)):
                    if lo < hi:
                        mm = pe.matmul(bank[0:R, 2 * (s % 2) + lo // 512, 0:hi - lo],
                                       QT[hp, h // 2, t * R:(t + 1) * R], KT[hp, h // 2, lo:hi], start=True, stop=True)
                mm.then_inc(S("at_s"), 1)

            def attention(base, causal):
                for s in range(ATT + 2):
                    if 2 <= s < ATT:
                        pe.wait_ge(S("at_mask"), base(ATT) + s - 1)
                        scores(s, causal)
                    if 1 <= s <= ATT:
                        u = s - 1
                        kn = step(u, causal)[2]
                        pe.wait_ge(S("at_exp"), base(ATT) + u + 1)
                        if u >= 1:
                            pe.wait_ge(S("at_pt"), base(ATT) + u)
                        for kb in range(kn // R):
                            mm = pe.transpose(bank[0:R, 4 + kb // 4, (kb % 4) * P:(kb % 4) * P + R],
                                              SM[:, u % 2, kb * R:(kb + 1) * R], ident[0:R, 0:R])
                        mm.then_inc(S("at_tr"), 1)
                    if s >= 2:
                        u = s - 2
                        t, h, kn = step(u, causal)
                        pe.wait_ge(S("at_pt"), base(ATT) + u + 1)
                        if h == 0 and u >= H:
                            pe.wait_ge(S("at_norm"), base(3 * T) + 3 * (u // H))
                        last = kn // R - 1
                        for kb in range(last + 1):
                            mm = pe.matmul(bank[0:R, 6 + h // 4, (h % 4) * (DH + 1):(h % 4 + 1) * (DH + 1)],
                                           PT[:, u % 2, kb, :], V[:, kb, h, :], start=(kb == 0), stop=(kb == last))
                        mm.then_inc(S("at_av"), 1)

            def gate(r, xt, t):
                for c in range(C):
                    mm = pe.matmul(bank[0:R, 7, t * E:(t + 1) * E], xt[:, c, t * R:(t + 1) * R],
                                   gw[:, c, GW[r]:GW[r] + E], start=(c == 0), stop=(c == C - 1))
                if t == T - 1:
                    mm.then_inc(S("rt_pe"), 1)

            def router(r):
                pe.wait_ge(S("rt_vec"), ROUTED[r] + ROUTER_OPS[r])
                for t in range(T):
                    mm = pe.transpose(bank[0:E, 1 + t // 4, (t % 4) * R:(t % 4 + 1) * R], COMB[:, t], ident[0:R, 0:R])
                mm.then_inc(S("rt_pe"), 1)
                pe.wait_ge(S("rt_act"), RT_ACT[r] + 5)
                pe.wait_ge(S("comb_low"), r + 2)
                for e in range(E):
                    for i, (lo, hi) in enumerate(HALVES):
                        g = 2 * e + i
                        if g >= 5:
                            pe.wait_ge(S("rt_cb"), 2 * E * (r // 2) + g - 4)
                        n = hi - lo + (hi - lo) % 2
                        pe.matmul(bank[:, 3 + g % 5, 0:n], SEL[:, e], combH[:, lo:lo + n], start=True, stop=False)
                        pe.matmul(bank[:, 3 + g % 5, 0:n], SEL[:, e], combL[:, lo:lo + n],
                                  start=False, stop=True).then_inc(S("rt_spread"), 1)

            def mixture(r, xt, slots):
                pe.wait_ge(S("rt_cb"), 2 * E * (r // 2 + 1))
                pe.wait_ge(S("ld_b2"), 16 * (r + 1))
                for t in range(T):
                    pe.matmul(bank[0:R, t, :], combT[:, t * R:(t + 1) * R], b2[:], start=True, stop=False, skip_group_check=True)

                def first(u):
                    e, i = divmod(u, 2)
                    lo, hi = HALVES[i]
                    w = W[:, slots[e]:slots[e] + D].rearrange("p (c n) -> p c n", c=C)
                    if i == 0:
                        pe.wait_ge(S("ld_m2" if r == 2 else "ld_m0a" if e < 4 else "ld_m0b"), 16)
                    for c in range(C):
                        mm = pe.matmul(bank[:, 5 + u % 3, 0:hi - lo], w[:, c], xt[:, c, lo:hi], start=(c == 0), stop=(c == C - 1))
                    mm.then_inc(S("mo_h"), 1)

                def second(u):
                    e, i = divmod(u, 2)
                    at = slots[e] + D
                    pe.wait_ge(S("mo_hs"), UB[r] + u + 1)
                    for t in range(3 * i, 3 + 2 * i):
                        k = t - 3 * i
                        mm = pe.matmul(bank[0:R, t, :], hs[:, u % 2, k * R:(k + 1) * R], W[:, at:at + D],
                                       start=False, stop=(e == E - 1), skip_group_check=True)
                    mm.then_inc(S("mo_used"), 1)

                for u in range(UNITS + 1):
                    if u < UNITS:
                        first(u)
                    if u >= 1:
                        second(u - 1)

            def slots(r):
                pe.wait_ge(S("rt_vec"), ROUTED[r] + ROUTER_OPS[r])
                def sums(rows, at, w, a, b, start=False, stop=False):
                    return pe.matmul(bank[rows, 0, at:at + (b - a) * E], w, MK[:, a:b].rearrange("p t e -> p (t e)"),
                                     start=start, stop=stop, skip_group_check=True)

                all_r, all_p = slice(0, R), slice(0, P)
                sums(all_r, 64, TRI[:], 0, T, start=True)
                for d in range(1, T):
                    sums(all_r, 64 + d * E, ones[0:R, 0:R], 0, T - d, stop=(d == T - 1))
                mm = sums(all_p, 128, ones[0:R, :], 0, T, start=True, stop=True)
                mm.then_inc(S("sl_pe"), 1)

            def second_biases():
                for t in range(T):
                    mm = pe.transpose(bank[0:E, 1 + t // 4, (t % 4) * R:(t % 4 + 1) * R], COMB[:, t], ident[0:R, 0:R])
                mm.then_inc(S("rt_pe"), 1)
                pe.wait_ge(S("rt_act"), RT_ACT[1] + 3)
                pe.wait_ge(S("ld_b2"), 32)
                for t in range(T):
                    pe.matmul(bank[0:R, 3 + t, :], combT[:, t * R:(t + 1) * R], b2[:], start=True, stop=True).then_inc(S("b2_full"), 1)

            def block_loop(r):
                n = CH[r]

                def product(p, b, dst, high, low, opens, closes):
                    for h in range(2):
                        w_hi, w_lo = (x.rearrange("p (k n) -> p k n", k=2) for x in half(r, p, h))
                        pe.wait_ge(*split(r, p, h, b, "hi"))
                        for k in range(2):
                            pe.matmul(dst, high[2 * h + k], w_hi[:, k], start=(opens and h == 0 and k == 0), stop=False)
                            pe.matmul(dst, low[2 * h + k], w_hi[:, k], start=False, stop=False)
                        pe.wait_ge(*split(r, p, h, b, "lo"))
                        for k in range(2):
                            mm = pe.matmul(dst, high[2 * h + k], w_lo[:, k], start=False, stop=(closes and h == 1 and k == 1))
                        mm.then_inc(split(r, p, h, b, "used")[0], 1)

                def first(name, j, b):
                    c = b * n + j
                    if (name, j) == ("a", 0):
                        pe.wait_ge(S("b_xbt"), b + (B0[r] + 1))
                        pe.wait_ge(S("b_xbl"), b + (B0[r] + 1))
                    before = c if j == 0 and n % 2 else c - 1
                    if not (isinstance(before, int) and before <= 0):
                        if (r, name) == (3, "a"):
                            pe.wait_ge(S("b3_s"), before)
                        else:
                            pe.wait_ge(S("b_h"), before + C0[r])
                    bank0 = 0 if name == "a" else 2
                    product((name, j), b, bank[:, bank0 + j % 2, :], [xbh[:, k] for k in range(C)], [xbl[:, k] for k in range(C)], True, True)

                def turn(j, b):
                    pe.wait_ge(S("b_h"), b * n + (C0[r] + j + 1))
                    for i in range(4):
                        mm = pe.transpose(bank[:, 4 + j % 2, i * P:(i + 1) * P], hrow[:, j % 2, i * P:(i + 1) * P], ident[:])
                    mm.then_inc(S("b_tr"), 1)

                def second(j, b):
                    if j == 0 and not isinstance(b, int):
                        pe.wait_ge(S("st_y"), b + B0[r])
                    pe.wait_ge(S("b_ht"), b * n + (C0[r] + j + 1))
                    pe.wait_ge(S("b_hl"), b * n + (C0[r] + j + 1))
                    product(("y", j), b, bank[:, 7, :], [hTh[:, j % 2, i * P:(i + 1) * P] for i in range(4)],
                            [hTl[:, j % 2, i * P:(i + 1) * P] for i in range(4)], j == 0, j == n - 1)

                def nodes(b):
                    pe.wait_ge(S("ld_xb"), b * 16 + (16 * X0[r] + 16))
                    for k in range(C):
                        mm = pe.transpose(bank[:, 6, k * P:(k + 1) * P], xblk[:, k * P:(k + 1) * P], ident[:])
                    mm.then_inc(S("b_xt"), 1)

                def body1(b, before):
                    first("a", 0, b)
                    if before is not None:
                        turn(1, before)
                    first("a", 1, b)
                    turn(0, b)
                    if before is not None:
                        second(1, before)
                    nodes(b + 1)
                    second(0, b)

                def body3(b, before):
                    first("a", 0, b)
                    if before is not None:
                        turn(2, before)
                    first("g", 0, b)
                    if before is not None:
                        second(2, before)
                    for j in (1, 2):
                        first("a", j, b)
                        turn(j - 1, b)
                        first("g", j, b)
                        if j == 2:
                            nodes(b + 1)
                        second(j - 1, b)

                body = body1 if r == 1 else body3
                nodes(0)
                body(0, None)
                with pe.Fori(1, BLOCKS) as b:
                    body(b, b - 1)
                turn(n - 1, BLOCKS - 1)
                second(n - 1, BLOCKS - 1)

            def edge_tile(s, ready, first, last=False):
                pe.wait_ge(S("oh_ready"), ready)
                for k in range(T):
                    pe.matmul(bank[0:R, k, :], OH[:, s, 0, k * R:(k + 1) * R], OH[:, s, 1, 0:512],
                              start=first, stop=last, skip_group_check=True)
                for k in range(T):
                    mm = pe.matmul(bank[0:R, 5 + k // 4, (k % 4) * (N - 512):(k % 4 + 1) * (N - 512)],
                                   OH[:, s, 0, k * R:(k + 1) * R], OH[:, s, 1, 512:N],
                                   start=first and k % 4 == 0, stop=last, skip_group_check=True)
                mm.then_inc(S("oh_used"), 1)

            for s in range(4):
                edge_tile(s, 2 * s + 2, s == 0)
            with pe.Fori(1, ET // 4 - 1) as i:
                for s in range(4):
                    edge_tile(s, i * 8 + 2 * s + 2, False)
            for s in range(4):
                edge_tile(s, 2 * (ET - 4 + s) + 2, False, s == 3)
            pe.wait_ge(S("consts"), CONSTS)
            pe.wait_ge(S("cnt_a"), 5)
            pe.wait_ge(S("cnt_v"), 2)
            for i, (lo, hi) in enumerate(HALVES):
                for k in range(T):
                    mm = pe.matmul(bank[:, 5 + i, 0:hi - lo], ones[0:R, :], AT[:, k, lo:hi], start=(k == 0), stop=(k == T - 1))
                mm.then_inc(S("deg_pe"), 1)
            for t in range(T):
                for k in range(T):
                    mm = pe.matmul(bank[0:R, 7, t:t + 1], AT[:, k, t * R:(t + 1) * R], ones[0:R, 0:1], start=(k == 0), stop=(k == T - 1))
            mm.then_inc(S("deg_pe"), 1)
            ln_to_feats(0)
            pe.wait_ge(S("deg_vec"), 10)
            for i, tiles in enumerate(((0, 1, 2), (3, 4))):
                for k, t in enumerate(tiles):
                    mm = pe.matmul(bank[:, 5 + i, k * R:(k + 1) * R], ones[0:R, :], diag[:, t, :], start=True, stop=True)
                mm.then_inc(S("deg_pe"), 1)
            feats_ready(0)
            pe.wait_ge(S("deg_vec"), 12)
            for j, (m, lo, hi) in enumerate(GROUPS):
                for k in range(T):
                    mm = pe.matmul(bank[:, j, 0:hi - lo], XN[:, k, m * P:(m + 1) * P], AT[:, k, lo:hi], start=(k == 0), stop=(k == T - 1))
                mm.then_inc(S("agg_full"), 1)
            pe.wait_ge(S("ld_l0"), 16)
            pe.wait_ge(S("agg_done"), 8)
            project([(Wl, MT), (Wr, XT[:])], S("h_full"))
            to_rows(HB, S("rows_full"), S("bn_out"), 0)

            pe.wait_ge(S("rows_vec"), 2 * T)
            for t in range(T):
                for k in range(T):
                    mm = pe.transpose(bank[0:R, t, k * P:k * P + R] if k < 4 else bank[0:R, 5 + t // 4, t % 4 * P:t % 4 * P + R],
                                      AT[:, k, t * R:(t + 1) * R], ident[0:R, 0:R])
                mm.then_inc(S("msk_pe"), 1)

            pe.wait_ge(S("msk_act"), 2 * T)
            ln_to_feats(2)
            pe.wait_ge(S("aff_done"), 4)
            for g in range(2 * T + 3):
                i, t = divmod(g, T)
                if t == 0:
                    pe.wait_ge(S(f"ld_a0_{i}"), 16)
                if g >= 8:
                    pe.wait_ge(S("kvq_done"), g - 7)
                row_group(g % 8, XT, t, (Wq, Wk, Wv)[i], S("kvq_full"))
            pe.wait_ge(S("kvq_done"), 2 * T + 3)
            pe.wait_ge(S("qk_vec"), 27)
            to_feats(QR, S("tr_full"))
            feats_ready(2)
            pe.wait_ge(S("qk_vec"), 32)
            to_feats(KR, S("tr_full"))
            feats_ready(3)
            scores(0, True)
            scores(1, True)
            for t in (3, 4):
                row_group(2 + t, XT, t, Wv, S("kvq_full"))
            pe.wait_ge(S("kvq_done"), 3 * T)
            attention(lambda k: 0, True)
            pe.wait_ge(S("at_norm"), 3 * T)
            to_feats(OR, S("tr_full"))
            feats_ready(4)
            pe.wait_ge(S("ld_a0_3"), 16)
            project([(Wo, OT)], S("wo0_full"))
            pe.wait_ge(S("wo0_done"), 8)
            pe.wait_ge(S("ld_small"), 48)
            for t in range(T):
                gate(0, YT, t)
            router(0)
            mixture(0, YT, M0)

            ln_to_feats(3)
            feats_ready(5)
            with pe.Fori(0, LAYERS) as layer:
                pe.wait_ge(S("ld_g0"), layer * 16 + 16)
                project([(Wq, XT[:])], S("g_q_full"))
                pe.wait_ge(S("ld_g1"), layer * 16 + 16)
                project([(Wk, XT[:])], S("g_k_full"), S("g_q_done"), layer * 8)
                pe.wait_ge(S("ld_g2"), layer * 16 + 16)
                for t in range(4):
                    pe.wait_ge(S("g_k_done"), layer * 8 + t + 5)
                    row_group(4 + t, XT, t, Wv, S("g_v_full"))
                scores(0, False)
                scores(1, False)
                pe.wait_ge(S("g_v_done"), layer * 5 + 1)
                row_group(4, XT, 4, Wv, S("g_v_full"))
                pe.wait_ge(S("g_v_done"), layer * 5 + 5)
                attention(lambda k: layer * k + k, False)
                to_feats(OR, S("g_tr_full"), S("at_norm"), layer * (3 * T) + 3 * T, 3)
                pe.wait_ge(S("g_tr_v"), layer * 3 + 3)
                pe.wait_ge(S("g_tr_a"), layer * 2 + 2)
                pe.wait_ge(S("ld_g3"), layer * 16 + 16)
                project([(Wo, OT)], S("g_wo_full"))
                pe.wait_ge(S("ld_gf"), layer * 16 + 16)
                for i, (lo, hi) in enumerate(HALVES):
                    for c in range(C):
                        if i == 0:
                            pe.wait_ge(S("g_x1v" if c % 2 else "g_x1"), layer * 2 + (c // 2 + 1))
                        mm = pe.matmul(bank[:, i, 0:hi - lo], Wf1[:, c], X1T[:, c, lo:hi], start=(c == 0), stop=(c == C - 1))
                    mm.then_inc(S("g_f1_full"), 1)
                pe.wait_ge(S("g_f1_done"), layer * 2 + 2)
                for j, (m, lo, hi) in enumerate(GROUPS):
                    pe.matmul(bank[:, j, 0:hi - lo], Wf2[:, m * P:(m + 1) * P], RT[:, lo:hi],
                              start=True, stop=True).then_inc(S("g_w2_full"), 1)
                pe.wait_ge(S("g_x2"), layer * 2 + 2)
                pe.wait_ge(S("g_x2v"), layer * 2 + 2)
            to_rows(XT, S("rows_full"))

            routed_feats(4, 6, 1)
            feats_ready(6)
            slots(1)
            second_biases()
            pe.wait_ge(S("b2_done"), 5)
            block_loop(1)

            ln_to_feats(5)
            feats_ready(7)
            pe.wait_ge(S("ld_l23"), 32)
            for t in range(T):
                row_group(t, XT, t, Wb, None, BASES)
                for c in range(C):
                    mm = pe.matmul(bank[0:R, 5, t * 32:(t + 1) * 32], XT[:, c, t * R:(t + 1) * R],
                                   gw[:, c, GW["comb"]:GW["comb"] + 32], start=(c == 0), stop=(c == C - 1))
                mm.then_inc(S("bs_full"), 1)
            pe.wait_ge(S("bs_done"), 5)
            pe.wait_ge(S("self_loops"), 5)
            for t in range(T):
                b = (6, 7, 0, 1, 2)[t]
                for k in range(T):
                    mm = pe.matmul(bank[0:R, b, 0:BASES], AT[:, k, t * R:(t + 1) * R], BS[:, k], start=(k == 0), stop=(k == T - 1))
                mm.then_inc(S("ag_full"), 1)
            for t in range(T):
                b = (3, 4, 5, 6, 7)[t]
                if b >= 5:
                    pe.wait_ge(S("l2_vec"), 4)
                row_group(b, XT, t, Wres, None, last=False)
                if t == 0:
                    pe.wait_ge(S("l2_vec"), 1)
                pe.matmul(bank[0:R, b, :], ones[0:1, 0:R], rvec[0:1, 0, :], start=False, stop=True).then_inc(S("res_full"), 1)

            routed_feats(6, 8, 2)
            feats_ready(8)
            router(2)
            mixture(2, XT, M2)

            pe.wait_ge(S("mo_out"), 10)
            ln_to_feats(7)
            feats_ready(9)
            pe.wait_ge(S("ld_l23"), 32)
            for t in range(T):
                row_group(t, XT, t, W3, S("xw_full"))
            pe.wait_ge(S("xw_done"), 5)
            for j, (m, lo, hi) in enumerate(GROUPS):
                for k in range(T):
                    mm = pe.matmul(bank[:, j, 0:hi - lo], XW[:, k, m * P:(m + 1) * P], AT[:, k, lo:hi], start=(k == 0), stop=(k == T - 1))
                mm.then_inc(S("h_full"), 1)
            to_rows(HB, S("rows_full"), S("bn_out"), 4)

            routed_feats(8, 10, 3)
            feats_ready(10)
            slots(3)
            block_loop(3)

        @block.scalar
        def _(act):
            def copy_feats(dst, full, done, fbase, dbase, scale=None):
                for t in (1, 3):
                    act.wait_ge(full, fbase + t + 1)
                    act.activation(dst[:, :, t * R:(t + 1) * R], bank[:, t, 0:C * R].rearrange("p (c n) -> p c n", c=C),
                                   ACT.Copy, scale=1.0 if scale is None else scale).then_inc(done, 1)

            def feats(k, dst, scale=None):
                copy_feats(dst, S("tr_full"), S("tr_a"), T * k, 2 * k, scale)

            def bn_apply(src, dst, func, ready, count, done, chunks=range(C)):
                act.wait_ge(ready, count)
                for m in chunks:
                    act.activation(dst[:, m], src[:, m], func, scale=bsc[:, m:m + 1], bias=bsh[:, m:m + 1]).then_inc(done, 1)

            def exps(base, causal):
                for s in range(ATT + (2 if causal else 0)):
                    if s < ATT:
                        kn = step(s, causal)[2]
                        act.wait_ge(S("at_mask"), base(ATT) + s + 1)
                        act.activation(SM[:, s % 2, 0:kn], SM[:, s % 2, 0:kn], ACT.Exp, scale=-1.0,
                                       bias=nmx[:, s:s + 1]).then_inc(S("at_exp"), 1)
                    if causal and s >= 1 and s <= ATT:
                        u = s - 1
                        act.wait_ge(S("at_tr"), u + 1)
                        if u >= 2:
                            act.wait_ge(S("at_av"), u - 1)
                        nb = step(u, causal)[2] // R
                        n4 = min(nb, 4)
                        ins = act.activation(PT[:, u % 2, 0:n4, :],
                                             bank[0:R, 4, :].rearrange("p (k n) -> p k n", k=4)[:, 0:n4, 0:R], ACT.Copy)
                        if nb > 4:
                            ins = act.activation(PT[:, u % 2, 4, :], bank[0:R, 5, 0:R], ACT.Copy)
                        ins.then_inc(S("at_pt"), 1)

            def router(r):
                act.wait_ge(S("rt_vec"), ROUTED[r] + 3)
                act.activation(EX[:], LG[:], ACT.Exp).then_inc(S("rt_act"), 1)
                if r == 3:
                    return
                act.wait_ge(S("rt_pe"), 2 * r + 2)
                act.activation(combT[:, 0:500], bank[0:E, 1, 0:500], ACT.Copy).then_inc(S("rt_act"), 1)
                act.activation(combT[:, 500:N], bank[0:E, 2, 0:R], ACT.Copy).then_inc(S("rt_act"), 1)
                if r == 1:
                    return
                act.activation(combH[:, 0:500], bank[0:E, 1, 0:500], ACT.Copy).then_inc(S("rt_act"), 1)
                act.activation(combH[:, 500:N], bank[0:E, 2, 0:R], ACT.Copy).then_inc(S("rt_act"), 1)
                for e in range(E):
                    for i, (lo, hi) in enumerate(HALVES):
                        g = 2 * e + i
                        act.wait_ge(S("rt_spread"), 2 * E * (r // 2) + g + 1)
                        act.activation(CB[:, e, lo:hi], bank[:, 3 + g % 5, 0:hi - lo], ACT.Copy).then_inc(S("rt_cb"), 1)

            def mixture(r, bcol):
                for u in range(UNITS):
                    lo, hi = HALVES[u % 2]
                    act.wait_ge(S("mo_h"), UB[r] + u + 1)
                    if u >= 2:
                        act.wait_ge(S("mo_used"), UB[r] + u - 1)
                    act.activation(hg[:, u % 2, 0:hi - lo], bank[:, 5 + u % 3, 0:hi - lo], ACT.Gelu_apprx_tanh,
                                   bias=fvec[:, bcol + u // 2:bcol + u // 2 + 1]).then_inc(S("mo_act"), 1)

            def block_loop(r):
                n = CH[r]

                def high(p, b):
                    if p == ("y", 0) and isinstance(b, int):
                        act.wait_ge(S("sc"), 16 * 2 * T * (r // 2 + 1))
                    for h in range(2):
                        if h == 0:
                            act.wait_ge(S(f"ld{r}_{p[0]}{p[1]}"), b * 16 + 16)
                        before = nth(r, p, h, b) - SLOTS[r][WHERE[r][p][0]]
                        if not (isinstance(before, int) and before <= 0):
                            act.wait_ge(split(r, p, h, b, "used")[0], before)
                        act.activation(half(r, p, h)[0], part(PLACE[r][p])[:, HALF * h:HALF * (h + 1)],
                                       ACT.Copy).then_inc(split(r, p, h, b, "hi")[0], 1)

                def nodes(b):
                    act.wait_ge(S("b_xt"), b + (X0[r] + 1))
                    if not (isinstance(b, int) and b == 0):
                        act.wait_ge(*used(r, STREAMS[r]["a"][-1], b - 1))
                    act.activation(xbh.rearrange("p c n -> p (c n)"), bank[:, 6, :], ACT.Copy).then_inc(S("b_xbt"), 1)

                def silu(j, b):
                    c = b * n + j
                    act.wait_ge(*used(3, ("a", j), b))
                    before = c if j == 0 else c - 1
                    if not (isinstance(before, int) and before <= 0):
                        act.wait_ge(S("b_h"), before + C0[3])
                    act.activation(act_s[:, j % 2], bank[:, j % 2, :], ACT.Silu).then_inc(S("b3_s"), 1)

                def hidden(j, b):
                    c = b * n + j
                    act.wait_ge(S("b_tr"), c + (C0[r] + 1))
                    src = bank[:, 4 + j % 2, :]
                    if r == 1:
                        act.wait_ge(S("m1b"), b + 1)
                        for i in range(4):
                            act.activation(act_s[:, j % 2, i * P:(i + 1) * P], src[:, i * P:(i + 1) * P], ACT.Relu,
                                           bias=m1b[:, 4 * j + i:4 * j + i + 1]).then_inc(S("b1_relu"), 1)
                        act.wait_ge(S("b1_relu"), c * 4 + 4)
                        src = act_s[:, j % 2]
                    act.activation(hTh[:, j % 2], src, ACT.Copy).then_inc(S("b_ht"), 1)

                def output(b):
                    act.wait_ge(*used(r, ("y", n - 1), b))
                    if not (isinstance(b, int) and b == 0):
                        act.wait_ge(S("st"), b * 16 + 16 * B0[r])
                    act.activation(yblk, bank[:, 7, :], ACT.Copy).then_inc(S("st_y"), 1)
                    act.wait_ge(S("st_y"), b + (B0[r] + 1))
                    act.dma_start(YS[b * P:(b + 1) * P] if isinstance(b, int) else YS[bass.ds(b * P, P)], yblk).then_inc(S("st"), 16)

                def body1(b, before):
                    nodes(b)
                    high(("a", 0), b)
                    high(("a", 1), b)
                    if before is not None:
                        hidden(1, before)
                    high(("y", 0), b)
                    hidden(0, b)
                    if before is not None:
                        output(before)
                    high(("y", 1), b)

                def body3(b, before):
                    high(("a", 0), b)
                    if before is not None:
                        silu(2, before)
                    nodes(b)
                    high(("g", 0), b)
                    if before is not None:
                        high(("y", 2), before)
                        hidden(2, before)
                    high(("a", 1), b)
                    silu(0, b)
                    high(("g", 1), b)
                    high(("y", 0), b)
                    if before is not None:
                        output(before)
                    hidden(0, b)
                    high(("a", 2), b)
                    silu(1, b)
                    high(("g", 2), b)
                    high(("y", 1), b)
                    hidden(1, b)

                body = body1 if r == 1 else body3
                body(0, None)
                with act.Fori(1, BLOCKS) as b:
                    body(b, b - 1)
                if r == 3:
                    silu(2, BLOCKS - 1)
                    high(("y", 2), BLOCKS - 1)
                hidden(n - 1, BLOCKS - 1)
                output(BLOCKS - 1)

            act.wait_ge(S("oh_used"), ET)
            for k in range(T):
                act.activation(AT[:, k, 0:512], bank[0:R, k, :], ACT.Copy).then_inc(S("cnt_a"), 1)
            feats(0, XT)
            act.wait_ge(S("ld_small"), 48)
            for j, (m, lo, hi) in enumerate(GROUPS):
                act.wait_ge(S("h_full"), j + 1)
                act.activation(HB[:, m, lo:hi], bank[:, j, 0:hi - lo], ACT.Identity,
                               bias=fvec[:, FV["l0_b"] + m:FV["l0_b"] + m + 1]).then_inc(S("h_done"), 1)
            bn_apply(HB, HB, ACT.Relu, S("bn_vec"), 16, S("bn_out"))

            for t in range(T):
                act.wait_ge(S("msk_pe"), T)
                act.activation(MASK[:, t, 0:4 * R].rearrange("p (k n) -> p k n", k=4),
                               bank[0:R, t, :].rearrange("p (k n) -> p k n", k=4)[:, :, 0:R], ACT.Copy).then_inc(S("msk_act"), 1)
                act.activation(MASK[:, t, 4 * R:N], bank[0:R, 5 + t // 4, t % 4 * P:t % 4 * P + R], ACT.Copy).then_inc(S("msk_act"), 1)
            feats(1, XT)
            def values(t, b):
                act.wait_ge(S("kvq_full"), 2 * T + t + 1)
                act.activation(V[:, t, :, 0:DH], bank[0:R, b, :].rearrange("p (h d) -> p h d", h=H),
                               ACT.Copy).then_inc(S("kvq_done"), 1)

            for g in range(2 * T):
                i, t = divmod(g, T)
                act.wait_ge(S("kvq_full"), g + 1)
                act.activation((QR, KR)[i][:, t], bank[0:R, g % 8, :], ACT.Copy).then_inc(S("kvq_done"), 1)
            for t in range(3):
                values(t, 2 + t)
            act.wait_ge(S("aff_done"), 6)
            feats(2, QT, gq[:, 0:1])
            feats(3, KT)
            for t in (3, 4):
                values(t, 2 + t)
            exps(lambda k: 0, True)
            feats(4, OT)
            for j, (m, lo, hi) in enumerate(GROUPS):
                act.wait_ge(S("wo0_full"), j + 1)
                act.activation(YT[:, m, lo:hi], bank[:, j, 0:hi - lo], ACT.Copy).then_inc(S("wo0_done"), 1)
            router(0)
            mixture(0, FV["m0_b1"])

            feats(5, XT)
            with act.Fori(0, LAYERS) as layer:
                act.wait_ge(S("g_bq"), layer + 1)
                for j, (m, lo, hi) in enumerate(GROUPS):
                    act.wait_ge(S("g_q_full"), layer * 8 + j + 1)
                    act.activation(QT[:, m, lo:hi], bank[:, j, 0:hi - lo], ACT.Identity,
                                   scale=float(DH) ** -0.5, bias=bq8[:, m:m + 1]).then_inc(S("g_q_done"), 1)
                for t in range(T):
                    act.wait_ge(S("g_v_full"), layer * 5 + t + 1)
                    act.activation(V[:, t, :, 0:DH], bank[0:R, 4 + t % 4, :].rearrange("p (h d) -> p h d", h=H),
                                   ACT.Copy).then_inc(S("g_v_done"), 1)
                exps(lambda k: layer * k + k, False)
                copy_feats(OT, S("g_tr_full"), S("g_tr_a"), layer * T, 0)
                bn_apply(HC, X1T, ACT.Identity, S("bn_vec"), layer * 34 + (16 + 17), S("g_x1"), (0, 2))
                for i, (lo, hi) in enumerate(HALVES):
                    act.wait_ge(S("g_f1_full"), layer * 2 + i + 1)
                    act.activation(RT[:, lo:hi], bank[:, i, 0:hi - lo], ACT.Relu,
                                   bias=lvec[:, LV["b1"]:LV["b1"] + 1]).then_inc(S("g_f1_done"), 1)
                bn_apply(HC, XT, ACT.Identity, S("bn_vec"), layer * 34 + (16 + 34), S("g_x2"), (0, 2))

            act.wait_ge(S("lf_vec"), 12)
            for t in range(T):
                act.activation(XN[:, t], bank[0:R, t, :], ACT.Identity, scale=rstd[0:R, t:t + 1],
                               bias=nbias[:, t:t + 1]).then_inc(S("normed"), 1)
            feats(6, XT)
            router(1)
            block_loop(1)

            feats(7, XT)
            act.wait_ge(S("bs_full"), 5)
            for t in range(T):
                act.activation(BS[:, t], bank[0:R, t, 0:BASES], ACT.Copy, scale=dinvr[:, t:t + 1]).then_inc(S("bs_done"), 1)
            act.wait_ge(S("l2_vec"), L2_OPS + 12)
            for t in range(T):
                act.activation(XN[:, t], XN[:, t], ACT.Identity, scale=rstd[0:R, t:t + 1],
                               bias=nbias[:, t:t + 1]).then_inc(S("normed"), 1)

            feats(8, XT)
            router(2)
            mixture(2, FV["m2_b1"])

            feats(9, XT)
            for t in range(T):
                act.wait_ge(S("xw_full"), t + 1)
                act.activation(XW[:, t], bank[0:R, t, :], ACT.Copy, scale=dinvr[:, t:t + 1]).then_inc(S("xw_done"), 1)
            bn_apply(HB, HB, ACT.Gelu, S("bn_vec"), LAST_BN + 16, S("bn_out"))

            feats(10, XT)
            router(3)
            block_loop(3)

        @block.vector
        def _(dve):
            def copy_feats(dst, full, done, fbase, scale=None):
                for t in (0, 2, 4):
                    dve.wait_ge(full, fbase + t + 1)
                    src = bank[:, t, 0:C * R].rearrange("p (c n) -> p c n", c=C)
                    d = dst[:, :, t * R:(t + 1) * R]
                    ins = dve.tensor_copy(d, src) if scale is None else dve.tensor_scalar(d, src, scale, None, ALU.mult)
                    ins.then_inc(done, 1)

            def feats(k, dst, scale=None):
                copy_feats(dst, S("tr_full"), S("tr_v"), T * k, scale)

            def stats_rows(c, src, before=None):
                for t in range(T):
                    if before is not None:
                        before(t)
                    c(dve.bn_stats(st[0:R, t], src(t)))
                for t in range(T):
                    if t == 0:
                        c.sync()
                    c(dve.bn_aggr(mv[0:R, t], st[0:R, t]))
                c.sync()
                c(dve.tensor_scalar(ve[0:R, :], mv[0:R, :, 1], EPS, None, ALU.add))

            def centre(c):
                c(dve.scalar_tensor_tensor(out=nbias[:], in0=mv[0:R, :, 0], scalar=-1.0, in1=rstd[0:R, :], op0=ALU.mult, op1=ALU.mult))

            def ln(k, src=X, before=None):
                c = Chain(dve, S("ln_vec"), LN[k])
                stats_rows(c, lambda t: src[:, t], before)
                dve.wait_ge(S("pow"), POW[f"ln{k}"])
                for t in range(T):
                    c(dve.tensor_scalar(XN[:, t], src[:, t], mv[0:R, t, 0:1], rstd[0:R, t:t + 1], ALU.subtract, ALU.mult))

            def bn(src, done, vec, gamma, beta, dbase=0, vbase=0, power=POW["bn0"], produce=None):
                c = Chain(dve, vec, vbase)
                if produce is not None:
                    produce(0)
                for j, (m, lo, hi) in enumerate(GROUPS):
                    if produce is not None and j + 1 < len(GROUPS):
                        produce(j + 1)
                    dve.wait_ge(done, dbase + j + 1)
                    c(dve.bn_stats(st[:, j], src[:, m, lo:hi]))
                c.sync()
                if not isinstance(vbase, int):
                    c(dve.memset(nop[:, 47:48], 0.0))
                for m in range(C):
                    c(dve.bn_aggr(mv[:, m], st[:, 2 * m:2 * m + 2]))
                c.sync()
                c(dve.tensor_scalar(ve[:, 0:C], mv[:, 0:C, 1], EPS, None, ALU.add))
                dve.wait_ge(S("pow"), power)
                c(dve.tensor_tensor(bsc[:], gamma, rstd[:, 0:C], ALU.mult))
                c.sync()
                c(dve.tensor_tensor(bms[:], mv[:, 0:C, 0], bsc[:], ALU.mult))
                c.sync()
                c(dve.tensor_tensor(bsh[:], beta, bms[:], ALU.subtract))
                c.sync()

            def add_norm(base):
                c = Chain(dve, S("rows_vec"), base)
                for t in range(T):
                    c(dve.tensor_tensor(X[:, t], X[:, t], XN[:, t], ALU.add))
                c.sync()

            def add_rows(before, base):
                c = Chain(dve, S("rows_vec"), base)

                def add(t):
                    dve.wait_ge(S("rows_full"), before + t + 1)
                    c(dve.tensor_tensor(X[:, t], bank[0:R, t, :], X[:, t], ALU.add))
                    c.sync()

                return add

            def attention(base, mask, causal):
                cn = Chain(dve, S("at_norm"), base(3 * T))
                for s in range(ATT + 2):
                    if s < ATT:
                        t, _, kn = step(s, causal)
                        dve.wait_ge(S("at_s"), base(ATT) + s + 1)
                        if s >= 2:
                            dve.wait_ge(S("at_tr"), base(ATT) + s - 1)
                        if not causal:
                            dve.memset(nop[:, s:s + 1], 0.0)
                        scores = bank[0:R, 2 * (s % 2):2 * (s % 2) + 2, :].rearrange("p b n -> p (b n)")[:, 0:kn]
                        dve.tensor_tensor_reduce(out=SM[:, s % 2, 0:kn], in0=scores, in1=mask(t), scale=-1.0, scalar=3e38,
                                                 op0=ALU.add, op1=ALU.min, accum_out=nmx[:, s:s + 1]).then_inc(S("at_mask"), 1)
                    if not causal and 1 <= s <= ATT:
                        u = s - 1
                        t = u // H
                        dve.wait_ge(S("at_tr"), base(ATT) + u + 1)
                        if u >= 2:
                            dve.wait_ge(S("at_av"), base(ATT) + u - 1)
                        at = AT[:, :, t * R:(t + 1) * R]
                        pt = bank[0:R, 4:6, :].rearrange("p b (k n) -> p (b k) n", n=P)[:, 0:T, 0:R]
                        dve.tensor_tensor(PT[:, u % 2], pt, at, ALU.mult).then_inc(S("at_pt"), 1)
                    if s >= 2 and (s - 2) % H == H - 1:
                        t = step(s - 2, causal)[0]
                        dve.wait_ge(S("at_av"), base(ATT) + s - 1)
                        o = bank[0:R, 6:8, 0:4 * (DH + 1)].rearrange("p b (h d) -> p b h d", h=4)
                        cn(dve.tensor_scalar(rden[:].rearrange("p (b h) -> p b h", b=2), o[:, :, :, DH], 1e-16, None, ALU.add))
                        cn.sync()
                        cn(dve.reciprocal(rden[:], rden[:]))
                        cn.sync()
                        for b in range(2):
                            ins = dve.tensor_tensor(OR[:, t, b * 256:(b + 1) * 256].rearrange("p (h d) -> p h d", h=4),
                                                    o[:, b, :, 0:DH], bcast(rden[:, 4 * b:4 * b + 4], DH), ALU.mult)
                            if b == 1:
                                cn(ins)

            def router(r):
                c = Chain(dve, S("rt_vec"), ROUTED[r])
                dve.wait_ge(S("rt_pe"), 2 * r + 1)
                logits = bank[0:R, 7, 0:T * E].rearrange("p (t e) -> p t e", t=T)
                if r in RB:
                    bias = rbias[0:R, RB[r]:RB[r] + E].unsqueeze(1).broadcast_to([R, T, E])
                    c(dve.tensor_tensor(LG[:], logits, bias, ALU.add))
                else:
                    c(dve.tensor_copy(LG[:], logits))
                c.sync()
                c(dve.tensor_reduce(red[:, 0], LG[:], AX.X, ALU.max))
                c.sync()
                c(dve.tensor_tensor(LG[:], LG[:], bcast(red[:, 0], E), ALU.subtract))
                dve.wait_ge(S("rt_act"), RT_ACT[r] + 1)
                c(dve.tensor_reduce(red[:, 1], EX[:], AX.X, ALU.add))
                c.sync()
                c(dve.reciprocal(red[:, 1], red[:, 1]))
                c.sync()
                c(dve.tensor_tensor(COMB[:] if r == 0 else PR[:], EX[:], bcast(red[:, 1], E), ALU.mult))
                if r > 0:
                    c.sync()
                    best = LG if r == 1 else PR
                    for t in range(T):
                        c(dve.max(m8[:, t], best[:, t]))
                    c.sync()
                    for t in range(T):
                        c(dve.max_index(i8[:, t], m8[:, t], best[:, t]))
                    c.sync()
                    c(dve.tensor_copy(if8[:], i8[:]))
                    c.sync()
                    for k in range(2):
                        c(dve.tensor_tensor(EQ[:, k], iota8[0:R].unsqueeze(1).broadcast_to([R, T, E]),
                                            if8[:, :, k:k + 1].broadcast_to([R, T, E]), ALU.is_equal))
                    c.sync()
                    c(dve.tensor_tensor(MK[:], EQ[:, 0], EQ[:, 1], ALU.add))
                    c.sync()
                    c(dve.tensor_tensor(COMB[:], PR[:], MK[:], ALU.mult))
                if r in (1, 3):
                    c.sync()
                    c(dve.tensor_reduce(red[:, 2], COMB[:], AX.X, ALU.add))
                    c.sync()
                    c(dve.reciprocal(red[:, 2], red[:, 2]))
                    c.sync()
                    c(dve.tensor_tensor(COMB[:], COMB[:], bcast(red[:, 2], E), ALU.mult))
                assert c.n == ROUTED[r] + ROUTER_OPS[r]
                if r in (0, 2):
                    dve.wait_ge(S("rt_act"), RT_ACT[r] + 5)
                    for b, lo, hi in ((1, 0, 500), (2, 500, N)):
                        dve.tensor_tensor(combL[:, lo:hi], bank[0:E, b, 0:hi - lo], combH[:, lo:hi].bitcast(F32),
                                          ALU.subtract).then_inc(S("comb_low"), 1)

            def slots(r):
                c = Chain(dve, S("sl_vec"), SLOT_OPS * (r // 2))
                dve.wait_ge(S("sl_pe"), r // 2 + 1)
                rank = bank[0:R, 0, 64:64 + T * E].rearrange("p (t e) -> p t e", t=T)
                chosen = nblk[:, 2]
                more = gtmp[:, 0:E * PER].rearrange("p (e j) -> p e j", e=E)
                sums = gtmp.rearrange("p (e f) -> p e f", e=E)
                pick = etmp.rearrange("p (k t e) -> p k t e", k=2, t=T)
                c(dve.tensor_reduce(chosen, bank[:, 0, 128:128 + T * E].rearrange("p (t e) -> p e t", t=T), AX.X, ALU.add))
                c.sync()
                c(dve.tensor_tensor(more, bcast(chosen, PER), THR[:], ALU.is_gt))
                c.sync()
                c(dve.tensor_reduce(nblk[:, 0], more, AX.X, ALU.add))
                c.sync()
                c(dve.tensor_tensor(sums, nblk[:, 0].unsqueeze(1).broadcast_to([P, E, E]), LT[:], ALU.mult))
                c.sync()
                c(dve.tensor_reduce(nblk[:, 1], sums, AX.X, ALU.add))
                c.sync()
                c(dve.scalar_tensor_tensor(out=slot[:], in0=nblk[0:R, 1].unsqueeze(1).broadcast_to([R, T, E]), scalar=float(P),
                                           in1=rank, op0=ALU.mult, op1=ALU.add))
                c.sync()
                c(dve.tensor_tensor(pick, EQ[:], slot[:].unsqueeze(1).broadcast_to([R, 2, T, E]), ALU.mult))
                c.sync()
                c(dve.tensor_reduce(sl[:], pick, AX.X, ALU.add))
                c.sync()
                c(dve.tensor_copy(slu[:], sl[:]))
                c(dve.tensor_tensor(nblk[:, 2], nblk[:, 0], nblk[:, 1], ALU.add))
                c.sync()
                c(dve.tensor_tensor(btmp, bcast(iota_b[:], E), nblk[:, 2].unsqueeze(1).broadcast_to([P, BLOCKS, E]), ALU.is_ge))
                c.sync()
                c(dve.tensor_reduce(eb[:, 0], btmp, AX.X, ALU.add))
                c.sync()
                c(dve.tensor_scalar(eb[:, 0], eb[:, 0], float(E - 1), None, ALU.min))
                c.sync()
                c(dve.tensor_tensor(eb[:, 1, 1:], eb[:, 0, 1:], eb[:, 0, 0:BLOCKS - 1], ALU.not_equal))
                c.sync()
                c(dve.tensor_copy(ebi[:, 0], eb[0:1, 0]))
                c(dve.tensor_copy(ebi[:, 1, 1:], eb[0:1, 1, 1:]))
                c(dve.tensor_tensor(pick, EQ[:], COMB[:].unsqueeze(1).broadcast_to([R, 2, T, E]), ALU.mult))
                assert c.n == SLOT_OPS * (r // 2 + 1)
                c.sync()
                dve.tensor_reduce(wk[:], pick, AX.X, ALU.add).then_inc(S("wk"), 1)
                if r == 1:
                    c = Chain(dve, S("bias"))
                    c(dve.tensor_tensor(btmp, bcast(eb[:, 0], E), iota8[:].unsqueeze(1).broadcast_to([P, BLOCKS, E]), ALU.is_equal))
                    c.sync()
                    of_expert = fvec[:, FV["m1_b1"]:FV["m1_b1"] + E * M1].rearrange("p (e m) -> p m e", e=E)
                    c(dve.tensor_tensor(bprod, btmp.unsqueeze(2).broadcast_to([P, BLOCKS, M1, E]),
                                        of_expert.unsqueeze(1).broadcast_to([P, BLOCKS, M1, E]), ALU.mult))
                    c.sync()
                    c(dve.tensor_reduce(biases, bprod, AX.X, ALU.add))
                    c.sync()

            def block_loop(r):
                n = CH[r]

                def lows(p, b):
                    low(dve, r, p, b, part(PLACE[r][p]))

                def nodes(b):
                    dve.wait_ge(S("b_xbt"), b + (B0[r] + 1))
                    dve.tensor_tensor(xbl.rearrange("p c n -> p (c n)"), bank[:, 6, :], xbh.rearrange("p c n -> p (c n)").bitcast(F32),
                                      ALU.subtract).then_inc(S("b_xbl"), 1)

                def hidden(j, b):
                    c = b * n + j
                    dve.wait_ge(*used(r, ("a" if r == 1 else "g", j), b))
                    if r == 3:
                        dve.wait_ge(S("b3_s"), c + 1)
                    before = c if j == 0 and n % 2 else c - 1
                    if not (isinstance(before, int) and before <= 0):
                        dve.wait_ge(S("b_tr"), before + C0[r])
                    if r == 1:
                        ins = dve.tensor_copy(hrow[:, j % 2], bank[:, j % 2, :])
                    else:
                        ins = dve.tensor_tensor(hrow[:, j % 2], act_s[:, j % 2], bank[:, 2 + j % 2, :], ALU.mult)
                    ins.then_inc(S("b_h"), 1)

                def turned(j, b):
                    dve.wait_ge(S("b_ht"), b * n + (C0[r] + j + 1))
                    dve.tensor_tensor(hTl[:, j % 2], act_s[:, j % 2] if r == 1 else bank[:, 4 + j % 2, :], hTh[:, j % 2].bitcast(F32),
                                      ALU.subtract).then_inc(S("b_hl"), 1)

                def body1(b, before):
                    nodes(b)
                    lows(("a", 0), b)
                    lows(("a", 1), b)
                    hidden(0, b)
                    if before is not None:
                        turned(1, before)
                    at = slice(b, b + 1) if isinstance(b, int) else bass.ds(b, 1)
                    dve.tensor_copy(m1b[:], biases[:, at].rearrange("p b m -> p (b m)")).then_inc(S("m1b"), 1)
                    lows(("y", 0), b)
                    hidden(1, b)
                    turned(0, b)

                def body3(b, before):
                    lows(("a", 0), b)
                    if before is not None:
                        hidden(2, before)
                    nodes(b)
                    lows(("g", 0), b)
                    if before is not None:
                        turned(2, before)
                    for j in (1, 2):
                        lows(("a", j), b)
                        hidden(j - 1, b)
                        lows(("g", j), b)
                        turned(j - 1, b)

                body = body1 if r == 1 else body3
                body(0, None)
                with dve.Fori(1, BLOCKS) as b:
                    body(b, b - 1)
                if r == 3:
                    hidden(n - 1, BLOCKS - 1)
                turned(n - 1, BLOCKS - 1)
                dve.wait_ge(S("wk"), 1 + r // 2)
                c = Chain(dve, S("add"), 2 * T * (r // 2))

                def add(t):
                    dve.wait_ge(S(f"gathered{t}"), 32 * (r // 2 + 1))
                    for k in range(2):
                        c(dve.scalar_tensor_tensor(out=X[:, t], in0=G[k][:, t], scalar=wk[:, k, t:t + 1], in1=X[:, t],
                                                   op0=ALU.mult, op1=ALU.add))
                        c.sync()

                return add

            def mixture(r):
                dve.wait_ge(S("rt_cb"), 2 * E * (r // 2 + 1))
                for u in range(UNITS):
                    lo, hi = HALVES[u % 2]
                    dve.wait_ge(S("mo_act"), UB[r] + u + 1)
                    dve.tensor_tensor(hs[:, u % 2, 0:hi - lo], hg[:, u % 2, 0:hi - lo], CB[:, u // 2, lo:hi],
                                      ALU.mult).then_inc(S("mo_hs"), 1)
                c = Chain(dve, S("mo_out"), T * (r // 2))
                for t in range(T):
                    dve.wait_ge(S("mo_used"), UB[r] + UNITS - (1 if t < 3 else 0))
                    c(dve.tensor_tensor(X[:, t], X[:, t], bank[0:R, t, :], ALU.add))
                c.sync()

            c = Chain(dve, S("oh_idx"))
            dve.wait_ge(S("ld_idx"), 16)
            c(dve.tensor_copy(idxf, idxi))
            c.sync()
            dve.wait_ge(S("consts"), CONSTS)

            def one_hots(s, at):
                for k in range(2):
                    dve.tensor_scalar(OH[:, s, k, 0:N], iota16[:, 0:N], at(k), None, ALU.is_equal).then_inc(S("oh_ready"), 1)

            for s in range(4):
                one_hots(s, lambda k: idxf[:, k * ET + s:k * ET + s + 1])
            with dve.Fori(1, ET // 4) as i:
                for s in range(4):
                    dve.wait_ge(S("oh_used"), i * 4 + s - 3)
                    one_hots(s, lambda k: idxf[:, bass.ds(i * 4 + (k * ET + s), 1)])
            dve.wait_ge(S("ld_x"), 16)
            ln(0)
            dve.wait_ge(S("ln_vec"), LN[0] + 16)
            add_norm(0)
            dve.wait_ge(S("oh_used"), ET)
            c = Chain(dve, S("cnt_v"))
            c(dve.tensor_copy(AT[:, 0:4, 512:N], bank[0:R, 5, 0:4 * (N - 512)].rearrange("p (k n) -> p k n", k=4)))
            c(dve.tensor_copy(AT[:, 4, 512:N], bank[0:R, 6, 0:N - 512]))
            c = Chain(dve, S("deg_vec"))
            for i, (lo, hi) in enumerate(HALVES):
                dve.wait_ge(S("deg_pe"), i + 1)
                c(dve.tensor_scalar(cmx[:, lo:hi], bank[:, 5 + i, 0:hi - lo], 1.0, None, ALU.max))
                c.sync()
                c(dve.reciprocal(rcntb[:, lo:hi], cmx[:, lo:hi]))
            dve.wait_ge(S("deg_pe"), 3)
            c(dve.tensor_scalar(degr[:], bank[0:R, 7, 0:T], 1.0, None, ALU.add))
            feats(0, XT)
            dve.wait_ge(S("pow"), POW["deg"])
            for t in range(T):
                c(dve.tensor_scalar(diag[:, t], ident[0:R, 0:R], dinvr[:, t:t + 1], None, ALU.mult))
            for i, (lo, hi) in enumerate(HALVES):
                dve.wait_ge(S("deg_pe"), 4 + i)
                c(dve.tensor_copy(dinvb[:, lo:hi], bank[:, 5 + i, 0:hi - lo]))
            assert c.n == 12
            for j, (m, lo, hi) in enumerate(GROUPS):
                dve.wait_ge(S("agg_full"), j + 1)
                dve.tensor_tensor(MT[:, m, lo:hi], bank[:, j, 0:hi - lo], rcntb[:, lo:hi], ALU.mult).then_inc(S("agg_done"), 1)
            dve.wait_ge(S("ld_small"), 48)
            bn(HB, S("h_done"), S("bn_vec"), fvec[:, FV["l0_g"]:FV["l0_g"] + C], fvec[:, FV["l0_be"]:FV["l0_be"] + C])

            c = Chain(dve, S("ln_vec"), LN[1])
            stats_rows(c, lambda t: X[:, t], add_rows(0, T))
            dve.wait_ge(S("pow"), POW["ln1"])
            c(dve.tensor_tensor(rstd2[:], rstd[0:R, :], rstd[0:R, :], ALU.mult))
            c.sync()
            c(dve.tensor_tensor(rstd2[:], rstd2[:], mv[0:R, :, 1], ALU.mult))
            c.sync()
            c(dve.tensor_scalar(ve[0:R, :], rstd2[:], EPS, None, ALU.add))
            c.sync()
            dve.wait_ge(S("pow"), POW["ln2"])
            c(dve.tensor_tensor(rstd2[:], rstd[0:R, :], rstd3[:], ALU.mult))
            c.sync()
            for t in range(T):
                c(dve.tensor_scalar(XN[:, t], X[:, t], mv[0:R, t, 0:1], rstd2[:, t:t + 1], ALU.subtract, ALU.mult))
            assert c.n == LN[3]
            feats(1, XT)
            c = Chain(dve, S("aff_done"))
            dve.wait_ge(S("tr_v"), 6)
            dve.wait_ge(S("tr_a"), 4)
            for k in range(C):
                c(dve.tensor_scalar(XT[:, k], XT[:, k], fvec[:, FV["ln_g"] + k:FV["ln_g"] + k + 1],
                                    fvec[:, FV["ln_b"] + k:FV["ln_b"] + k + 1], ALU.mult, ALU.add))
            c(dve.tensor_scalar(gq[:], fvec[:, FV["qn"]:FV["qn"] + 1], float(DH) ** 0.5, None, ALU.mult))
            c.sync()
            c(dve.tensor_tensor(gq[:], gq[:], fvec[:, FV["kn"]:FV["kn"] + 1], ALU.mult))
            dve.memset(V[:, :, :, DH:DH + 1], 1.0).then_inc(S("v_ones"), 1)
            c = Chain(dve, S("qk_vec"))
            for i, dst in enumerate((QR, KR)):
                for t in range(T):
                    dve.wait_ge(S("kvq_done"), i * T + t + 1)
                    c(dve.tensor_tensor(SQ[:, t % 2], dst[:, t], dst[:, t], ALU.mult))
                    c.sync()
                    c(dve.tensor_reduce(ss[:, i, t * H:(t + 1) * H], SQ[:, t % 2].rearrange("p (h d) -> p h d", h=H), AX.X, ALU.add))
                c.sync()
                c(dve.tensor_scalar(ss[:, i], ss[:, i], 1e-12, None, ALU.add))
            for i, dst in enumerate((QR, KR)):
                dve.wait_ge(S("pow"), POW["qk"[i]])
                for t in range(T):
                    d = dst[:, t].rearrange("p (h d) -> p h d", h=H)
                    c(dve.tensor_tensor(d, d, bcast(ssr[:, i, t * H:(t + 1) * H], DH), ALU.mult))
            assert c.n == 32
            dve.wait_ge(S("aff_done"), 6)
            feats(2, QT, gq[:, 0:1])
            feats(3, KT)
            attention(lambda k: 0, lambda t: CM[:, N - (t + 1) * R:N], True)
            feats(4, OT)
            dve.wait_ge(S("ld_small"), 48)
            router(0)
            mixture(0)

            ln(3)
            dve.memset(V[:, :, :, DH:DH + 1], 1.0).then_inc(S("v_ones"), 1)
            feats(5, XT)
            dve.wait_ge(S("msk_done"), T)
            with dve.Fori(0, LAYERS) as layer:
                dve.wait_ge(S("ld_lvec"), layer * 16 + 16)
                dve.tensor_scalar(bq8[:], lvec[:, LV["bq"]:LV["bq"] + C], float(DH) ** -0.5, None, ALU.mult).then_inc(S("g_bq"), 1)
                for j, (m, lo, hi) in enumerate(GROUPS):
                    dve.wait_ge(S("g_k_full"), layer * 8 + j + 1)
                    dve.tensor_copy(KT[:, m, lo:hi], bank[:, j, 0:hi - lo]).then_inc(S("g_k_done"), 1)
                attention(lambda k: layer * k + k, lambda t: MASK[:, t], False)
                copy_feats(OT, S("g_tr_full"), S("g_tr_v"), layer * T)
                for name, full, bias, res, base in (("1", "g_wo_full", "bo", XT, 8), ("2", "g_w2_full", "b2", X1T, 8)):
                    def residual(j):
                        m, lo, hi = GROUPS[j]
                        dve.wait_ge(S(full), layer * 8 + j + 1)
                        dve.scalar_tensor_tensor(out=HC[:, m, lo:hi], in0=bank[:, j, 0:hi - lo],
                                                 scalar=lvec[:, LV[bias] + m:LV[bias] + m + 1], in1=res[:, m, lo:hi],
                                                 op0=ALU.add, op1=ALU.add).then_inc(S("h_done"), 1)
                    k = int(name) - 1
                    bn(HC, S("h_done"), S("bn_vec"),
                       lvec[:, LV["g" + name]:LV["g" + name] + C], lvec[:, LV["be" + name]:LV["be" + name] + C],
                       layer * 16 + (8 + 8 * k), layer * 34 + (16 + 17 * k), layer * 2 + (POW["ln3"] + 1 + k), lambda j: residual(j))
                    for m in (1, 3):
                        dve.tensor_scalar((X1T, XT)[k][:, m], HC[:, m], bsc[:, m:m + 1], bsh[:, m:m + 1],
                                          ALU.mult, ALU.add).then_inc(S(f"g_x{name}v"), 1)

            c = Chain(dve, S("lf_vec"))
            dve.wait_ge(S("rows_full"), 2 * T)
            stats_rows(c, lambda t: bank[0:R, t, :])
            dve.wait_ge(S("pow"), POW["lf"])
            dve.wait_ge(S("ld_rvec"), 16)
            centre(c)
            assert c.n == 12
            dve.wait_ge(S("ld_rvec"), 16)
            for t in range(T):
                dve.wait_ge(S("normed"), t + 1)
                c(dve.tensor_tensor(XN[:, t], XN[:, t], rvec[0:R, 0], ALU.mult))
            c.sync()
            dve.wait_ge(S("lf_beta"), T)

            def add(t):
                c(dve.tensor_tensor(X[:, t], X[:, t], XN[:, t], ALU.add))
                c.sync()

            ln(4, before=add)
            feats(6, XT)
            router(1)
            slots(1)
            c = Chain(dve, S("b2_done"))
            for t in range(T):
                dve.wait_ge(S("b2_full"), t + 1)
                c(dve.tensor_tensor(X[:, t], X[:, t], bank[0:R, 3 + t, :], ALU.add))
            c.sync()
            ln(5, before=block_loop(1))
            for t in range(T):
                d = AT[:, t, t * R:(t + 1) * R]
                dve.tensor_tensor(d, d, ident[0:R, 0:R], ALU.add).then_inc(S("self_loops"), 1)
            feats(7, XT)
            c = Chain(dve, S("l2_vec"))
            dve.wait_ge(S("ld_rvec"), 32)
            c(dve.tensor_tensor(rvec[0:1, 0], rvec[0:1, 0], rvec[0:1, 1], ALU.add))
            dve.wait_ge(S("bs_full"), 5)
            c(dve.tensor_tensor(WGT[:], bank[0:R, 5, 0:T * 32].rearrange("p (t n) -> p t n", t=T),
                                rbias[0:R, RB["comb"]:RB["comb"] + 32].unsqueeze(1).broadcast_to([R, T, 32]), ALU.add))
            for t in range(T):
                dve.wait_ge(S("ag_full"), t + 1)
                c(dve.tensor_scalar(AG[:, t], bank[0:R, (6, 7, 0, 1, 2)[t], 0:BASES], dinvr[:, t:t + 1], None, ALU.mult))
            c.sync()
            assert c.n == L2_TILE0
            for t in range(T):
                for b in (0, 1):
                    c(basis(dve, CV[:, b], t, b))
                c.sync()
                c(dve.tensor_tensor(CV[:, 0], CV[:, 0], CV[:, 1], ALU.add))
                c.sync()
                dve.wait_ge(S("l2_half"), 3 * t + 3)
                c(dve.tensor_tensor(CV[:, 2], CV[:, 0], PV[:, t % 2, 0], ALU.add))
                c.sync()
                dve.wait_ge(S("res_full"), t + 1)
                c(dve.tensor_tensor(XN[:, t], CV[:, 2], bank[0:R, 3 + t, :], ALU.add))
            c.sync()
            assert c.n == L2_OPS
            stats_rows(c, lambda t: XN[:, t])
            dve.wait_ge(S("pow"), POW["l2"])
            centre(c)
            for t in range(T):
                dve.wait_ge(S("normed"), T + t + 1)
                c(dve.tensor_tensor(XN[:, t], XN[:, t], rvec[0:R, 2], ALU.mult))
                c.sync()
                c(dve.tensor_tensor(XN[:, t], XN[:, t], rvec[0:R, 3], ALU.add))
                c.sync()
                c(dve.scalar_tensor_tensor(out=X[:, t], in0=XN[:, t], scalar=0.0, in1=X[:, t], op0=ALU.max, op1=ALU.add))
            c.sync()

            ln(6)
            feats(8, XT)
            router(2)
            mixture(2)

            ln(7)
            feats(9, XT)
            dve.wait_ge(S("ln_vec"), LN[7] + 16)
            add_norm(2 * T)
            c = Chain(dve, S("h3_scaled"))

            def convolved(j):
                m, lo, hi = GROUPS[j]
                dve.wait_ge(S("h_full"), 8 + j + 1)
                c(dve.tensor_tensor(HB[:, m, lo:hi], bank[:, j, 0:hi - lo], dinvb[:, lo:hi], ALU.mult))
                c.sync()
                dve.tensor_scalar(HB[:, m, lo:hi], HB[:, m, lo:hi], fvec[:, FV["l3_b"] + m:FV["l3_b"] + m + 1], None,
                                  ALU.add).then_inc(S("h_done"), 1)

            bn(HB, S("h_done"), S("bn_vec"), fvec[:, FV["l3_g"]:FV["l3_g"] + C], fvec[:, FV["l3_be"]:FV["l3_be"] + C],
               8 + 16 * LAYERS, LAST_BN, POW["bn3"], convolved)

            ln(8, before=add_rows(2 * T, 3 * T))
            feats(10, XT)
            router(3)
            slots(3)
            add = block_loop(3)
            for t in range(T):
                add(t)


def _by_feature(v):
    return np.asarray(v).reshape(-1, P).T


def _rhs(w):
    w = np.asarray(w)
    return w.reshape(-1, P, w.shape[1]).transpose(1, 0, 2)


def kernel(**inputs):
    import concourse.bacc as bacc
    from concourse.bass_utils import run_bass_kernel_spmd

    g = {k: np.asarray(v) for k, v in inputs.items()}
    cat = np.concatenate
    L = {}
    L["x"] = g["x"].reshape(T, R, D).transpose(1, 0, 2)
    L["edges"] = cat([g["src"].reshape(ET, R).T, g["dst"].reshape(ET, R).T], 1)
    f = _by_feature
    L["fvec"] = cat([f(g["L0_gnn_b_l"]), f(g["L0_gnn_gamma"]), f(g["L0_gnn_beta"]), f(g["L0_ffn_ln_g"]), f(g["L0_ffn_ln_b"]),
                     f(cat([g["L0_ffn_qn_g"]] * 2)), f(cat([g["L0_ffn_kn_g"]] * 2)), f(g["L0_ffn_b1"]),
                     f(g["L1_ffn_b1"]), f(g["L2_ffn_b1"]), f(g["L3_gnn_b"]), f(g["L3_gnn_gamma"]), f(g["L3_gnn_beta"])], 1)
    L["lvec"] = np.stack([cat([f(g["L1_gnn_" + n][l]) for n in ("bq", "bo", "b1", "b2", "g1", "beta1", "g2", "beta2")], 1)
                          for l in range(LAYERS)])
    L["gw"] = _rhs(cat([g["L0_ffn_gate_W"], g["L1_ffn_gate_w"], g["L2_ffn_Wg"], g["L3_ffn_router_w"].T, g["L2_gnn_W_comb"]], 1))
    L["rbias"] = cat([g["L0_ffn_gate_b"], g["L1_ffn_gate_b"], g["L2_ffn_bg"], g["L2_gnn_b_comb"]])[None]
    L["rvec1"] = np.stack([g["L1_gnn_ln_g"], g["L1_gnn_ln_b"]])[None]
    L["rvec2"] = np.stack([g["L2_gnn_conv_bias"], g["L2_gnn_b_res"], g["L2_gnn_gamma"], g["L2_gnn_beta"]])[None]
    L["b2"] = np.stack([g["L0_ffn_b2"], g["L1_ffn_b2"], g["L2_ffn_b2"]])
    L["w_l0"] = cat([_rhs(g["L0_gnn_W_l"].T), _rhs(g["L0_gnn_W_r"].T)], 1).reshape(P, -1)
    L["w_a0"] = np.stack([_rhs(g["L0_ffn_" + n]).reshape(P, -1) for n in ("Wq", "Wk", "Wv", "Wo")], 1)
    L["w_g"] = np.stack([np.stack([_rhs(g["L1_gnn_" + n][l].T).reshape(P, -1) for n in ("Wq", "Wk", "Wv", "Wo")], 1) for l in range(LAYERS)])
    L["w_gf"] = np.stack([cat([_rhs(g["L1_gnn_W1"][l].T).reshape(P, -1), g["L1_gnn_W2"][l].T], 1) for l in range(LAYERS)])
    L["w_l2"] = cat([_rhs(g["L2_gnn_W_bases"]).reshape(P, -1), _rhs(g["L2_gnn_W_res"]).reshape(P, -1)], 1)
    L["w_l3"] = _rhs(g["L3_gnn_W"].T).reshape(P, -1)

    def chunks(ins, w2):
        J = w2.shape[1] // P
        first = [w.reshape(E, C, P, J, P).transpose(0, 3, 2, 1, 4).reshape(E, J, P, C * P) for w in ins]
        return cat(first + [w2.reshape(E, J, P, D)], 3)

    L["w_m0"] = chunks([g["L0_ffn_W1"]], g["L0_ffn_W2"])[:, 0]
    L["w_m2"] = chunks([g["L2_ffn_W1"]], g["L2_ffn_W2"])[:, 0]

    def parts(ins, w2, order):
        at = {}
        for name, w in ins.items():
            for j in range(w.shape[2] // D):
                at[name, j] = w[:, :, j * D:(j + 1) * D].reshape(E, C, P, D).transpose(0, 2, 1, 3)
        for j in range(w2.shape[1] // D):
            at["y", j] = w2[:, j * D:(j + 1) * D].reshape(E, 4, P, D).transpose(0, 2, 1, 3)
        return np.stack([at[p].reshape(E, P, -1) for p in order], 1)

    L["w_m1"] = parts({"a": g["L1_ffn_w1"]}, g["L1_ffn_w2"], PARTS[1])
    L["w_m3"] = parts({"a": g["L3_ffn_w1"].transpose(0, 2, 1), "g": g["L3_ffn_wgate"].transpose(0, 2, 1)},
                      g["L3_ffn_w2"].transpose(0, 2, 1), PARTS[3])

    nc = bacc.Bacc("TRN2", target_bir_lowering=False, num_devices=1)
    arrays, aps = {}, {}
    for name, a in L.items():
        a = np.ascontiguousarray(a)
        arrays["in_" + name] = a
        aps[name] = nc.dram_tensor("in_" + name, a.shape, mybir.dt.from_np(a.dtype), kind="ExternalInput").ap()
    out = nc.dram_tensor("out_x", (R, T, D), F32, kind="ExternalOutput").ap()
    graph_network(nc, aps, out)
    r = run_bass_kernel_spmd(nc, [arrays], core_ids=[0])
    return np.asarray(r.results[0]["out_x"]).transpose(1, 0, 2).reshape(N, D)
```
